# Optimizing a Trainium2 kernel written in Bass

```python
import numpy as np
import jax
import jax.numpy as jnp

def _softmax(x, axis=-1):
    return jax.nn.softmax(x, axis=axis)

def _gelu(x):
    return jax.nn.gelu(x, approximate=True)

def _silu(x):
    return jax.nn.silu(x)

def _sigmoid(x):
    return jax.nn.sigmoid(x)

def _layernorm(x, axis=-1, eps=1e-05):
    m = jnp.mean(x, axis=axis, keepdims=True)
    v = jnp.var(x, axis=axis, keepdims=True)
    return (x - m) / jnp.sqrt(v + eps)

def _scatter_add(tgt, idx, src, axis=0):
    return tgt.at[idx].add(src)

def _segment_sum(src, seg, n):
    return jax.ops.segment_sum(src, seg, n)
kernel_name = 'mk_decoder_postln_d2_seqx_r4_0d7c41'

def setup_inputs(seed: int=0):
    np.random.seed(seed)
    _w = jnp.asarray

    def _rec_inputs():
        import jax
        import jax.numpy as jnp
        _rk = jax.random.key(seed)
        x = -0.0003929 + 0.9999 * jax.random.normal(jax.random.fold_in(_rk, 1), (4, 512, 256), jnp.float32)
        _lenS = 512 - jax.random.randint(jax.random.fold_in(_rk, 7), (4,), 0, max(1, 512 // 4) + 1, jnp.int32)
        _lenS2 = 1601 - jax.random.randint(jax.random.fold_in(_rk, 8), (4,), 0, max(1, 1601 // 4) + 1, jnp.int32)
        _ctx_1024P = jax.random.normal(jax.random.fold_in(_rk, 11), (4, 16, 256), jnp.float32)
        _ctx_1024c = jax.random.dirichlet(jax.random.fold_in(_rk, 511), 0.3 * jnp.ones((16,), jnp.float32), (4, 1601))
        _ctx_1024t = jnp.einsum('bsk,bkd->bsd', _ctx_1024c, _ctx_1024P)
        _ctx_1024t = _ctx_1024t * jax.lax.rsqrt(jnp.mean(jnp.square(_ctx_1024t)) + 1e-12) * 0.953939
        ctx_1024 = 2.81802e-05 + 1.00001 * (_ctx_1024t + 0.3 * jax.random.normal(jax.random.fold_in(_rk, 611), (4, 1601, 256), jnp.float32))
        _validS = jnp.arange(512)[None, :] < _lenS[:, None]
        _validS2 = jnp.arange(1601)[None, :] < _lenS2[:, None]
        _causal = jnp.tril(jnp.ones((512, 512), dtype=bool))
        mask_BxS2_bk0 = jnp.logical_not(jnp.broadcast_to(_validS2[:, :], (4, 1601)))
        return (x, ctx_1024, mask_BxS2_bk0)
    x, ctx_1024, mask_BxS2_bk0 = _rec_inputs()

    def _L0_attn_setup():
        import jax, jax.numpy as jnp
        import numpy as np
        EMBED = 256
        HEADS = 16
        HD = EMBED // HEADS
        M = 32
        R = 2
        EPS = 1e-06
        C_CONST = 2.0 + EPS
        CHUNK = 128

        def _features(x, omega, quad_nodes, quad_weights):
            B, H, T, D = x.shape
            xn = x / jnp.maximum(jnp.linalg.norm(x, axis=-1, keepdims=True), 1e-12)
            proj = jnp.einsum('bhtd,rhdm->rbhtm', xn, omega)
            s = quad_nodes[:, None, None, None, None]
            sqrt_2s = jnp.sqrt(2.0 * jnp.maximum(s, 0.0))
            arg = jnp.clip(proj * sqrt_2s - s, -20.0, 20.0)
            feat = jnp.exp(arg) / np.sqrt(M).astype(np.float32)
            feat = feat * jnp.sqrt(jnp.maximum(quad_weights, 0.0))[:, None, None, None, None]
            return jnp.transpose(feat, (1, 2, 3, 0, 4)).reshape(B, H, T, R * M)
        key = jax.random.key(seed)
        ks = jax.random.split(key, 4)
        B, T = (2, 512)
        x = jax.random.normal(ks[0], (B, T, EMBED), jnp.float32)
        Wqkv = jax.random.normal(ks[1], (EMBED, 3 * EMBED), jnp.float32) * 0.02
        bqkv = jnp.zeros((3 * EMBED,), jnp.float32)
        Wout = jax.random.normal(ks[2], (EMBED, EMBED), jnp.float32) * 0.02
        bout = jnp.zeros((EMBED,), jnp.float32)
        omega = jax.random.normal(ks[3], (R, HEADS, HD, M), jnp.float32)
        nodes, weights = np.polynomial.laguerre.laggauss(R)
        quad_nodes = jnp.asarray(nodes / C_CONST, jnp.float32)
        quad_weights = jnp.asarray(weights * (C_CONST / 4.0), jnp.float32)
        return {'x': x, 'Wqkv': Wqkv, 'bqkv': bqkv, 'Wout': Wout, 'bout': bout, 'omega': omega, 'quad_nodes': quad_nodes, 'quad_weights': quad_weights}
    _L0_attn_all = _L0_attn_setup()
    _L0_attn_in = {k: v for k, v in _L0_attn_all.items() if k in ('Wqkv', 'bqkv', 'Wout', 'bout', 'omega', 'quad_nodes', 'quad_weights')}
    del _L0_attn_all

    def _L0_xattn_setup():
        import jax, jax.numpy as jnp
        import numpy as np
        D1, D2, D3 = (256, 256, 256)
        key = jax.random.key(seed)
        k1, k2, kw, kb = jax.random.split(key, 4)
        x1 = jax.random.normal(k1, (8, 512, D1), dtype=jnp.float32)
        x2 = jax.random.normal(k2, (8, 512, D2), dtype=jnp.float32)
        bound = 1.0 / np.sqrt(D1 + D2)
        W = jax.random.uniform(kw, (D3, D1 + D2), minval=-bound, maxval=bound, dtype=jnp.float32)
        b = jax.random.uniform(kb, (D3,), minval=-bound, maxval=bound, dtype=jnp.float32)
        return {'x1': x1, 'x2': x2, 'W': W, 'b': b}
    _L0_xattn_all = _L0_xattn_setup()
    _L0_xattn_in = {k: v for k, v in _L0_xattn_all.items() if k in ('W', 'b')}
    del _L0_xattn_all

    def _L0_ffn_setup():
        import jax, jax.numpy as jnp
        import numpy as np
        B, S, D, F, E = (4, 512, 256, 1024, 8)
        LN_EPS = 1e-05
        key = jax.random.key(seed)
        ks = jax.random.split(key, 6)
        sc = 0.02
        return {'x': jax.random.normal(ks[0], (B, S, D), dtype=jnp.float32), 'Wr': jax.random.normal(ks[1], (D, E), dtype=jnp.float32) * sc, 'br': jnp.zeros((E,), jnp.float32), 'ln_g': jnp.ones((D,), jnp.float32), 'ln_b': jnp.zeros((D,), jnp.float32), 'W1': jax.random.normal(ks[2], (E, D, F), dtype=jnp.float32) * sc, 'b1': jnp.zeros((E, F), jnp.float32), 'W2': jax.random.normal(ks[3], (E, F, D), dtype=jnp.float32) * sc, 'b2': jnp.zeros((E, D), jnp.float32)}
    _L0_ffn_all = _L0_ffn_setup()
    _L0_ffn_in = {k: v for k, v in _L0_ffn_all.items() if k in ('Wr', 'br', 'ln_g', 'ln_b', 'W1', 'b1', 'W2', 'b2')}
    del _L0_ffn_all

    def _L1_attn_setup():
        import jax, jax.numpy as jnp
        import numpy as np
        S, B, F = (512, 2, 256)
        H, D = (16, 64)
        P = H * D
        key = jax.random.key(seed)
        k1, k2, k3 = jax.random.split(key, 3)
        return {'src': jax.random.normal(k1, (S, B, F), dtype=jnp.float32), 'in_proj_weight': jax.random.normal(k2, (3 * P, F), dtype=jnp.float32) * (1.0 / np.sqrt(F)), 'in_proj_bias': jnp.zeros((3 * P,), dtype=jnp.float32), 'out_proj_weight': jax.random.normal(k3, (F, P), dtype=jnp.float32) * (1.0 / np.sqrt(P)), 'out_proj_bias': jnp.zeros((F,), dtype=jnp.float32)}
    _L1_attn_all = _L1_attn_setup()
    _L1_attn_in = {k: v for k, v in _L1_attn_all.items() if k in ('in_proj_weight', 'in_proj_bias', 'out_proj_weight', 'out_proj_bias')}
    del _L1_attn_all

    def _L1_xattn_setup():
        import jax, jax.numpy as jnp
        import numpy as np
        HEADS = 8
        DIM_HEAD = 64
        SCALE = DIM_HEAD ** (-0.5)
        LN_EPS = 1e-05
        NEG_INF = -1e+30

        def layernorm(x, gamma, beta):
            mu = jnp.mean(x, axis=-1, keepdims=True)
            var = jnp.var(x, axis=-1, keepdims=True)
            return (x - mu) * jax.lax.rsqrt(var + LN_EPS) * gamma + beta
        key = jax.random.key(seed)
        ks = jax.random.split(key, 8)
        b, f, n, d, inner = (8, 2048, 64, 256, HEADS * DIM_HEAD)
        x = jax.random.normal(ks[0], (b, f, d), dtype=jnp.float32)
        latents = jax.random.normal(ks[1], (b, n, d), dtype=jnp.float32)
        key_padding_mask = jax.random.randint(ks[2], (b, f), 0, 2) > 0
        s = 0.02
        return {'x': x, 'latents': latents, 'key_padding_mask': key_padding_mask, 'kv_gate': jnp.float32(-4.0), 'gamma_media': jnp.ones((d,), jnp.float32), 'beta_media': jnp.zeros((d,), jnp.float32), 'gamma_lat': jnp.ones((d,), jnp.float32), 'beta_lat': jnp.zeros((d,), jnp.float32), 'Wq': jax.random.normal(ks[3], (d, inner), jnp.float32) * s, 'Wk': jax.random.normal(ks[4], (d, inner), jnp.float32) * s, 'Wv': jax.random.normal(ks[5], (d, inner), jnp.float32) * s, 'Wout': jax.random.normal(ks[6], (inner, d), jnp.float32) * s}
    _L1_xattn_all = _L1_xattn_setup()
    _L1_xattn_in = {k: v for k, v in _L1_xattn_all.items() if k in ('kv_gate', 'gamma_media', 'beta_media', 'gamma_lat', 'beta_lat', 'Wq', 'Wk', 'Wv', 'Wout')}
    del _L1_xattn_all

    def _L1_ffn_setup():
        import jax, jax.numpy as jnp
        import numpy as np
        TOP_K = 2
        key = jax.random.key(seed)
        ks = jax.random.split(key, 6)
        B, S, D, F, E = (2, 512, 256, 1024, 8)
        sd = 1.0 / np.sqrt(D)
        sf = 1.0 / np.sqrt(F)
        return {'x': jax.random.normal(ks[0], (B, S, D), jnp.float32), 'gate_w': jax.random.normal(ks[1], (D, E), jnp.float32) * sd, 'w1': jax.random.normal(ks[2], (E, D, F), jnp.float32) * sd, 'b1': jax.random.normal(ks[3], (E, F), jnp.float32) * 0.01, 'w2': jax.random.normal(ks[4], (E, F, D), jnp.float32) * sf, 'b2': jax.random.normal(ks[5], (E, D), jnp.float32) * 0.01}
    _L1_ffn_all = _L1_ffn_setup()
    _L1_ffn_in = {k: v for k, v in _L1_ffn_all.items() if k in ('gate_w', 'w1', 'b1', 'w2', 'b2')}
    del _L1_ffn_all
    return {'x': x, 'ctx_1024': ctx_1024, 'mask_BxS2_bk0': mask_BxS2_bk0, 'L0_attn_Wqkv': _L0_attn_in['Wqkv'], 'L0_attn_bqkv': _L0_attn_in['bqkv'], 'L0_attn_Wout': _L0_attn_in['Wout'], 'L0_attn_bout': _L0_attn_in['bout'], 'L0_attn_omega': _L0_attn_in['omega'], 'L0_attn_quad_nodes': _L0_attn_in['quad_nodes'], 'L0_attn_quad_weights': _L0_attn_in['quad_weights'], 'L0_xattn_W': _L0_xattn_in['W'], 'L0_xattn_b': _L0_xattn_in['b'], 'L0_ffn_Wr': _L0_ffn_in['Wr'], 'L0_ffn_br': _L0_ffn_in['br'], 'L0_ffn_ln_g': _L0_ffn_in['ln_g'], 'L0_ffn_ln_b': _L0_ffn_in['ln_b'], 'L0_ffn_W1': _L0_ffn_in['W1'], 'L0_ffn_b1': _L0_ffn_in['b1'], 'L0_ffn_W2': _L0_ffn_in['W2'], 'L0_ffn_b2': _L0_ffn_in['b2'], 'L1_attn_in_proj_weight': _L1_attn_in['in_proj_weight'], 'L1_attn_in_proj_bias': _L1_attn_in['in_proj_bias'], 'L1_attn_out_proj_weight': _L1_attn_in['out_proj_weight'], 'L1_attn_out_proj_bias': _L1_attn_in['out_proj_bias'], 'L1_xattn_kv_gate': _L1_xattn_in['kv_gate'], 'L1_xattn_gamma_media': _L1_xattn_in['gamma_media'], 'L1_xattn_beta_media': _L1_xattn_in['beta_media'], 'L1_xattn_gamma_lat': _L1_xattn_in['gamma_lat'], 'L1_xattn_beta_lat': _L1_xattn_in['beta_lat'], 'L1_xattn_Wq': _L1_xattn_in['Wq'], 'L1_xattn_Wk': _L1_xattn_in['Wk'], 'L1_xattn_Wv': _L1_xattn_in['Wv'], 'L1_xattn_Wout': _L1_xattn_in['Wout'], 'L1_ffn_gate_w': _L1_ffn_in['gate_w'], 'L1_ffn_w1': _L1_ffn_in['w1'], 'L1_ffn_b1': _L1_ffn_in['b1'], 'L1_ffn_w2': _L1_ffn_in['w2'], 'L1_ffn_b2': _L1_ffn_in['b2']}

def reference(x, ctx_1024, mask_BxS2_bk0, L0_attn_Wqkv, L0_attn_bqkv, L0_attn_Wout, L0_attn_bout, L0_attn_omega, L0_attn_quad_nodes, L0_attn_quad_weights, L0_xattn_W, L0_xattn_b, L0_ffn_Wr, L0_ffn_br, L0_ffn_ln_g, L0_ffn_ln_b, L0_ffn_W1, L0_ffn_b1, L0_ffn_W2, L0_ffn_b2, L1_attn_in_proj_weight, L1_attn_in_proj_bias, L1_attn_out_proj_weight, L1_attn_out_proj_bias, L1_xattn_kv_gate, L1_xattn_gamma_media, L1_xattn_beta_media, L1_xattn_gamma_lat, L1_xattn_beta_lat, L1_xattn_Wq, L1_xattn_Wk, L1_xattn_Wv, L1_xattn_Wout, L1_ffn_gate_w, L1_ffn_w1, L1_ffn_b1, L1_ffn_w2, L1_ffn_b2):
    import jax
    import jax.numpy as jnp

    def _L0_attn_ref(x, Wqkv, bqkv, Wout, bout, omega, quad_nodes, quad_weights):
        import jax, jax.numpy as jnp
        import numpy as np
        EMBED = 256
        HEADS = 16
        HD = EMBED // HEADS
        M = 32
        R = 2
        EPS = 1e-06
        C_CONST = 2.0 + EPS
        CHUNK = 128

        def _features(x, omega, quad_nodes, quad_weights):
            B, H, T, D = x.shape
            xn = x / jnp.maximum(jnp.linalg.norm(x, axis=-1, keepdims=True), 1e-12)
            proj = jnp.einsum('bhtd,rhdm->rbhtm', xn, omega)
            s = quad_nodes[:, None, None, None, None]
            sqrt_2s = jnp.sqrt(2.0 * jnp.maximum(s, 0.0))
            arg = jnp.clip(proj * sqrt_2s - s, -20.0, 20.0)
            feat = jnp.exp(arg) / np.sqrt(M).astype(np.float32)
            feat = feat * jnp.sqrt(jnp.maximum(quad_weights, 0.0))[:, None, None, None, None]
            return jnp.transpose(feat, (1, 2, 3, 0, 4)).reshape(B, H, T, R * M)
        B, T, C = x.shape
        qkv = x @ Wqkv + bqkv
        q, k, v = jnp.split(qkv, 3, axis=-1)
        resh = lambda t: t.reshape(B, T, HEADS, HD).transpose(0, 2, 1, 3)
        q, k, v = (resh(q), resh(k), resh(v))
        qf = _features(q, omega, quad_nodes, quad_weights)
        kf = _features(k, omega, quad_nodes, quad_weights)
        Fd = R * M
        nc = T // CHUNK
        to_chunks = lambda t, last: t.reshape(B, HEADS, nc, CHUNK, last).transpose(2, 0, 1, 3, 4)
        qc = to_chunks(qf, Fd)
        kc = to_chunks(kf, Fd)
        vc = to_chunks(v, HD)

        def step(carry, inp):
            kv_state, k_state = carry
            q_ch, k_ch, v_ch = inp
            kv_prod = jnp.einsum('bhtf,bhtd->bhtfd', k_ch, v_ch)
            kv_cur = jnp.cumsum(kv_prod, axis=2) + kv_state[:, :, None]
            k_cur = jnp.cumsum(k_ch, axis=2) + k_state[:, :, None]
            ctx = jnp.einsum('bhtf,bhtfd->bhtd', q_ch, kv_cur)
            den = jnp.maximum(jnp.einsum('bhtf,bhtf->bht', q_ch, k_cur), 1e-06)
            out_ch = ctx / den[..., None]
            return ((kv_cur[:, :, -1], k_cur[:, :, -1]), out_ch)
        init = (jnp.zeros((B, HEADS, Fd, HD), jnp.float32), jnp.zeros((B, HEADS, Fd), jnp.float32))
        _, outs = jax.lax.scan(step, init, (qc, kc, vc))
        out = outs.transpose(1, 2, 0, 3, 4).reshape(B, HEADS, T, HD)
        out = out.transpose(0, 2, 1, 3).reshape(B, T, C)
        return out @ Wout + bout

    def _L0_xattn_ref(x1, x2, W, b):
        import jax, jax.numpy as jnp
        import numpy as np
        D1, D2, D3 = (256, 256, 256)
        d1 = x1.shape[-1]
        W1 = W[:, :d1]
        W2 = W[:, d1:]
        part1 = jnp.einsum('bld,ed->ble', x1, W1)
        part2 = jnp.einsum('bld,ed->be', x2, W2) / x2.shape[1]
        return part1 + part2[:, None, :] + b

    def _L0_ffn_ref(x, Wr, br, ln_g, ln_b, W1, b1, W2, b2):
        import jax, jax.numpy as jnp
        import numpy as np
        B, S, D, F, E = (4, 512, 256, 1024, 8)
        LN_EPS = 1e-05
        tokens_shape = x.shape[:-1]
        xt = x.reshape(-1, x.shape[-1])
        router_logits = xt @ Wr + br
        router_probs = jax.nn.softmax(router_logits, axis=-1)
        gates = jnp.max(router_probs, axis=-1, keepdims=True)
        idx = jnp.argmax(router_probs, axis=-1)
        onehot = jax.nn.one_hot(idx, E, dtype=xt.dtype)
        mu = jnp.mean(xt, axis=-1, keepdims=True)
        var = jnp.mean(jnp.square(xt - mu), axis=-1, keepdims=True)
        xn = (xt - mu) * jax.lax.rsqrt(var + LN_EPS) * ln_g + ln_b
        h = jnp.einsum('te,td,edf->tf', onehot, xn, W1) + b1[idx]
        h = jax.nn.relu(h)
        y = jnp.einsum('te,tf,efd->td', onehot, h, W2) + b2[idx]
        y = y * gates
        return y.reshape(tokens_shape + (y.shape[-1],))

    def _L1_attn_ref(src, in_proj_weight, in_proj_bias, out_proj_weight, out_proj_bias):
        import jax, jax.numpy as jnp
        import numpy as np
        S, B, F = (512, 2, 256)
        H, D = (16, 64)
        P = H * D
        s, b, f = src.shape
        h, d = (H, D)
        qkv = jnp.einsum('sbf,pf->sbp', src, in_proj_weight) + in_proj_bias
        q, k, v = jnp.split(qkv, 3, axis=-1)

        def to_heads(x):
            return jnp.swapaxes(x.reshape(s, b * h, d), 0, 1)
        q = to_heads(q) / np.sqrt(d)
        k = to_heads(k)
        v = to_heads(v)
        attn = jnp.einsum('nsd,ntd->nst', q, k)
        attn = jax.nn.softmax(attn, axis=-1)
        out = jnp.einsum('nst,ntd->nsd', attn, v)
        out = jnp.swapaxes(out, 0, 1).reshape(s * b, h * d)
        out = out @ out_proj_weight.T + out_proj_bias
        return out.reshape(s, b, f)

    def _L1_xattn_ref(x, latents, key_padding_mask, kv_gate, gamma_media, beta_media, gamma_lat, beta_lat, Wq, Wk, Wv, Wout):
        import jax, jax.numpy as jnp
        import numpy as np
        HEADS = 8
        DIM_HEAD = 64
        SCALE = DIM_HEAD ** (-0.5)
        LN_EPS = 1e-05
        NEG_INF = -1e+30

        def layernorm(x, gamma, beta):
            mu = jnp.mean(x, axis=-1, keepdims=True)
            var = jnp.var(x, axis=-1, keepdims=True)
            return (x - mu) * jax.lax.rsqrt(var + LN_EPS) * gamma + beta
        b, f, d = x.shape
        n = latents.shape[1]
        x = layernorm(x, gamma_media, beta_media)
        latents = layernorm(latents, gamma_lat, beta_lat)
        kv = jnp.concatenate((x, latents * kv_gate), axis=1)
        q = (latents @ Wq).reshape(b, n, HEADS, DIM_HEAD)
        k = (kv @ Wk).reshape(b, f + n, HEADS, DIM_HEAD)
        v = (kv @ Wv).reshape(b, f + n, HEADS, DIM_HEAD)
        sim = jnp.einsum('bqhd,bkhd->bhqk', q * SCALE, k)
        sim = sim - jax.lax.stop_gradient(jnp.max(sim, axis=-1, keepdims=True))
        valid_feat = ~key_padding_mask
        valid_full = jnp.concatenate((valid_feat, jnp.ones((b, n), dtype=bool)), axis=1)
        sim = jnp.where(valid_full[:, None, None, :], sim, NEG_INF)
        attn = jax.nn.softmax(sim, axis=-1)
        out = jnp.einsum('bhqk,bkhd->bqhd', attn, v).reshape(b, n, HEADS * DIM_HEAD)
        return out @ Wout

    def _L1_ffn_ref(x, gate_w, w1, b1, w2, b2):
        import jax, jax.numpy as jnp
        import numpy as np
        TOP_K = 2
        B, S, D = x.shape
        T = B * S
        xf = x.reshape(T, D)
        gate_scores = jax.nn.softmax(xf @ gate_w, axis=-1)
        topk_scores, topk_idx = jax.lax.top_k(gate_scores, TOP_K)
        topk_scores = topk_scores / jnp.sum(topk_scores, axis=-1, keepdims=True)
        h = jax.nn.gelu(jnp.einsum('td,edf->etf', xf, w1) + b1[:, None, :], approximate=False)
        y = jnp.einsum('etf,efd->etd', h, w2) + b2[:, None, :]
        tok = jnp.arange(T)
        y_sel = y[topk_idx.T, tok[None, :]]
        out = jnp.einsum('kt,ktd->td', topk_scores.T, y_sel)
        return out.reshape(B, S, D)
    x = _layernorm(x + _L0_attn_ref(x, L0_attn_Wqkv, L0_attn_bqkv, L0_attn_Wout, L0_attn_bout, L0_attn_omega, L0_attn_quad_nodes, L0_attn_quad_weights), axis=-1)
    x = _layernorm(x + _L0_xattn_ref(x, ctx_1024, L0_xattn_W, L0_xattn_b), axis=-1)
    x = _layernorm(x + _L0_ffn_ref(x, L0_ffn_Wr, L0_ffn_br, L0_ffn_ln_g, L0_ffn_ln_b, L0_ffn_W1, L0_ffn_b1, L0_ffn_W2, L0_ffn_b2), axis=-1)
    x = _layernorm(x + _L1_attn_ref(x, L1_attn_in_proj_weight, L1_attn_in_proj_bias, L1_attn_out_proj_weight, L1_attn_out_proj_bias), axis=-1)
    x = _layernorm(x + _L1_xattn_ref(ctx_1024, x, mask_BxS2_bk0, L1_xattn_kv_gate, L1_xattn_gamma_media, L1_xattn_beta_media, L1_xattn_gamma_lat, L1_xattn_beta_lat, L1_xattn_Wq, L1_xattn_Wk, L1_xattn_Wv, L1_xattn_Wout), axis=-1)
    x = _layernorm(x + _L1_ffn_ref(x, L1_ffn_gate_w, L1_ffn_w1, L1_ffn_b1, L1_ffn_w2, L1_ffn_b2), axis=-1)
    return x

_drawn_inputs = setup_inputs


def setup_inputs(seed=0):
    import zlib

    import numpy as np

    out = dict(_drawn_inputs(seed))
    spreads = {'L0_attn_bqkv': (0.0, 0.1),
     'L0_attn_bout': (0.0, 0.1),
     'L0_ffn_br': (0.0, 0.1),
     'L0_ffn_ln_g': (1.0, 0.6),
     'L0_ffn_ln_b': (0.0, 0.35),
     'L0_ffn_b1': (0.0, 0.1),
     'L0_ffn_b2': (0.0, 0.1),
     'L1_attn_in_proj_bias': (0.0, 0.1),
     'L1_attn_out_proj_bias': (0.0, 0.1),
     'L1_xattn_gamma_media': (1.0, 0.545),
     'L1_xattn_beta_media': (0.0, 0.306),
     'L1_xattn_gamma_lat': (1.0, 0.585),
     'L1_xattn_beta_lat': (0.0, 0.1)}
    factors = {'L1_ffn_b1': 8.0, 'L1_ffn_b2': 8.0}
    for name, (base, spread) in spreads.items():
        noise = np.random.default_rng([zlib.crc32(name.encode()), seed]).standard_normal(out[name].shape)
        drawn = base * np.exp(spread * noise) if base else spread * noise
        out[name] = jnp.asarray(drawn.astype(out[name].dtype))
    for name, factor in factors.items():
        out[name] = (out[name] * factor).astype(out[name].dtype)
    return out
```

```python
from contextlib import ExitStack

import numpy as np

import concourse.bass as bass
from concourse import mybir

F32 = mybir.dt.float32
I32 = mybir.dt.int32
U32 = mybir.dt.uint32
U8 = mybir.dt.uint8
ALU = mybir.AluOpType
ACT = mybir.ActivationFunctionType
AX_X = mybir.AxisListType.X

P = 128
B, S, D = 4, 512, 256
KD = D // P
J = S // P
T = B * J
LN_EPS = 1e-5

H0, HD0, R0, M0 = 16, 16, 2, 32
FD0 = R0 * M0
PAIRS0 = H0 * FD0 // P
VW0 = HD0 + 1

E, F = 8, 1024
KF = F // P


def each(eng, go, pace, it):
    eng.wait_ge(go, it)
    eng.sem_inc(pace, 1)


def ends(eng, ended):
    eng.drain().then_inc(ended, 1)


def turn(sp, ended, go, pace, it, sems):
    sp.wait_ge(ended, it * 4)
    sp.sem_inc(pace, 1)
    sp.sem_clear(range(sems[0].num, sems[-1].num + 1))
    sp.sem_inc(go, 1)


def layer0_attention(nc, sc, g):
    ctx = ExitStack()
    with ctx:
        def sb(name, shape, dt=F32):
            return ctx.enter_context(nc.sbuf_tensor(name, shape, dt))

        loop_sems = []

        def sem(name, kept=False):
            s = ctx.enter_context(nc.semaphore(name))
            if not kept:
                loop_sems.append(s)
            return s

        PS = g["PS"]
        ident, X, LG = g["ident"], g["X"], g["LG"]

        wqkv = sb("wqkv", [P, KD, 3 * D])
        wout = sb("wout0", [P, KD, D])
        w1t = sb("w1t", [P, KD, D])
        w2t = sb("w2t", [P, KD, D])
        wr = sb("wr", [P, KD, E])
        omega = sb("omega", [P, KD, KD * 2 * P])
        bqkv = sb("bqkv", [P, 3 * D])
        bout = sb("bout0", [P, D])
        bx = sb("bx", [P, D])
        brt = sb("brt", [P, E])
        nodes = sb("nodes", [P, 2])
        fscale = sb("fscale", [P, 4])
        causal = sb("causal", [P, P])
        xT = sb("xT", [P, KD, S])
        ctxT = sb("ctxT", [P, KD, g["S2"]])
        xres = sb("xres", [P, J, D])
        qk = sb("qk", [P, J, 2 * D])
        v1 = sb("v1", [P, J, H0, VW0])
        sq = sb("sq", [P, 2, 2 * D])
        ss = sb("ss", [P, J, 2 * H0])
        rn = sb("rn", [P, J, 2 * H0])
        qkT = sb("qkT", [P, 4, S])
        fe = sb("fe", [P, 4, S])
        kfT = sb("kfT", [P, PAIRS0, S])
        qbd = sb("qbd", [P, PAIRS0, J, 2 * P])
        kfR = sb("kfR", [P, J - 1, PAIRS0, P])
        scm = sb("scm", [P, 2, 4, P])
        state = sb("state", [P, PAIRS0, 2 * VW0])
        den = sb("den", [P, H0])
        rden = sb("rden", [P, H0])
        osb = sb("osb", [P, D])
        oT = sb("oT", [P, KD, P])
        r1 = sb("r1", [P, D])
        r2 = sb("r2", [P, D])
        bn = sb("bn", [P, 2, 6])
        mv = sb("mv", [P, 2, 2])
        ve = sb("ve", [P, 2])
        rs = sb("rs", [P, 2])
        x1 = sb("x1", [P, J, D])
        x1T = sb("x1T", [P, KD, P])
        x1pb = sb("x1pb", [P, D])
        x2 = sb("x2", [P, J, D])
        x2T = sb("x2T", [P, KD, P])
        lgs = sb("lgs", [P, J, E])
        csum = sb("csum", [P, KD])
        cbc = sb("cbc", [P, KD, P])
        pb = sb("pb", [P, D])

        w_loaded = sem("a_w_loaded", True)
        xT_loaded = sem("a_xT_loaded", True)
        x_loaded = g["x_loaded"]
        consts = sem("a_consts", True)
        ended = sem("a_ended", True)
        go = sem("a_go", True)
        pace = sem("a_pace", True)
        chain = sem("a_chain")
        pchain = sem("a_pchain")
        ctx_loaded = sem("a_ctx_loaded")
        qkv_done = sem("a_qkv_done")
        qk_ready = sem("a_qk_ready")
        v_ready = sem("a_v_ready")
        sq_ready = sem("a_sq_ready")
        ss_ready = sem("a_ss_ready")
        qkn_ready = sem("a_qkn_ready")
        qkT_done = sem("a_qkT_done")
        qkT_ready = sem("a_qkT_ready")
        feat_done = sem("a_feat_done")
        feat_exp = sem("a_feat_exp")
        k_ready = sem("a_k_ready")
        q_clipped = sem("a_q_clipped")
        q_ready = sem("a_q_ready")
        kfR_done = sem("a_kfR_done")
        kfR_ready = sem("a_kfR_ready")
        scores_done = sem("a_scores_done")
        masked = sem("a_masked")
        av_done = sem("a_av_done")
        state_done = sem("a_state_done")
        state_ready = sem("a_state_ready")
        o_ready = sem("a_o_ready")
        oT_done = sem("a_oT_done")
        oT_ready = sem("a_oT_ready")
        proj_done = sem("a_proj_done")
        xres_ready = sem("a_xres_ready")
        r1_ready = sem("a_r1_ready")
        mv1_ready = sem("a_mv1_ready")
        rs1_ready = sem("a_rs1_ready")
        x1_ready = sem("a_x1_ready")
        x1T_done = sem("a_x1T_done")
        x1T_ready = sem("a_x1T_ready")
        x1pb_ready = sem("a_x1pb_ready")
        part_done = sem("a_part_done")
        r2_ready = sem("a_r2_ready")
        mv2_ready = sem("a_mv2_ready")
        rs2_ready = sem("a_rs2_ready")
        x2_ready = sem("a_x2_ready")
        x2T_done = sem("a_x2T_done")
        x2T_ready = sem("a_x2T_ready")
        lg_done = sem("a_lg_done")
        lg_ready = sem("a_lg_ready")
        cbc_ready = sem("a_cbc_ready")
        part2_done = sem("a_part2_done")
        pb_ready = sem("a_pb_ready")

        block = ctx.enter_context(nc.Block())

        @block.sync
        def _(sp):
            for dst, src in ((wqkv, g["L0_attn_Wqkv"]), (bqkv, g["L0_attn_bqkv"]), (omega, g["L0_attn_omega"]),
                             (nodes, g["L0_attn_nodes"]), (bout, g["L0_attn_bout"]), (wout, g["L0_attn_Wout"]),
                             (w1t, g["L0_xattn_W1"]), (w2t, g["L0_xattn_W2"]), (bx, g["L0_xattn_b"]),
                             (wr, g["L0_ffn_Wr"]), (brt, g["L0_ffn_br"])):
                sp.dma_start(dst[:], src).then_inc(w_loaded, 16)
            sp.dma_start(xT[:], g["xT"][0]).then_inc(xT_loaded, 16)
            sp.sem_inc(go, 1)
            with sp.Fori(1, B + 1) as it:
                each(sp, go, pace, it)
                sp.dma_start(ctxT[:], g["ctxT"][bass.ds(it - 1, 1)].rearrange("o p k s -> p (o k) s"))\
                    .then_inc(ctx_loaded, 16)
                sp.wait_ge(qkv_done, J)
                sp.dma_start(xT[:], g["xT"][bass.ds(it, 1)].rearrange("o p k s -> p (o k) s"))\
                    .then_inc(xT_loaded, 16)
                turn(sp, ended, go, pace, it, loop_sems)
            sp.wait_ge(xT_loaded, 16 * (B + 1))

        @block.gpsimd
        def _(pool):
            n = [0]

            def link(ins):
                n[0] += 1
                ins.then_inc(pchain, 1)
                pool.wait_ge(pchain, n[0])

            nc.gpsimd.memset(causal[:], 1.0).then_inc(consts, 1)
            pool.wait_ge(consts, 1)
            nc.gpsimd.affine_select(out=causal[:], in_=causal[:], compare_op=ALU.is_ge, fill=0.0, base=0,
                                    pattern=[[1, P]], channel_multiplier=-1).then_inc(consts, 1)
            nc.gpsimd.memset(qbd[:], 0.0).then_inc(consts, 1)
            nc.gpsimd.memset(v1[:], 1.0).then_inc(consts, 1)
            pool.wait_ge(w_loaded, 16 * 11)
            nc.gpsimd.tensor_scalar(fscale[:, 3:4], nodes[:, 0:1], 0.0, 2.0, ALU.max, ALU.mult).then_inc(consts, 1)
            nc.gpsimd.tensor_scalar(fscale[:, 1:2], nodes[:, 0:1], -1.0, None, ALU.mult).then_inc(consts, 1)
            nc.gpsimd.tensor_scalar(fscale[:, 2:3], nodes[:, 1:2], 0.0, 1.0 / M0, ALU.max, ALU.mult).then_inc(consts, 1)
            pool.wait_ge(consts, 7)
            nc.gpsimd.tensor_tensor(fscale[:, 0:1], fscale[:, 3:4], g["half"][:], ALU.pow).then_inc(consts, 1)
            pool.wait_ge(x_loaded, 16)
            with pool.Fori(1, B + 1) as it:
                each(pool, go, pace, it)
                n[0] = 0
                nc.gpsimd.tensor_tensor(xres[:], X[:, bass.ds(it * J - J, J), :],
                                        bout[:, None, :].to_broadcast([P, J, D]), ALU.add).then_inc(xres_ready, 1)

                def square(j):
                    pool.wait_ge(qk_ready, j + 1)
                    if j >= 2:
                        pool.wait_ge(ss_ready, j - 1)
                    nc.gpsimd.tensor_tensor(sq[:, j % 2, :], qk[:, j, :], qk[:, j, :], ALU.mult).then_inc(sq_ready, 1)

                def normalise(j):
                    pool.wait_ge(ss_ready, j + 1)
                    link(nc.gpsimd.tensor_scalar(rn[:, j, :], ss[:, j, :], 1e-24, None, ALU.max))
                    link(nc.gpsimd.tensor_tensor(rn[:, j, :], rn[:, j, :],
                                                 g["mhalf"][:].to_broadcast([P, 2 * H0]), ALU.pow))
                    v = qk[:, j, :].rearrange("p (h d) -> p h d", d=HD0)
                    nc.gpsimd.tensor_tensor(v, v, rn[:, j, :, None].to_broadcast([P, 2 * H0, HD0]), ALU.mult)\
                        .then_inc(qkn_ready, 1)

                for j in range(J + 1):
                    if j < J:
                        square(j)
                    if j >= 1:
                        normalise(j - 1)
                for p in range(PAIRS0):
                    pool.wait_ge(q_clipped, p + 1)
                    f = (2 * p + 1) % 4
                    for half in range(2):
                        at = slice(64 * half, 64 * half + 64)
                        ins = nc.gpsimd.tensor_scalar(
                            qbd[at, p, :, P * half:P * half + P],
                            fe[at, f, :].rearrange("p (j n) -> p j n", j=J), fscale[at, 2:3], None, ALU.mult)
                    ins.then_inc(q_ready, 1)
                for s in range(J + 1):
                    if s < J:
                        pool.wait_ge(mv1_ready, s + 1)
                        link(nc.gpsimd.tensor_scalar(ve[:, 0:1], mv[:, 0, 1:2], LN_EPS, None, ALU.add))
                        nc.gpsimd.tensor_tensor(rs[:, 0:1], ve[:, 0:1], g["mhalf"][:], ALU.pow).then_inc(rs1_ready, 1)
                    if s >= 1:
                        pool.wait_ge(mv2_ready, s)
                        link(nc.gpsimd.tensor_scalar(ve[:, 1:2], mv[:, 1, 1:2], LN_EPS, None, ALU.add))
                        nc.gpsimd.tensor_tensor(rs[:, 1:2], ve[:, 1:2], g["mhalf"][:], ALU.pow).then_inc(rs2_ready, 1)
                    if s < J:
                        pool.wait_ge(x1_ready, s + 1)
                        pool.wait_ge(pb_ready, 1)
                        if s >= 1:
                            pool.wait_ge(r2_ready, s)
                        nc.gpsimd.tensor_tensor(x1pb[:], x1[:, s, :], pb[:], ALU.add).then_inc(x1pb_ready, 1)
                pool.wait_ge(x2_ready, J)
                pool.wait_ge(lg_ready, J)
                nc.gpsimd.tensor_copy(X[:, bass.ds(it * J - J, J), :], x2[:])
                nc.gpsimd.tensor_copy(LG[:, bass.ds(it * J - J, J), :], lgs[:])
                ends(pool, ended)

        @block.scalar
        def _(act):
            act.wait_ge(consts, 8)
            with act.Fori(1, B + 1) as it:
                each(act, go, pace, it)
                for j in range(J):
                    act.wait_ge(qkT_done, j + 1)
                    nc.scalar.copy(qkT[:, :, j * P:(j + 1) * P],
                                   PS[:, 4 + j % 2, :].rearrange("p (c n) -> p c n", c=4)).then_inc(qkT_ready, 1)
                for f in range(2 * PAIRS0):
                    p = f // 2
                    act.wait_ge(feat_done, f + 1)
                    if p >= 2:
                        act.wait_ge(q_ready if f % 2 else k_ready, p - 1)
                    nc.scalar.activation(fe[:, f % 4, :], PS[:, f % 4, :], ACT.Exp, bias=fscale[:, 1:2],
                                         scale=fscale[:, 0:1]).then_inc(feat_exp, 1)
                for p in range(PAIRS0):
                    act.wait_ge(kfR_done, p + 1)
                    nc.scalar.copy(kfR[:, :, p, :],
                                   PS[:, 4 + p % 2, 0:(J - 1) * P].rearrange("p (j n) -> p j n", n=P))\
                        .then_inc(kfR_ready, 1)

                def turned(dst, bank, done, used, ready, s):
                    act.wait_ge(done, s + 1)
                    if s >= 1:
                        act.wait_ge(used, s)
                    nc.scalar.copy(dst[:], PS[:, bank, 0:D].rearrange("p (k n) -> p k n", k=KD)).then_inc(ready, 1)

                for s in range(J + 2):
                    if 0 <= s - 1 < J:
                        turned(oT, 4, oT_done, proj_done, oT_ready, s - 1)
                    if 0 <= s - 2 < J:
                        turned(x2T, 2, x2T_done, lg_done, x2T_ready, s - 2)
                    if 0 <= s - 1 < J:
                        turned(x1T, 5, x1T_done, part_done, x1T_ready, s - 1)
                ends(act, ended)

        @block.vector
        def _(dve):
            n = [0]

            def link(ins):
                n[0] += 1
                ins.then_inc(chain, 1)
                dve.wait_ge(chain, n[0])

            dve.wait_ge(w_loaded, 16 * 11)
            dve.wait_ge(consts, 8)
            with dve.Fori(1, B + 1) as it:
                each(dve, go, pace, it)
                n[0] = 0
                dve.wait_ge(ctx_loaded, 16)
                link(nc.vector.reduce_sum(csum[:], ctxT[:], AX_X))
                for k in range(KD):
                    ins = nc.vector.tensor_scalar(cbc[:, k, :], g["ones"][:], csum[:, k:k + 1], 1.0 / g["S2"],
                                                  ALU.mult, ALU.mult)
                ins.then_inc(cbc_ready, 1)

                def add_bias(j):
                    dve.wait_ge(qkv_done, j + 1)
                    u = PS[:, 2 * (j % 2):2 * (j % 2) + 2, :].rearrange("p b n -> p (b n)")
                    nc.vector.tensor_tensor(qk[:, j, :], u[:, 0:2 * D], bqkv[:, 0:2 * D], ALU.add).then_inc(qk_ready, 1)
                    nc.vector.tensor_tensor(v1[:, j, :, 0:HD0],
                                            u[:, 2 * D:3 * D].rearrange("p (h d) -> p h d", d=HD0),
                                            bqkv[:, 2 * D:3 * D].rearrange("p (h d) -> p h d", d=HD0),
                                            ALU.add).then_inc(v_ready, 1)

                def square_sums(j):
                    dve.wait_ge(sq_ready, j + 1)
                    nc.vector.reduce_sum(ss[:, j, :], sq[:, j % 2, :].rearrange("p (h d) -> p h d", d=HD0), AX_X)\
                        .then_inc(ss_ready, 1)

                for j in range(J + 1):
                    if j < J:
                        add_bias(j)
                    if j >= 1:
                        square_sums(j - 1)
                dve.wait_ge(part2_done, 1)
                nc.vector.tensor_tensor(pb[:], PS[:, 7, 0:D], bx[:], ALU.add).then_inc(pb_ready, 1)
                low, high = float(np.exp(-20.0)), float(np.exp(20.0))
                for f in range(2 * PAIRS0):
                    dve.wait_ge(feat_exp, f + 1)
                    dst, ready = (fe[:, f % 4, :], q_clipped) if f % 2 else (kfT[:, f // 2, :], k_ready)
                    nc.vector.tensor_scalar(dst, fe[:, f % 4, :], high, low, ALU.min, ALU.max).then_inc(ready, 1)

                def mask(s, q):
                    dve.wait_ge(scores_done, 4 * s + q + 1)
                    if 4 * s + q >= 2:
                        dve.wait_ge(av_done, 4 * s + q - 1)
                    nc.vector.tensor_tensor(scm[:, q % 2, :, :], PS[:, q % 2, :].rearrange("p (h n) -> p h n", n=P),
                                            causal[:, None, :].to_broadcast([P, 4, P]), ALU.mult).then_inc(masked, 1)

                def add_state(s):
                    dve.wait_ge(state_done, s + 1)
                    dve.wait_ge(av_done, 4 * s + 4)
                    new = PS[:, 7, 0:PAIRS0 * 2 * VW0].rearrange("p (a w) -> p a w", a=PAIRS0)
                    if s == 0:
                        ins = nc.vector.tensor_copy(state[:], new)
                    else:
                        dve.wait_ge(state_ready, s)
                        ins = nc.vector.tensor_tensor(state[:], new, state[:], ALU.add)
                    ins.then_inc(state_ready, 1)

                def divide(s):
                    dve.wait_ge(av_done, 4 * s + 4)
                    if s >= 1:
                        dve.wait_ge(oT_done, s)
                    o = PS[:, 6, 0:H0 * VW0].rearrange("p (h w) -> p h w", w=VW0)
                    link(nc.vector.tensor_scalar(den[:, :, None], o[:, :, HD0:VW0], 1e-6, None, ALU.max))
                    link(nc.vector.reciprocal(rden[:], den[:]))
                    nc.vector.tensor_tensor(osb[:].rearrange("p (h d) -> p h d", d=HD0), o[:, :, 0:HD0],
                                            rden[:, :, None].to_broadcast([P, H0, HD0]), ALU.mult).then_inc(o_ready, 1)

                def residual(s, i, done, add, r, ready, mv_ready):
                    dve.wait_ge(done, s + 1)
                    nc.vector.tensor_tensor(r[:], PS[:, 3, D * i:D * i + D], add, ALU.add).then_inc(ready, 1)
                    dve.wait_ge(ready, s + 1)
                    link(nc.vector.bn_stats(bn[:, i, :], r[:]))
                    nc.vector.bn_aggr(mv[:, i, :], bn[:, i, :]).then_inc(mv_ready, 1)

                def norm(s, i, rs_ready, r, dst, ready):
                    dve.wait_ge(rs_ready, s + 1)
                    nc.vector.tensor_scalar(dst, r[:], mv[:, i, 0:1], rs[:, i:i + 1], ALU.subtract, ALU.mult)\
                        .then_inc(ready, 1)

                for s in range(J + 2):
                    if s < J:
                        mask(s, 0)
                        mask(s, 1)
                    if 0 <= s - 2 < J:
                        dve.wait_ge(x1pb_ready, s - 1)
                        residual(s - 2, 1, part_done, x1pb[:], r2, r2_ready, mv2_ready)
                    if s < J:
                        mask(s, 2)
                    if 0 <= s - 1 < J:
                        if s == 1:
                            dve.wait_ge(xres_ready, 1)
                        residual(s - 1, 0, proj_done, xres[:, s - 1, :], r1, r1_ready, mv1_ready)
                    if 0 <= s - 2 < J:
                        norm(s - 2, 1, rs2_ready, r2, x2[:, s - 2, :], x2_ready)
                    if s < J:
                        mask(s, 3)
                    if 0 <= s - 1 < J:
                        norm(s - 1, 0, rs1_ready, r1, x1[:, s - 1, :], x1_ready)
                    if s < J - 1:
                        add_state(s)
                    if s < J:
                        divide(s)
                    if 0 <= s - 2 < J:
                        dve.wait_ge(lg_done, s - 1)
                        nc.vector.tensor_tensor(lgs[:, s - 2, :], PS[:, 2, D:D + E], brt[:], ALU.add)\
                            .then_inc(lg_ready, 1)
                ends(dve, ended)

        @block.tensor
        def _(pe):
            pe.wait_ge(w_loaded, 16 * 11)
            pe.wait_ge(g["consts"], g["n_consts"])
            with pe.Fori(1, B + 1) as it:
                each(pe, go, pace, it)
                pe.wait_ge(xT_loaded, 16 * it)
                pe.sem_inc(pace, 1)

                def qkv(j):
                    if j >= 2:
                        pe.wait_ge(v_ready, j - 1)
                    for half, cols in ((0, 2 * D), (1, D)):
                        for k in range(KD):
                            mm = nc.tensor.matmul(PS[:, 2 * (j % 2) + half, 0:cols], xT[:, k, j * P:(j + 1) * P],
                                                  wqkv[:, k, half * 2 * D:half * 2 * D + cols],
                                                  start=(k == 0), stop=(k == KD - 1))
                    mm.then_inc(qkv_done, 1)

                def turn_qk(j):
                    pe.wait_ge(qkn_ready, j + 1)
                    if j >= 2:
                        pe.wait_ge(qkT_ready, j - 1)
                    for c in range(4):
                        mm = nc.tensor.transpose(PS[:, 4 + j % 2, c * P:(c + 1) * P], qk[:, j, c * P:(c + 1) * P],
                                                 ident[:])
                    mm.then_inc(qkT_done, 1)

                for j in range(J + 2):
                    if j < J:
                        qkv(j)
                    if j >= 2:
                        turn_qk(j - 2)
                pe.wait_ge(cbc_ready, 1)
                for k in range(KD):
                    mm = nc.tensor.matmul(PS[:, 7, 0:D], cbc[:, k, :], w2t[:, k, :], start=(k == 0), stop=(k == KD - 1))
                mm.then_inc(part2_done, 1)
                pe.wait_ge(v_ready, J)
                pe.wait_ge(qkT_ready, J)
                for f in range(2 * PAIRS0):
                    p, q_side = f // 2, f % 2
                    if f >= 4:
                        pe.wait_ge(feat_exp, f - 3)
                    half = p // 4
                    nc.tensor.matmul(PS[:, f % 4, :], omega[:, half, (p % 4) * P:(p % 4 + 1) * P],
                                     qkT[:, half if q_side else 2 + half, :], start=True, stop=True).then_inc(feat_done, 1)
                for p in range(PAIRS0):
                    pe.wait_ge(k_ready, p + 1)
                    if p >= 2:
                        pe.wait_ge(kfR_ready, p - 1)
                    for j in range(J - 1):
                        mm = nc.tensor.transpose(PS[:, 4 + p % 2, j * P:(j + 1) * P], kfT[:, p, j * P:(j + 1) * P], ident[:])
                    mm.then_inc(kfR_done, 1)
                pe.wait_ge(feat_exp, 2 * PAIRS0)
                pe.wait_ge(pb_ready, 1)

                def scores(s, q):
                    if 4 * s + q >= 2:
                        pe.wait_ge(masked, 4 * s + q - 1)
                    if s == 0:
                        pe.wait_ge(q_ready, 2 * q + 2)
                    for i in range(2):
                        p = 2 * q + i
                        mm = nc.tensor.matmul(PS[:, q % 2, i * 2 * P:(i + 1) * 2 * P], kfT[:, p, s * P:(s + 1) * P],
                                              qbd[:, p, s, :], start=True, stop=True)
                    mm.then_inc(scores_done, 1)

                def weigh(s, q):
                    pe.wait_ge(masked, 4 * s + q + 1)
                    if s >= 1 and q == 0:
                        pe.wait_ge(o_ready, s)
                        pe.wait_ge(state_ready, s)
                    for i in range(4):
                        h = 4 * q + i
                        out = PS[:, 6, h * VW0:(h + 1) * VW0]
                        mm = nc.tensor.matmul(out, scm[:, q % 2, i, :], v1[:, s, h, :], start=True, stop=(s == 0))
                        if s >= 1:
                            mm = nc.tensor.matmul(out, qbd[:, h // 2, s, (h % 2) * P:(h % 2 + 1) * P],
                                                  state[:, h // 2, (h % 2) * VW0:(h % 2 + 1) * VW0],
                                                  start=False, stop=True)
                    mm.then_inc(av_done, 1)

                def new_state(s):
                    if s == 0:
                        pe.wait_ge(kfR_ready, PAIRS0)
                    else:
                        pe.wait_ge(state_ready, s)
                    for p in range(PAIRS0):
                        mm = nc.tensor.matmul(PS[:, 7, p * 2 * VW0:(p + 1) * 2 * VW0], kfR[:, s, p, :],
                                              v1[:, s, 2 * p:2 * p + 2, :].rearrange("p h w -> p (h w)"),
                                              start=True, stop=True)
                    mm.then_inc(state_done, 1)

                def turn_rows(s, src, bank, ready, used, done):
                    pe.wait_ge(ready, s + 1)
                    if used is not None and s >= 1:
                        pe.wait_ge(used, s)
                    if s == 0:
                        pe.wait_ge(kfR_ready, PAIRS0)
                    for k in range(KD):
                        mm = nc.tensor.transpose(PS[:, bank, k * P:(k + 1) * P], src[:, k * P:(k + 1) * P], ident[:])
                    mm.then_inc(done, 1)

                def project(s, at, lhs, ready, w, done):
                    pe.wait_ge(ready, s + 1)
                    for k in range(KD):
                        mm = nc.tensor.matmul(PS[:, 3, at:at + D], lhs[:, k, :], w[:, k, :],
                                              start=(k == 0), stop=(k == KD - 1))
                    mm.then_inc(done, 1)

                for s in range(J + 2):
                    main, first, second = s < J, 0 <= s - 1 < J, 0 <= s - 2 < J
                    if main:
                        scores(s, 0)
                        scores(s, 1)
                    if second:
                        pe.wait_ge(r1_ready, s - 1)
                        project(s - 2, D, x1T, x1T_ready, w1t, part_done)
                    if first:
                        turn_rows(s - 1, osb, 4, o_ready, oT_ready, oT_done)
                    if main:
                        weigh(s, 0)
                        scores(s, 2)
                    if first:
                        if s >= 2:
                            pe.wait_ge(r2_ready, s - 1)
                        project(s - 1, 0, oT, oT_ready, wout, proj_done)
                    if main:
                        weigh(s, 1)
                        scores(s, 3)
                    if second:
                        if s >= 3:
                            pe.wait_ge(lg_ready, s - 2)
                        turn_rows(s - 2, x2[:, s - 2, :], 2, x2_ready, x2T_ready, x2T_done)
                    if main:
                        weigh(s, 2)
                    if first:
                        turn_rows(s - 1, x1[:, s - 1, :], 5, x1_ready, x1T_ready, x1T_done)
                    if main:
                        weigh(s, 3)
                    if s < J - 1:
                        new_state(s)
                    if second:
                        pe.wait_ge(x2T_ready, s - 1)
                        for k in range(KD):
                            mm = nc.tensor.matmul(PS[:, 2, D:D + E], x2T[:, k, :], wr[:, k, :],
                                                  start=(k == 0), stop=(k == KD - 1))
                        mm.then_inc(lg_done, 1)
                ends(pe, ended)


def tiles_of(choices):
    return choices * T + E - 1


def experts(nc, top, g, layer):
    C = layer + 1
    TC = T * C
    NT = tiles_of(C)
    xs, ys = g["xs%d" % layer], g["ys%d" % layer]
    PS, X, LG, ident, ones = g["PS"], g["X"], g["LG"], g["ident"], g["ones"]
    ctx = ExitStack()
    with ctx:
        def sb(name, shape, dt=F32):
            return ctx.enter_context(nc.sbuf_tensor("f%d_%s" % (layer, name), shape, dt))

        def sem(name):
            return ctx.enter_context(nc.semaphore("f%d_%s" % (layer, name)))

        w1 = sb("w1", [P, E * KD * F])
        w2 = sb("w2", [P, E * KF * D])
        b1 = sb("b1", [P, E * KF])
        b2 = sb("b2", [P, E * D])
        slot = sb("slot", [P, TC], I32)
        tile_expert = sb("tile_expert", [P, NT + 2], I32)
        gates = sb("gates", [P, T, C])
        w_loaded, b_loaded = sem("w_loaded"), sem("b_loaded")

        def load_expert(eng, e):
            if e >= 1:
                eng.wait_ge(w_loaded, 32 * e)
            eng.dma_start(w1[:, e * KD * F:(e + 1) * KD * F], g["L%d_ffn_w1" % layer][e]).then_inc(w_loaded, 16)
            eng.dma_start(w2[:, e * KF * D:(e + 1) * KF * D], g["L%d_ffn_w2" % layer][e]).then_inc(w_loaded, 16)

        dispatch(nc, g, layer, slot, tile_expert, gates, load_expert, b1, b2, b_loaded)
        multiply(nc, g, layer, w1, w2, b1, b2, tile_expert, load_expert, w_loaded, b_loaded)
        collect(nc, g, layer, slot, gates)


EARLY = 1


def dispatch(nc, g, layer, slot, tile_expert, gates, load_expert, b1, b2, b_loaded):
    C = layer + 1
    TC = T * C
    NT = tiles_of(C)
    xs = g["xs%d" % layer]
    PS, X, LG, ones = g["PS"], g["X"], g["LG"], g["ones"]
    ctx = ExitStack()
    with ctx:
        def sb(name, shape, dt=F32):
            return ctx.enter_context(nc.sbuf_tensor("d%d_%s" % (layer, name), shape, dt))

        def sem(name):
            return ctx.enter_context(nc.semaphore("d%d_%s" % (layer, name)))

        before = sb("before", [P, P])
        iota = sb("iota", [P, NT + 2], I32)
        iotaf = sb("iotaf", [P, NT + 2])
        less = sb("less", [P, E])
        again = sb("again", [P, E, TC])
        lg2 = sb("lg2", [P, T, E])
        top = sb("top", [P, C, T])
        eq = sb("eq", [P, T, E])
        cand = sb("cand", [P, T, E])
        low = sb("low", [P, T])
        oh = sb("oh", [P, T, C, E])
        ex = sb("ex", [P, T, E])
        gd = sb("gd", [P, T])
        tot = sb("tot", [P, E, TC])
        cum = sb("cum", [P, E, TC])
        more = sb("more", [P, E, T])
        ntile = sb("ntile", [P, E])
        tend = sb("tend", [P, E])
        row0 = sb("row0", [P, E])
        base = sb("base", [P, E, TC])
        at = sb("at", [P, TC, E])
        slotf = sb("slotf", [P, TC])
        past = sb("past", [P, NT + 2, E])
        tef = sb("tef", [P, NT + 2])

        consts, chain, bchain = sem("consts"), sem("chain"), sem("bchain")
        oh_ready, counted, slot_ready = sem("oh_ready"), sem("counted"), sem("slot_ready")
        ex_in, ex_done, scattered = sem("ex_in"), sem("ex_done"), sem("scattered")
        stats_ready, rs_ready, xn_done, xn_ready = sem("stats_ready"), sem("rs_ready"), sem("xn_done"), sem("xn_ready")
        if layer == 0:
            xn = sb("xn", [P, T, D])
            lng = sb("lng", [P, D])
            lnb = sb("lnb", [P, D])
            bn = sb("bn", [P, T, 6])
            mv = sb("mv", [P, T, 2])
            rs = sb("rs", [P, T])
            ln_loaded = sem("ln_loaded")
        rows = xn if layer == 0 else X
        block = ctx.enter_context(nc.Block())

        @block.sync
        def _(sp):
            if layer == 0:
                sp.dma_start(lng[:], g["L0_ffn_ln_g"]).then_inc(ln_loaded, 16)
                sp.dma_start(lnb[:], g["L0_ffn_ln_b"]).then_inc(ln_loaded, 16)
            sp.dma_start(b1[:], g["L%d_ffn_b1" % layer]).then_inc(b_loaded, 16)
            sp.dma_start(b2[:], g["L%d_ffn_b2" % layer]).then_inc(b_loaded, 16)

        @block.gpsimd
        def _(pool):
            for e in range(EARLY):
                load_expert(pool, e)
            nc.gpsimd.memset(before[:], 1.0).then_inc(consts, 1)
            pool.wait_ge(consts, 1)
            nc.gpsimd.affine_select(out=before[:], in_=before[:], compare_op=ALU.is_gt, fill=0.0, base=0,
                                    pattern=[[1, P]], channel_multiplier=-1).then_inc(consts, 1)
            nc.gpsimd.iota(iota[:], [[1, NT + 2]], base=0, channel_multiplier=0).then_inc(consts, 1)
            nc.gpsimd.memset(again[:], 1.0).then_inc(consts, 1)
            pool.wait_ge(consts, 4)
            nc.gpsimd.memset(again[:, :, 0:1], 0.0).then_inc(consts, 1)
            nc.gpsimd.tensor_copy(iotaf[:], iota[:]).then_inc(consts, 1)
            if layer == 0:
                pool.wait_ge(stats_ready, T)
                nc.gpsimd.tensor_scalar(rs[:], mv[:, :, 1], LN_EPS, None, ALU.add).then_inc(rs_ready, 1)
                pool.wait_ge(rs_ready, 1)
                nc.gpsimd.tensor_tensor(rs[:], rs[:], g["mhalf"][:].to_broadcast([P, T]), ALU.pow).then_inc(rs_ready, 1)
            pool.wait_ge(slot_ready, 1)
            pool.wait_ge(g["xs_cleared"], 16 * 2)
            for t in range(T):
                if layer == 0:
                    pool.wait_ge(xn_ready, t + 1)
                for c in range(C):
                    n = t * C + c
                    pool.indirect_dma_start(out=xs[:, :], out_offset=bass.IndirectOffsetOnAxis(ap=slot[:, n:n + 1].bitcast(U32), axis=0),
                                            in_=rows[:, t, :], in_offset=None).then_inc(scattered, 16)
            pool.wait_ge(scattered, 16 * TC)

        @block.scalar
        def _(act):
            act.wait_ge(ex_in, 1)
            if C == 1:
                nc.scalar.activation(ex[:], ex[:], ACT.Exp).then_inc(ex_done, 1)
            else:
                nc.scalar.activation(gd[:], gd[:], ACT.Exp).then_inc(ex_done, 1)

        @block.vector
        def _(dve):
            n = [0]

            def link(ins):
                n[0] += 1
                ins.then_inc(chain, 1)
                dve.wait_ge(chain, n[0])

            dve.wait_ge(consts, 6)
            link(nc.vector.tensor_scalar(less[:], iotaf[:, 0:E], -100.0, None, ALU.add))
            for c in range(C):
                src = LG if c == 0 else lg2
                link(nc.vector.reduce_max(top[:, c, :], src[:], AX_X))
                link(nc.vector.tensor_tensor(eq[:], src[:], top[:, c, :, None].to_broadcast([P, T, E]), ALU.is_equal))
                link(nc.vector.tensor_scalar(cand[:], eq[:], -100.0, None, ALU.mult))
                link(nc.vector.tensor_tensor(cand[:], cand[:], iotaf[:, None, 0:E].to_broadcast([P, T, E]), ALU.add))
                link(nc.vector.tensor_reduce(low[:], cand[:], AX_X, ALU.min))
                ins = nc.vector.tensor_tensor(oh[:, :, c, :], less[:, None, :].to_broadcast([P, T, E]),
                                              low[:, :, None].to_broadcast([P, T, E]), ALU.is_equal)
                if c < C - 1:
                    link(ins)
                    link(nc.vector.tensor_scalar(lg2[:], oh[:, :, c, :], -1e30, None, ALU.mult))
                    link(nc.vector.tensor_tensor(lg2[:], lg2[:], LG[:], ALU.add))
                else:
                    ins.then_inc(oh_ready, 1)
            if C == 1:
                nc.vector.tensor_tensor(ex[:], LG[:], top[:, 0, :, None].to_broadcast([P, T, E]),
                                        ALU.subtract).then_inc(ex_in, 1)
            else:
                nc.vector.tensor_tensor(gd[:], top[:, 1, :], top[:, 0, :], ALU.subtract).then_inc(ex_in, 1)
            if layer == 0:
                for t in range(T):
                    nc.vector.bn_stats(bn[:, t, :], X[:, t, :]).then_inc(bchain, 1)
                for t in range(T):
                    dve.wait_ge(bchain, t + 1)
                    nc.vector.bn_aggr(mv[:, t, :], bn[:, t, :]).then_inc(stats_ready, 1)
            dve.wait_ge(ex_done, 1)
            if C == 1:
                link(nc.vector.reduce_sum(gd[:], ex[:], AX_X))
                link(nc.vector.reciprocal(gates[:, :, 0], gd[:]))
            else:
                link(nc.vector.tensor_scalar(low[:], gd[:], 1.0, None, ALU.add))
                link(nc.vector.reciprocal(gates[:, :, 0], low[:]))
                link(nc.vector.tensor_tensor(gates[:, :, 1], gates[:, :, 0], gd[:], ALU.mult))
            dve.wait_ge(counted, 1)
            sums = PS[:, 1, 0:TC * E].rearrange("p (n e) -> p e n", e=E)
            link(nc.vector.tensor_copy(tot[:], sums))
            flat = lambda a: a[:].rearrange("p e n -> p (e n)")
            link(nc.vector.tensor_tensor_scan(flat(cum), flat(again), flat(tot), 0.0, ALU.mult, ALU.add))
            link(nc.vector.tensor_scalar(slotf[:, 0:T], iotaf[:, 0:T], float(P), None, ALU.mult))
            link(nc.vector.tensor_tensor(more[:], cum[:, :, TC - 1:TC].to_broadcast([P, E, T]),
                                         slotf[:, None, 0:T].to_broadcast([P, E, T]), ALU.is_gt))
            link(nc.vector.reduce_sum(ntile[:], more[:], AX_X))
            link(nc.vector.tensor_tensor_scan(tend[:], ones[:, 0:E], ntile[:], 0.0, ALU.mult, ALU.add))
            link(nc.vector.tensor_tensor(row0[:], tend[:], ntile[:], ALU.subtract))
            link(nc.vector.tensor_scalar(row0[:], row0[:], float(P), None, ALU.mult))
            link(nc.vector.tensor_tensor(base[:], cum[:], tot[:], ALU.subtract))
            link(nc.vector.tensor_tensor(base[:], base[:], row0[:, :, None].to_broadcast([P, E, TC]), ALU.add))
            link(nc.vector.tensor_tensor(at[:], PS[:, 0, 0:TC * E].rearrange("p (n e) -> p n e", e=E),
                                         base[:].rearrange("p e n -> p n e"), ALU.add))
            link(nc.vector.tensor_tensor(at[:], at[:], oh[:].rearrange("p t c e -> p (t c) e"), ALU.mult))
            link(nc.vector.reduce_sum(slotf[:], at[:], AX_X))
            nc.vector.tensor_copy(slot[:], slotf[:]).then_inc(slot_ready, 1)
            if layer == 0:
                dve.wait_ge(rs_ready, 2)
                dve.wait_ge(ln_loaded, 32)
                for t in range(T):
                    link(nc.vector.tensor_scalar(xn[:, t, :], X[:, t, :], mv[:, t, 0:1], rs[:, t:t + 1],
                                                 ALU.subtract, ALU.mult))
                    link(nc.vector.tensor_tensor(xn[:, t, :], xn[:, t, :], lng[:], ALU.mult))
                    nc.vector.tensor_tensor(xn[:, t, :], xn[:, t, :], lnb[:], ALU.add).then_inc(xn_ready, 1)
            link(nc.vector.tensor_tensor(past[:], iotaf[:, :, None].to_broadcast([P, NT + 2, E]),
                                         tend[:, None, :].to_broadcast([P, NT + 2, E]), ALU.is_ge))
            link(nc.vector.reduce_sum(tef[:], past[:], AX_X))
            link(nc.vector.tensor_scalar(tef[:], tef[:], float(E - 1), None, ALU.min))
            link(nc.vector.tensor_copy(tile_expert[:], tef[:]))

        @block.tensor
        def _(pe):
            pe.wait_ge(oh_ready, 1)
            pe.wait_ge(consts, 2)
            flat = oh[:].rearrange("p t c e -> p (t c e)")
            nc.tensor.matmul(PS[:, 0, 0:TC * E], before[:], flat, start=True, stop=True)
            nc.tensor.matmul(PS[:, 1, 0:TC * E], ones[:], flat, start=True, stop=True).then_inc(counted, 1)


def multiply(nc, g, layer, w1, w2, b1, b2, tile_expert, load_expert, w_loaded, b_loaded):
    C = layer + 1
    NT = tiles_of(C)
    xs, ys = g["xs%d" % layer], g["ys%d" % layer]
    PS, ident = g["PS"], g["ident"]
    XB, HB, TB, YB = 0, 1, 3, 5
    ctx = ExitStack()
    with ctx:
        def sb(name, shape, dt=F32):
            return ctx.enter_context(nc.sbuf_tensor("m%d_%s" % (layer, name), shape, dt))

        def sem(name):
            return ctx.enter_context(nc.semaphore("m%d_%s" % (layer, name)))

        xin = sb("xin", [P, D])
        xT = sb("xT", [P, KD, P])
        hrow = sb("hrow", [P, F])
        hT = sb("hT", [P, KF, P])
        y = sb("y", [P, D])
        xin_loaded, xT_done, xT_ready = sem("xin_loaded"), sem("xT_done"), sem("xT_ready")
        h_done, hrow_ready, hT_done, hT_ready = sem("h_done"), sem("hrow_ready"), sem("hT_done"), sem("hT_ready")
        y_done, y_ready, y_free = sem("y_done"), sem("y_ready"), sem("y_free")
        pace = sem("pace")
        block = ctx.enter_context(nc.Block())
        rows = lambda a, i: a[bass.ds(i * P, P), :]

        @block.sync
        def _(sp):
            sp.dma_start(xin[:], xs[0:P, :]).then_inc(xin_loaded, 16)
            sp.wait_ge(xT_done, 1)
            sp.dma_start(xin[:], xs[P:2 * P, :]).then_inc(xin_loaded, 16)
            sp.sem_inc(y_free, 16)
            with sp.Fori(1, NT + 1) as it:
                sp.wait_ge(xT_done, it + 1)
                sp.dma_start(xin[:], rows(xs, it + 1)).then_inc(xin_loaded, 16)
                sp.wait_ge(y_ready, it)
                sp.dma_start(rows(ys, it - 1), y[:]).then_inc(y_free, 16)
            sp.wait_ge(y_free, 16 * (NT + 1))
            sp.wait_ge(xin_loaded, 16 * (NT + 2))

        @block.gpsimd
        def _(pool):
            for e in range(EARLY, E):
                load_expert(pool, e)
            pool.wait_ge(w_loaded, 32 * E)

        @block.tensor
        def _(pe):
            def turn_tile():
                for k in range(KD):
                    mm = nc.tensor.transpose(PS[:, XB, k * P:(k + 1) * P], xin[:, k * P:(k + 1) * P], ident[:])
                mm.then_inc(xT_done, 1)

            def hidden(e):
                pe.wait_ge(w_loaded, e * 32 + 32)
                pe.sem_inc(pace, 1)
                for n in range(F // 512):
                    for k in range(KD):
                        mm = nc.tensor.matmul(PS[:, HB + n, :], xT[:, k, :],
                                              w1[:, bass.ds(e * (KD * F) + (k * F + n * 512), 512)],
                                              start=(k == 0), stop=(k == KD - 1))
                mm.then_inc(h_done, 1)

            pe.wait_ge(xin_loaded, 16)
            turn_tile()
            pe.wait_ge(xT_ready, 1)
            hidden(pe.value_load(tile_expert[0:1, 0:1], min_val=0, max_val=E - 1))
            pe.wait_ge(xin_loaded, 32)
            turn_tile()
            with pe.Fori(1, NT + 1) as it:
                e = pe.value_load(tile_expert[0:1, bass.ds(it - 1, 1)], min_val=0, max_val=E - 1)
                e1 = pe.value_load(tile_expert[0:1, bass.ds(it, 1)], min_val=0, max_val=E - 1)
                pe.wait_ge(hrow_ready, it)
                pe.sem_inc(pace, 1)
                for c in range(KF):
                    mm = nc.tensor.transpose(PS[:, TB + c // 4, (c % 4) * P:(c % 4 + 1) * P],
                                             hrow[:, c * P:(c + 1) * P], ident[:])
                mm.then_inc(hT_done, 1)
                pe.wait_ge(xT_ready, it + 1)
                pe.sem_inc(pace, 1)
                hidden(e1)
                pe.wait_ge(xin_loaded, it * 16 + 32)
                pe.sem_inc(pace, 1)
                turn_tile()
                pe.wait_ge(hT_ready, it)
                pe.sem_inc(pace, 1)
                for c in range(KF):
                    mm = nc.tensor.matmul(PS[:, YB, 0:D], hT[:, c, :], w2[:, bass.ds(e * (KF * D) + c * D, D)],
                                          start=(c == 0), stop=(c == KF - 1))
                mm.then_inc(y_done, 1)

        def activate(eng, it, e):
            eng.wait_ge(hT_done, it)
            eng.sem_inc(pace, 1)
            for c in range(KF):
                src = PS[:, TB + c // 4, (c % 4) * P:(c % 4 + 1) * P]
                bias = b1[:, bass.ds(e * KF + c, 1)]
                if layer == 0:
                    ins = nc.vector.tensor_scalar(hT[:, c, :], src, bias, 0.0, ALU.add, ALU.max)
                else:
                    ins = nc.scalar.activation(hT[:, c, :], src, ACT.Gelu, bias=bias)
            ins.then_inc(hT_ready, 1)

        @block.scalar
        def _(act):
            turned = PS[:, XB, 0:D].rearrange("p (k n) -> p k n", k=KD)
            hidden_rows = PS[:, HB:HB + 2, :].rearrange("p b n -> p (b n)")
            act.wait_ge(b_loaded, 32)
            act.wait_ge(xT_done, 1)
            nc.scalar.copy(xT[:], turned).then_inc(xT_ready, 1)
            act.wait_ge(h_done, 1)
            nc.scalar.copy(hrow[:], hidden_rows).then_inc(hrow_ready, 1)
            act.wait_ge(xT_done, 2)
            nc.scalar.copy(xT[:], turned).then_inc(xT_ready, 1)
            with act.Fori(1, NT + 1) as it:
                if layer == 1:
                    activate(act, it, act.value_load(tile_expert[0:1, bass.ds(it - 1, 1)], min_val=0, max_val=E - 1))
                act.wait_ge(h_done, it + 1)
                act.sem_inc(pace, 1)
                nc.scalar.copy(hrow[:], hidden_rows).then_inc(hrow_ready, 1)
                act.wait_ge(xT_done, it + 2)
                act.sem_inc(pace, 1)
                nc.scalar.copy(xT[:], turned).then_inc(xT_ready, 1)

        @block.vector
        def _(dve):
            dve.wait_ge(b_loaded, 32)
            with dve.Fori(1, NT + 1) as it:
                e = dve.value_load(tile_expert[0:1, bass.ds(it - 1, 1)], min_val=0, max_val=E - 1)
                if layer == 0:
                    activate(dve, it, e)
                dve.wait_ge(y_free, it * 16)
                dve.sem_inc(pace, 1)
                dve.wait_ge(y_done, it)
                dve.sem_inc(pace, 1)
                nc.vector.tensor_tensor(y[:], PS[:, YB, 0:D], b2[:, bass.ds(e * D, D)], ALU.add).then_inc(y_ready, 1)


def collect(nc, g, layer, slot, gates):
    C = layer + 1
    ys, X = g["ys%d" % layer], g["X"]
    GROUP = 4
    ctx = ExitStack()
    with ctx:
        def sb(name, shape, dt=F32):
            return ctx.enter_context(nc.sbuf_tensor("c%d_%s" % (layer, name), shape, dt))

        def sem(name):
            return ctx.enter_context(nc.semaphore("c%d_%s" % (layer, name)))

        yg = sb("yg", [P, GROUP, C, D])
        bn, mv, ve, rs = sb("bn", [P, T, 6]), sb("mv", [P, T, 2]), sb("ve", [P, T]), sb("rs", [P, T])
        gathered = [sem("gathered%d" % i) for i in range(T // GROUP)]
        chain, stats_ready, rs_ready, used = sem("chain"), sem("stats_ready"), sem("rs_ready"), sem("used")
        block = ctx.enter_context(nc.Block())

        @block.gpsimd
        def _(pool):
            for q in range(T // GROUP):
                if q >= 1:
                    pool.wait_ge(used, q)
                for t in range(q * GROUP, (q + 1) * GROUP):
                    for c in range(C):
                        n = t * C + c
                        pool.indirect_dma_start(out=yg[:, t % GROUP, c, :], out_offset=None, in_=ys[:, :],
                                                in_offset=bass.IndirectOffsetOnAxis(ap=slot[:, n:n + 1].bitcast(U32), axis=0))\
                            .then_inc(gathered[q], 16)
            for q in range(T // GROUP):
                pool.wait_ge(stats_ready, q + 1)
                at = slice(q * GROUP, (q + 1) * GROUP)
                nc.gpsimd.tensor_scalar(ve[:, at], mv[:, at, 1], LN_EPS, None, ALU.add).then_inc(rs_ready, 1)
                pool.wait_ge(rs_ready, 2 * q + 1)
                nc.gpsimd.tensor_tensor(rs[:, at], ve[:, at], g["mhalf"][:].to_broadcast([P, GROUP]), ALU.pow)\
                    .then_inc(rs_ready, 1)

        @block.vector
        def _(dve):
            n = [0]

            def link(ins):
                n[0] += 1
                ins.then_inc(chain, 1)
                dve.wait_ge(chain, n[0])

            for q in range(T // GROUP):
                dve.wait_ge(gathered[q], 16 * GROUP * C)
                for t in range(q * GROUP, (q + 1) * GROUP):
                    for c in range(C):
                        ins = nc.vector.scalar_tensor_tensor(X[:, t, :], yg[:, t % GROUP, c, :], gates[:, t, c:c + 1],
                                                             X[:, t, :], ALU.mult, ALU.add)
                        if c == C - 1 and t % GROUP == GROUP - 1:
                            ins.then_inc(used, 1)
                            dve.wait_ge(used, q + 1)
                        else:
                            link(ins)
                    link(nc.vector.bn_stats(bn[:, t, :], X[:, t, :]))
                    ins = nc.vector.bn_aggr(mv[:, t, :], bn[:, t, :])
                ins.then_inc(stats_ready, 1)
            for q in range(T // GROUP):
                dve.wait_ge(rs_ready, 2 * q + 2)
                for t in range(q * GROUP, (q + 1) * GROUP):
                    nc.vector.tensor_scalar(X[:, t, :], X[:, t, :], mv[:, t, 0:1], rs[:, t:t + 1], ALU.subtract, ALU.mult)


def experts0(nc, top, g):
    experts(nc, top, g, 0)

H1, HD1 = 16, 64
P1 = H1 * HD1
NQ = 3 * P1 // 512


def layer1_attention(nc, top, g):
    ctx = ExitStack()
    with ctx:
        def sb(name, shape, dt=F32):
            return ctx.enter_context(nc.sbuf_tensor("l1_" + name, shape, dt))

        loop_sems = []

        def sem(name, kept=False):
            s = ctx.enter_context(nc.semaphore("l1_" + name))
            if not kept:
                loop_sems.append(s)
            return s

        PS, X, ident = g["PS"], g["X"], g["ident"]
        Xg = X[:].rearrange("p (s g) d -> p s g d", s=B)

        w = sb("w", [P, KD, 3 * P1])
        wb = sb("wb", [P, 3 * P1])
        wo = sb("wo", [P, KF, D])
        bo = sb("bo", [P, D])
        xg = sb("xg", [P, B, D])
        xres = sb("xres", [P, B, D])
        xT = sb("xT", [P, B, KD, P])
        qkv = sb("qkv", [P, B, 3 * P1])
        prod = sb("prod", [P, 2, P1])
        sc = sb("sc", [P, B, B, H1])
        mx = sb("mx", [P, B, H1])
        o = sb("o", [P, B, P1])
        oT = sb("oT", [P, 2, KF, P])
        r = sb("r", [P, B, D])
        bn, mv, ve, rs = sb("bn", [P, B, 6]), sb("mv", [P, B, 2]), sb("ve", [P, B]), sb("rs", [P, B])

        w_loaded, ended, go, pace = sem("w_loaded", True), sem("ended", True), sem("go", True), sem("pace", True)
        chain = sem("chain")
        xg_ready, xT_done, xT_ready = sem("xg_ready"), sem("xT_done"), sem("xT_ready")
        qkv_done, qkv_ready = sem("qkv_done"), sem("qkv_ready")
        sc_ready, ex_ready = sem("sc_ready"), sem("ex_ready")
        o_ready, oT_done, oT_ready, proj_done = sem("o_ready"), sem("oT_done"), sem("oT_ready"), sem("proj_done")
        mv_ready, rs_ready = sem("mv_ready"), sem("rs_ready")
        block = ctx.enter_context(nc.Block())
        CHUNKS = [(s, n) for s in range(B) for n in range(4)] + [(s, n) for s in range(B) for n in (4, 5)]
        NB = 6

        @block.sync
        def _(sp):
            for dst, src in ((w, "L1_attn_w"), (wb, "L1_attn_b"), (wo, "L1_attn_wo"), (bo, "L1_attn_bo")):
                sp.dma_start(dst[:], g[src]).then_inc(w_loaded, 16)
            sp.sem_inc(go, 1)
            with sp.Fori(1, J + 1) as it:
                each(sp, go, pace, it)
                turn(sp, ended, go, pace, it, loop_sems)

        @block.gpsimd
        def _(pool):
            with pool.Fori(1, J + 1) as it:
                each(pool, go, pace, it)
                for s in range(B):
                    pool.wait_ge(mv_ready, s + 1)
                    nc.gpsimd.tensor_scalar(ve[:, s:s + 1], mv[:, s, 1:2], LN_EPS, None, ALU.add).then_inc(rs_ready, 1)
                    pool.wait_ge(rs_ready, 2 * s + 1)
                    nc.gpsimd.tensor_tensor(rs[:, s:s + 1], ve[:, s:s + 1], g["mhalf"][:], ALU.pow).then_inc(rs_ready, 1)
                ends(pool, ended)

        @block.scalar
        def _(act):
            with act.Fori(1, J + 1) as it:
                each(act, go, pace, it)
                act.wait_ge(xT_done, 1)
                nc.scalar.copy(xT[:].rearrange("p s k n -> p (s k n)"),
                               PS[:, 6:8, :].rearrange("p b n -> p (b n)")).then_inc(xT_ready, 1)
                act.wait_ge(sc_ready, 1)
                nc.scalar.activation(sc[:], sc[:], ACT.Exp, scale=HD1 ** -0.5).then_inc(ex_ready, 1)
                for s in range(B):
                    act.wait_ge(oT_done, s + 1)
                    if s >= 2:
                        act.wait_ge(proj_done, s - 1)
                    nc.scalar.copy(oT[:, s % 2].rearrange("p c n -> p (c n)"),
                                   PS[:, 6:8, :].rearrange("p b n -> p (b n)")).then_inc(oT_ready, 1)
                ends(act, ended)

        @block.vector
        def _(dve):
            n = [0]

            def link(ins):
                n[0] += 1
                ins.then_inc(chain, 1)
                dve.wait_ge(chain, n[0])

            dve.wait_ge(w_loaded, 64)
            with dve.Fori(1, J + 1) as it:
                each(dve, go, pace, it)
                n[0] = 0
                nc.vector.tensor_copy(xg[:], Xg[:, :, bass.ds(it - 1, 1), :].rearrange("p s o d -> p (s o) d"))\
                    .then_inc(xg_ready, 1)
                dve.wait_ge(xg_ready, 1)
                link(nc.vector.tensor_tensor(xres[:], xg[:], bo[:, None, :].to_broadcast([P, B, D]), ALU.add))

                def add_bias(c):
                    s, m = CHUNKS[c]
                    dve.wait_ge(qkv_done, c + 1)
                    at = slice(m * 512, (m + 1) * 512)
                    nc.vector.tensor_tensor(qkv[:, s, at], PS[:, c % NB, :], wb[:, at], ALU.add).then_inc(qkv_ready, 1)

                def heads(s, part):
                    return qkv[:, s, part * P1:(part + 1) * P1].rearrange("p (h d) -> p h d", d=HD1)

                for c in range(4 * B):
                    add_bias(c)
                dve.wait_ge(qkv_ready, 4 * B)
                for i in range(B * B):
                    s, t = i // B, i % B
                    pv = prod[:, i % 2, :].rearrange("p (h d) -> p h d", d=HD1)
                    link(nc.vector.tensor_tensor(pv, heads(s, 0), heads(t, 1), ALU.mult))
                    link(nc.vector.reduce_sum(sc[:, s, t, :], pv, AX_X))
                    if i % 2 == 1:
                        add_bias(4 * B + i // 2)
                link(nc.vector.reduce_max(mx[:], sc[:].rearrange("p s t h -> p s h t"), AX_X))
                nc.vector.tensor_tensor(sc[:], sc[:], mx[:, :, None, :].to_broadcast([P, B, B, H1]),
                                        ALU.subtract).then_inc(sc_ready, 1)
                dve.wait_ge(ex_ready, 1)
                link(nc.vector.reduce_sum(mx[:], sc[:].rearrange("p s t h -> p s h t"), AX_X))
                link(nc.vector.reciprocal(mx[:], mx[:]))
                link(nc.vector.tensor_tensor(sc[:], sc[:], mx[:, :, None, :].to_broadcast([P, B, B, H1]), ALU.mult))
                dve.wait_ge(qkv_ready, NQ * B)

                def mixed(s):
                    ov = o[:, s, :].rearrange("p (h d) -> p h d", d=HD1)
                    for t in range(B):
                        pv = ov if t == 0 else prod[:, t % 2, :].rearrange("p (h d) -> p h d", d=HD1)
                        link(nc.vector.tensor_tensor(pv, heads(t, 2),
                                                     sc[:, s, t, :, None].to_broadcast([P, H1, HD1]), ALU.mult))
                        if t:
                            ins = nc.vector.tensor_tensor(ov, ov, pv, ALU.add)
                            if t < B - 1:
                                link(ins)
                    ins.then_inc(o_ready, 1)

                def residual(s):
                    dve.wait_ge(proj_done, s + 1)
                    link(nc.vector.tensor_tensor(r[:, s, :], PS[:, s, 0:D], xres[:, s, :], ALU.add))
                    link(nc.vector.bn_stats(bn[:, s, :], r[:, s, :]))
                    nc.vector.bn_aggr(mv[:, s, :], bn[:, s, :]).then_inc(mv_ready, 1)

                def norm(s):
                    dve.wait_ge(rs_ready, 2 * s + 2)
                    link(nc.vector.tensor_scalar(r[:, s, :], r[:, s, :], mv[:, s, 0:1], rs[:, s:s + 1],
                                                 ALU.subtract, ALU.mult))

                for s in range(B + 2):
                    if s < B:
                        mixed(s)
                    if 0 <= s - 1 < B:
                        residual(s - 1)
                    if 0 <= s - 2 < B:
                        norm(s - 2)
                nc.vector.tensor_copy(Xg[:, :, bass.ds(it - 1, 1), :].rearrange("p s o d -> p (s o) d"), r[:])
                ends(dve, ended)

        @block.tensor
        def _(pe):
            pe.wait_ge(w_loaded, 64)
            with pe.Fori(1, J + 1) as it:
                each(pe, go, pace, it)
                pe.wait_ge(xg_ready, 1)
                for s in range(B):
                    for k in range(KD):
                        n = s * KD + k
                        mm = nc.tensor.transpose(PS[:, 6 + n // 4, (n % 4) * P:(n % 4 + 1) * P],
                                                 xg[:, s, k * P:(k + 1) * P], ident[:])
                mm.then_inc(xT_done, 1)
                pe.wait_ge(xT_ready, 1)
                for c, (s, m) in enumerate(CHUNKS):
                    if c >= NB:
                        pe.wait_ge(qkv_ready, c - NB + 1)
                    for k in range(KD):
                        mm = nc.tensor.matmul(PS[:, c % NB, :], xT[:, s, k, :], w[:, k, m * 512:(m + 1) * 512],
                                              start=(k == 0), stop=(k == KD - 1))
                    mm.then_inc(qkv_done, 1)
                pe.wait_ge(qkv_ready, NQ * B)

                def turn_out(s):
                    pe.wait_ge(o_ready, s + 1)
                    if s >= 1:
                        pe.wait_ge(oT_ready, s)
                    for c in range(KF):
                        mm = nc.tensor.transpose(PS[:, 6 + c // 4, (c % 4) * P:(c % 4 + 1) * P],
                                                 o[:, s, c * P:(c + 1) * P], ident[:])
                    mm.then_inc(oT_done, 1)

                def project(s):
                    pe.wait_ge(oT_ready, s + 1)
                    for c in range(KF):
                        mm = nc.tensor.matmul(PS[:, s, 0:D], oT[:, s % 2, c, :], wo[:, c, :],
                                              start=(c == 0), stop=(c == KF - 1))
                    mm.then_inc(proj_done, 1)

                for s in range(B):
                    turn_out(s)
                    project(s)
                ends(pe, ended)

HX, HDX = 8, 64
PX = HX * HDX


def layer1_cross(nc, top, g):
    S2 = g["S2"]
    KEYS = S2 + S
    CT = -(-S2 // P)
    LAST = S2 - (CT - 1) * P
    KT = -(-KEYS // P)
    KLAST = KEYS - (KT - 1) * P
    CH = [(c * 512, min(512, KEYS - c * 512)) for c in range(-(-KEYS // 512))]
    NCH = len(CH)
    FIRST = 2
    ROWS = HX * J
    ctx = ExitStack()
    with ctx:
        def sb(name, shape, dt=F32):
            return ctx.enter_context(nc.sbuf_tensor("x_" + name, shape, dt))

        loop_sems = []

        def sem(name, kept=False):
            s = ctx.enter_context(nc.semaphore("x_" + name))
            if not kept:
                loop_sems.append(s)
            return s

        PS, X, LG, ident = g["PS"], g["X"], g["LG"], g["ident"]
        wq, wk, wv = sb("wq", [P, KD, PX]), sb("wk", [P, KD, PX]), sb("wv", [P, KD, PX])
        wo = sb("wo", [P, PX // P, D])
        wg = sb("wg", [P, KD, E])
        cols = sb("cols", [P, 4 * KD + 1])
        cx = sb("cx", [P, CT, D])
        lx = sb("lx", [P, J, D])
        ln = sb("ln", [P, J, D])
        NS = CT + J
        bn, mv, ve, rs = sb("bn", [P, NS, 6]), sb("mv", [P, NS, 2]), sb("ve", [P, NS]), sb("rs", [P, NS])
        kvT = sb("kvT", [P, KD, KEYS])
        latT = sb("latT", [P, KD, S])
        kT = sb("kT", [P, HX // 2, KEYS])
        v = sb("v", [P, KT, PX])
        qz = sb("qz", [P, HX, S])
        mask8 = sb("mask8", [P, S2], U8)
        maskf = sb("maskf", [P, KEYS])
        sm = sb("sm", [P, 2, KEYS])
        mx = sb("mx", [P, 2, 2])
        nm = sb("nm", [P, 2])
        rsum = sb("rsum", [P, 4])
        rrec = sb("rrec", [P, 2])
        pT = sb("pT", [P, 2, KT, P])
        place = kvT[:].rearrange("p k n -> p (k n)")
        o = place[:, 0:J * PX].rearrange("p (j n) -> p j n", j=J)
        oT = place[:, J * PX:J * PX + 2 * PX].rearrange("p (b c n) -> p b c n", b=2, n=P)
        x5 = place[:, J * PX + 2 * PX:J * PX + 2 * PX + J * D].rearrange("p (j d) -> p j d", j=J)
        x5T = sb("x5T", [P, 2, KD, P])

        w_loaded, ended, go, pace = sem("w_loaded", True), sem("ended", True), sem("go", True), sem("pace", True)
        consts = sem("consts", True)
        chain, bchain = sem("chain"), sem("bchain")
        cx_loaded, mask_loaded, lx_ready = sem("cx_loaded"), sem("mask_loaded"), sem("lx_ready")
        stats_ready, rs_ready, ln_ready = sem("stats_ready"), sem("rs_ready"), sem("ln_ready")
        nT_done, nT_ready, gated = sem("nT_done"), sem("nT_ready"), sem("gated")
        kv_done, kv_ready, kv_ready2 = sem("kv_done"), sem("kv_ready"), sem("kv_ready2")
        s_done, s_read, nm_ready, p_ready = sem("s_done"), sem("s_read"), sem("nm_ready"), sem("p_ready")
        pT_done, pT_act, pT_dve = sem("pT_done"), sem("pT_act"), sem("pT_dve")
        av_done, o_ready = sem("av_done"), sem("o_ready")
        oT_done, oT_ready, proj_done = sem("oT_done"), sem("oT_ready"), sem("proj_done")
        mv_ready, rs5_ready, x5_ready = sem("mv_ready"), sem("rs5_ready"), sem("x5_ready")
        x5T_done, x5T_ready, lg_done = sem("x5T_done"), sem("x5T_ready"), sem("lg_done")
        block = ctx.enter_context(nc.Block())

        GROUPS = [("lat", 0, J)] + [("ctx", t, min(4, CT - t)) for t in range(0, CT, 4)]
        MADE = [("q", i, 0) for i in range(HX // 2)] + \
               [("k", i, c) for i in range(HX // 2) for c in range(NCH)] + [("v", t, 0) for t in range(KT)]

        def width(t0, nt):
            return min(S2, (t0 + nt) * P) - t0 * P

        def keys(t):
            return P if t < KT - 1 else KLAST

        def move_turned(copy, r, q):
            bank = PS[:, 5 + (r * NCH + q) % 2, :]
            if q < NCH - 1:
                return copy(pT[:, r % 2, 4 * q:4 * q + 4, :].rearrange("p t n -> p (t n)"), bank)
            return copy(pT[0:KLAST, r % 2, KT - 1, :], bank[0:KLAST, 0:P])

        @block.sync
        def _(sp):
            for dst, src in ((wq, "L1_xattn_Wq"), (wk, "L1_xattn_Wk"), (wv, "L1_xattn_Wv"), (wo, "L1_xattn_Wout"),
                             (wg, "L1_ffn_gate"), (cols, "L1_xattn_cols")):
                sp.dma_start(dst[:], g[src]).then_inc(w_loaded, 16)
            sp.sem_inc(go, 1)
            with sp.Fori(1, B + 1) as it:
                each(sp, go, pace, it)
                c = g["ctx"][bass.ds(it - 1, 1)].rearrange("o s d -> (o s) d")
                sp.dma_start(cx[:, 0:CT - 1, :], c[0:(CT - 1) * P, :].rearrange("(t p) d -> p t d", p=P)).then_inc(cx_loaded, 16)
                sp.dma_start(cx[0:LAST, CT - 1, :], c[(CT - 1) * P:S2, :]).then_inc(cx_loaded, 16)
                sp.dma_start(mask8[:], g["mask"][bass.ds(it - 1, 1), :].to_broadcast([P, S2])).then_inc(mask_loaded, 16)
                turn(sp, ended, go, pace, it, loop_sems)

        @block.gpsimd
        def _(pool):
            nc.gpsimd.memset(maskf[:], 0.0).then_inc(consts, 1)
            nc.gpsimd.memset(qz[:], 0.0).then_inc(consts, 1)
            with pool.Fori(1, B + 1) as it:
                each(pool, go, pace, it)
                pool.wait_ge(stats_ready, 1)
                nc.gpsimd.tensor_scalar(ve[:], mv[:, :, 1], LN_EPS, None, ALU.add).then_inc(rs_ready, 1)
                pool.wait_ge(rs_ready, 1)
                nc.gpsimd.tensor_tensor(rs[:], ve[:], g["mhalf"][:].to_broadcast([P, NS]), ALU.pow).then_inc(rs_ready, 1)
                for j in range(J):
                    pool.wait_ge(mv_ready, j + 1)
                    nc.gpsimd.tensor_scalar(ve[:, j:j + 1], mv[:, j, 1:2], LN_EPS, None, ALU.add).then_inc(rs5_ready, 1)
                    pool.wait_ge(rs5_ready, 2 * j + 1)
                    nc.gpsimd.tensor_tensor(rs[:, j:j + 1], ve[:, j:j + 1], g["mhalf"][:], ALU.pow).then_inc(rs5_ready, 1)
                ends(pool, ended)

        @block.scalar
        def _(act):
            act.wait_ge(w_loaded, 16 * 6)
            act.wait_ge(consts, 2)
            with act.Fori(1, B + 1) as it:
                each(act, go, pace, it)
                for i, (kind, t0, nt) in enumerate(GROUPS):
                    for k in range(KD):
                        n = i * KD + k
                        act.wait_ge(nT_done, n + 1)
                        if kind == "lat":
                            dst, wd, at = latT[:, k, :], S, 2 * KD
                        else:
                            wd, at = width(t0, nt), 0
                            dst = kvT[:, k, t0 * P:t0 * P + wd]
                        nc.scalar.activation(dst, PS[:, n % 4, 0:wd], ACT.Identity, bias=cols[:, at + KD + k:at + KD + k + 1],
                                             scale=cols[:, at + k:at + k + 1]).then_inc(nT_ready, 1)
                for i, (kind, a, c) in enumerate(MADE):
                    if i % 2:
                        continue
                    act.wait_ge(kv_done, i + 1)
                    src = PS[:, 4 + i % 4, :]
                    if kind == "q":
                        for h in range(2):
                            at = slice(64 * h, 64 * h + 64)
                            ins = nc.scalar.mul(qz[at, 2 * a + h, :], src[at, :], HDX ** -0.5)
                    elif kind == "k":
                        ins = nc.scalar.copy(kT[:, a, CH[c][0]:CH[c][0] + CH[c][1]], src[:, 0:CH[c][1]])
                    else:
                        ins = nc.scalar.copy(v[0:keys(a), a, :], src[0:keys(a), :])
                    ins.then_inc(kv_ready, 1)
                for r in range(ROWS + 1):
                    if r >= 1:
                        for q in (0, 2, 4):
                            act.wait_ge(pT_done, (r - 1) * NCH + q + 1)
                            if r - 1 >= 2:
                                act.wait_ge(av_done, r - 2)
                            move_turned(nc.scalar.copy, r - 1, q).then_inc(pT_act, 1)
                    if r < ROWS:
                        act.wait_ge(nm_ready, r + 1)
                        if r >= 4:
                            act.wait_ge(o_ready, r - 3)
                        nc.scalar.activation(sm[:, r % 2, :], sm[:, r % 2, :], ACT.Exp, bias=nm[:, r % 2:r % 2 + 1],
                                             accum_out=rsum[:, r % 4:r % 4 + 1]).then_inc(p_ready, 1)
                for j in range(J):
                    act.wait_ge(oT_done, j + 1)
                    if j >= 2:
                        act.wait_ge(proj_done, j - 1)
                    nc.scalar.copy(oT[:, j % 2].rearrange("p c n -> p (c n)"), PS[:, j % 2, :]).then_inc(oT_ready, 1)
                for j in range(J):
                    act.wait_ge(x5T_done, j + 1)
                    if j >= 2:
                        act.wait_ge(lg_done, j - 1)
                    nc.scalar.copy(x5T[:, j % 2].rearrange("p c n -> p (c n)"), PS[:, 4 + j % 2, 0:D]).then_inc(x5T_ready, 1)
                ends(act, ended)

        @block.vector
        def _(dve):
            n = [0]

            def link(ins):
                n[0] += 1
                ins.then_inc(chain, 1)
                dve.wait_ge(chain, n[0])

            dve.wait_ge(consts, 2)
            with dve.Fori(1, B + 1) as it:
                each(dve, go, pace, it)
                n[0] = 0
                link(nc.vector.tensor_copy(lx[:], X[:, bass.ds(it * J - J, J), :]))
                rows = [(lx[:, j, :], ln[:, j, :], P) for j in range(J)] + \
                       [(cx[0:P if t < CT - 1 else LAST, t, :], cx[0:P if t < CT - 1 else LAST, t, :],
                         P if t < CT - 1 else LAST) for t in range(CT)]
                link(nc.vector.memset(mv[:, NS - 1, :], 1.0))
                for i, (src, _, np_) in enumerate(rows):
                    if i == J:
                        dve.wait_ge(cx_loaded, 32)
                    nc.vector.bn_stats(bn[0:np_, i, :], src).then_inc(bchain, 1)
                for i, (src, _, np_) in enumerate(rows):
                    dve.wait_ge(bchain, i + 1)
                    ins = nc.vector.bn_aggr(mv[0:np_, i, :], bn[0:np_, i, :])
                ins.then_inc(stats_ready, 1)
                dve.wait_ge(mask_loaded, 16)
                link(nc.vector.tensor_scalar(maskf[:, 0:S2], mask8[:], -1e30, None, ALU.mult))
                dve.wait_ge(rs_ready, 2)
                for i, (src, dst, np_) in enumerate(rows):
                    nc.vector.tensor_scalar(dst, src, mv[0:np_, i, 0:1], rs[0:np_, i:i + 1], ALU.subtract, ALU.mult)\
                        .then_inc(ln_ready, 1)
                dve.wait_ge(nT_ready, KD)
                for k in range(KD):
                    ins = nc.vector.tensor_scalar(kvT[:, k, S2:KEYS], latT[:, k, :], cols[:, 4 * KD:4 * KD + 1], None, ALU.mult)
                ins.then_inc(gated, 1)
                for i, (kind, a, c) in enumerate(MADE):
                    if i % 2 == 0:
                        continue
                    dve.wait_ge(kv_done, i + 1)
                    src = PS[:, 4 + i % 4, :]
                    if kind == "q":
                        for h in range(2):
                            at = slice(64 * h, 64 * h + 64)
                            ins = nc.vector.tensor_scalar(qz[at, 2 * a + h, :], src[at, :], HDX ** -0.5, None, ALU.mult)
                    elif kind == "k":
                        ins = nc.vector.tensor_copy(kT[:, a, CH[c][0]:CH[c][0] + CH[c][1]], src[:, 0:CH[c][1]])
                    else:
                        ins = nc.vector.tensor_copy(v[0:keys(a), a, :], src[0:keys(a), :])
                    ins.then_inc(kv_ready2, 1)

                def read_scores(r, part):
                    lo, hi = (0, FIRST) if part == 0 else (FIRST, NCH)
                    a, b = CH[lo][0], CH[hi - 1][0] + CH[hi - 1][1]
                    dve.wait_ge(s_done, 2 * r + part + 1)
                    if r >= 2:
                        dve.wait_ge(pT_done, (r - 1) * NCH)
                    nc.vector.tensor_tensor_reduce(
                        out=sm[:, r % 2, a:b], in0=PS[:, lo:NCH, :].rearrange("p b n -> p (b n)")[:, 0:b - a],
                        in1=maskf[:, a:b], scale=1.0, scalar=-3e38, op0=ALU.add, op1=ALU.max,
                        accum_out=mx[:, r % 2, part:part + 1]).then_inc(s_read, 1)

                def weigh(r):
                    h, q = r // J, r % J
                    dve.wait_ge(p_ready, r + 1)
                    link(nc.vector.reciprocal(rrec[:, r % 2:r % 2 + 1], rsum[:, r % 4:r % 4 + 1]))
                    dve.wait_ge(av_done, r + 1)
                    nc.vector.tensor_scalar(o[:, q, h * HDX:(h + 1) * HDX], PS[:, 7, 0:HDX], rrec[:, r % 2:r % 2 + 1],
                                            None, ALU.mult).then_inc(o_ready, 1)

                for r in range(ROWS + 2):
                    if r < ROWS:
                        read_scores(r, 0)
                    if 0 <= r - 1 < ROWS:
                        for q in (1, 3):
                            dve.wait_ge(pT_done, (r - 1) * NCH + q + 1)
                            if r - 1 >= 2:
                                dve.wait_ge(av_done, r - 2)
                            move_turned(nc.vector.tensor_copy, r - 1, q).then_inc(pT_dve, 1)
                    if r < ROWS:
                        read_scores(r, 1)
                        dve.wait_ge(s_read, 2 * r + 2)
                        if r >= 2:
                            dve.wait_ge(p_ready, r - 1)
                        nc.vector.tensor_scalar(nm[:, r % 2:r % 2 + 1], mx[:, r % 2, 0:1], mx[:, r % 2, 1:2], -1.0,
                                                ALU.max, ALU.mult).then_inc(nm_ready, 1)
                    if r >= 2:
                        weigh(r - 2)
                for j in range(J):
                    dve.wait_ge(proj_done, j + 1)
                    link(nc.vector.tensor_tensor(lx[:, j, :], PS[:, 2 + j % 2, 0:D], lx[:, j, :], ALU.add))
                    link(nc.vector.bn_stats(bn[:, j, :], lx[:, j, :]))
                    nc.vector.bn_aggr(mv[:, j, :], bn[:, j, :]).then_inc(mv_ready, 1)
                for j in range(J):
                    dve.wait_ge(rs5_ready, 2 * j + 2)
                    nc.vector.tensor_scalar(x5[:, j, :], lx[:, j, :], mv[:, j, 0:1], rs[:, j:j + 1], ALU.subtract, ALU.mult)\
                        .then_inc(x5_ready, 1)
                dve.wait_ge(x5_ready, J)
                nc.vector.tensor_copy(X[:, bass.ds(it * J - J, J), :], x5[:])
                dve.wait_ge(lg_done, J)
                nc.vector.tensor_copy(LG[:, bass.ds(it * J - J, J), :],
                                      PS[:, 6, 0:J * E].rearrange("p (j e) -> p j e", e=E))
                ends(dve, ended)

        @block.tensor
        def _(pe):
            pe.wait_ge(w_loaded, 16 * 6)
            with pe.Fori(1, B + 1) as it:
                each(pe, go, pace, it)
                for i, (kind, t0, nt) in enumerate(GROUPS):
                    pe.wait_ge(ln_ready, J if kind == "lat" else J + t0 + nt)
                    for k in range(KD):
                        n = i * KD + k
                        if n >= 4:
                            pe.wait_ge(nT_ready, n - 3)
                        for t in range(nt):
                            if kind == "lat":
                                src, np_ = ln[:, t, k * P:(k + 1) * P], P
                            else:
                                np_ = P if t0 + t < CT - 1 else LAST
                                src = cx[0:np_, t0 + t, k * P:(k + 1) * P]
                            mm = nc.tensor.transpose(PS[:, n % 4, t * P:t * P + np_], src, ident[0:np_, 0:np_])
                        mm.then_inc(nT_done, 1)
                pe.wait_ge(nT_ready, KD)
                for i, (kind, a, c) in enumerate(MADE):
                    if i >= 4:
                        pe.wait_ge(kv_ready if i % 2 == 0 else kv_ready2, (i - 4) // 2 + 1)
                    if i == HX // 2:
                        pe.wait_ge(nT_ready, KD * len(GROUPS))
                        pe.wait_ge(gated, 1)
                    for k in range(KD):
                        if kind == "q":
                            out, lhs, rhs = PS[:, 4 + i % 4, :], wq[:, k, a * P:(a + 1) * P], latT[:, k, :]
                        elif kind == "k":
                            out, lhs = PS[:, 4 + i % 4, 0:CH[c][1]], wk[:, k, a * P:(a + 1) * P]
                            rhs = kvT[:, k, CH[c][0]:CH[c][0] + CH[c][1]]
                        else:
                            out, lhs = PS[0:keys(a), 4 + i % 4, :], kvT[:, k, a * P:a * P + keys(a)]
                            rhs = wv[:, k, :]
                        mm = nc.tensor.matmul(out, lhs, rhs, start=(k == 0), stop=(k == KD - 1))
                    mm.then_inc(kv_done, 1)
                pe.wait_ge(kv_ready, (len(MADE) + 1) // 2)
                pe.wait_ge(kv_ready2, len(MADE) // 2)

                def scores(r, c):
                    h, q = r // J, r % J
                    if r >= 1 and c in (0, FIRST):
                        pe.wait_ge(s_read, 2 * r - 1 if c == 0 else 2 * r)
                    mm = nc.tensor.matmul(PS[:, c, 0:CH[c][1]], qz[:, h, q * P:(q + 1) * P],
                                          kT[:, h // 2, CH[c][0]:CH[c][0] + CH[c][1]], start=True, stop=True)
                    if c in (FIRST - 1, NCH - 1):
                        mm.then_inc(s_done, 1)

                def turn_probs(r, q):
                    if q == 0:
                        pe.wait_ge(p_ready, r + 1)
                    i = r * NCH + q
                    if i >= 2:
                        j = i - 2
                        rr, qq = j // NCH, j % NCH
                        if qq % 2 == 0:
                            pe.wait_ge(pT_act, 3 * rr + qq // 2 + 1)
                        else:
                            pe.wait_ge(pT_dve, 2 * rr + qq // 2 + 1)
                    bank = PS[:, 5 + i % 2, :]
                    for t in range(4 * q, min(4 * q + 4, KT)):
                        mm = nc.tensor.transpose(bank[0:keys(t), (t % 4) * P:(t % 4 + 1) * P],
                                                 sm[:, r % 2, t * P:t * P + keys(t)], ident[:])
                    mm.then_inc(pT_done, 1)

                def values(r):
                    h = r // J
                    pe.wait_ge(pT_act, 3 * r + 3)
                    pe.wait_ge(pT_dve, 2 * r + 2)
                    if r >= 1:
                        pe.wait_ge(o_ready, r)
                    for t in range(KT):
                        mm = nc.tensor.matmul(PS[:, 7, 0:HDX], pT[0:keys(t), r % 2, t, :],
                                              v[0:keys(t), t, h * HDX:(h + 1) * HDX], start=(t == 0), stop=(t == KT - 1))
                    mm.then_inc(av_done, 1)

                for r in range(ROWS + 2):
                    for c in range(NCH):
                        if r < ROWS:
                            scores(r, c)
                        if 0 <= r - 1 < ROWS:
                            turn_probs(r - 1, c)
                    if r >= 2:
                        values(r - 2)
                pe.wait_ge(o_ready, ROWS)
                pe.wait_ge(s_read, 2 * ROWS)
                for j in range(J + 1):
                    if j < J:
                        if j >= 2:
                            pe.wait_ge(oT_ready, j - 1)
                        for c in range(PX // P):
                            mm = nc.tensor.transpose(PS[:, j % 2, c * P:(c + 1) * P], o[:, j, c * P:(c + 1) * P], ident[:])
                        mm.then_inc(oT_done, 1)
                    if j >= 1:
                        i = j - 1
                        pe.wait_ge(oT_ready, i + 1)
                        if i >= 2:
                            pe.wait_ge(mv_ready, i - 1)
                        for c in range(PX // P):
                            mm = nc.tensor.matmul(PS[:, 2 + i % 2, 0:D], oT[:, i % 2, c, :], wo[:, c, :],
                                                  start=(c == 0), stop=(c == PX // P - 1))
                        mm.then_inc(proj_done, 1)
                pe.wait_ge(pT_act, 3 * ROWS)
                pe.wait_ge(pT_dve, 2 * ROWS)
                for j in range(J + 1):
                    if j < J:
                        pe.wait_ge(x5_ready, j + 1)
                        if j >= 2:
                            pe.wait_ge(x5T_ready, j - 1)
                        for k in range(KD):
                            mm = nc.tensor.transpose(PS[:, 4 + j % 2, k * P:(k + 1) * P], x5[:, j, k * P:(k + 1) * P], ident[:])
                        mm.then_inc(x5T_done, 1)
                    if j >= 1:
                        i = j - 1
                        pe.wait_ge(x5T_ready, i + 1)
                        for k in range(KD):
                            mm = nc.tensor.matmul(PS[:, 6, i * E:(i + 1) * E], x5T[:, i % 2, k, :], wg[:, k, :],
                                                  start=(k == 0), stop=(k == KD - 1))
                        mm.then_inc(lg_done, 1)
                ends(pe, ended)


def experts1(nc, top, g):
    experts(nc, top, g, 1)


def expert_inputs(a, layer, names):
    w1, b1, w2, b2 = (a["L%d_ffn_%s" % (layer, n)] for n in names)
    pre = "L%d_ffn_" % layer
    return {
        pre + "w1": w1.reshape(E, KD, P, F).transpose(0, 2, 1, 3).reshape(E, P, KD * F),
        pre + "w2": w2.reshape(E, KF, P, D).transpose(0, 2, 1, 3).reshape(E, P, KF * D),
        pre + "b1": b1.reshape(E, KF, P).transpose(2, 0, 1).reshape(P, E * KF),
        pre + "b2": spread(b2),
    }


def more_inputs(a):
    return {
        "L0_ffn_ln_g": spread(a["L0_ffn_ln_g"]), "L0_ffn_ln_b": spread(a["L0_ffn_ln_b"]),
        "L1_attn_w": rows_of(a["L1_attn_in_proj_weight"].T, KD), "L1_attn_b": spread(a["L1_attn_in_proj_bias"]),
        "L1_attn_wo": rows_of(a["L1_attn_out_proj_weight"].T, KF), "L1_attn_bo": spread(a["L1_attn_out_proj_bias"]),
        "ctx": a["ctx_1024"], "mask": a["mask_BxS2_bk0"],
        "L1_xattn_Wq": rows_of(a["L1_xattn_Wq"], KD), "L1_xattn_Wk": rows_of(a["L1_xattn_Wk"], KD),
        "L1_xattn_Wv": rows_of(a["L1_xattn_Wv"], KD), "L1_xattn_Wout": rows_of(a["L1_xattn_Wout"], PX // P),
        "L1_xattn_cols": np.concatenate(
            [columns(a["L1_xattn_" + n], KD) for n in ("gamma_media", "beta_media", "gamma_lat", "beta_lat")]
            + [np.broadcast_to(a["L1_xattn_kv_gate"].reshape(1, 1), (P, 1))], 1),
        "L1_ffn_gate": rows_of(a["L1_ffn_gate_w"], KD),
        **expert_inputs(a, 0, ("W1", "b1", "W2", "b2")),
        **expert_inputs(a, 1, ("w1", "b1", "w2", "b2")),
    }


def constants(nc, ctx, g):
    sb = lambda name, shape, dt=F32: ctx.enter_context(nc.sbuf_tensor(name, shape, dt))
    g["PS"] = ctx.enter_context(nc.psum_tensor("PS", [P, 8, 512], F32))
    g["X"] = sb("X", [P, T, D])
    g["LG"] = sb("LG", [P, T, E])
    g["ident"] = sb("ident", [P, P])
    g["ones"] = sb("ones", [P, P])
    g["half"] = sb("half", [P, 1])
    g["mhalf"] = sb("mhalf", [P, 1])
    g["x_loaded"] = ctx.enter_context(nc.semaphore("x_loaded"))
    g["consts"] = ctx.enter_context(nc.semaphore("consts_ready"))
    g["xs_cleared"] = ctx.enter_context(nc.semaphore("xs_cleared"))
    zeros = sb("zeros", [P, D])
    for layer in range(2):
        n = tiles_of(layer + 1)
        g["xs%d" % layer] = nc.dram_tensor("xs%d" % layer, ((n + 2) * P, D), F32, kind="Internal").ap()
        g["ys%d" % layer] = nc.dram_tensor("ys%d" % layer, (n * P, D), F32, kind="Internal").ap()
    with nc.Block() as block:
        @block.sync
        def _(sp):
            sp.dma_start(g["X"][:], g["x"]).then_inc(g["x_loaded"], 16)
            sp.wait_ge(g["consts"], 6)
            for layer in range(2):
                n = tiles_of(layer + 1) + 2
                sp.dma_start(g["xs%d" % layer].rearrange("(n p) d -> p n d", p=P),
                             zeros[:, None, :].to_broadcast([P, n, D])).then_inc(g["xs_cleared"], 16)

        @block.gpsimd
        def _(pool):
            pool.memset(g["ident"][:], 0.0).then_inc(g["consts"], 1)
            pool.memset(g["ones"][:], 1.0).then_inc(g["consts"], 1)
            pool.memset(g["half"][:], 0.5).then_inc(g["consts"], 1)
            pool.memset(g["mhalf"][:], -0.5).then_inc(g["consts"], 1)
            pool.wait_ge(g["consts"], 4)
            pool.affine_select(out=g["ident"][:], in_=g["ident"][:], compare_op=ALU.not_equal, fill=1.0, base=0,
                               pattern=[[-1, P]], channel_multiplier=1).then_inc(g["consts"], 1)
            pool.memset(zeros[:], 0.0).then_inc(g["consts"], 1)
        g["n_consts"] = 6


def store(nc, ctx, g):
    stored = ctx.enter_context(nc.semaphore("stored"))
    with nc.Block() as block:
        @block.sync
        def _(sp):
            sp.dma_start(g["out"].rearrange("b (j p) d -> p (b j) d", p=P), g["X"][:]).then_inc(stored, 16)
            sp.wait_ge(stored, 16)


def build(nc, g):
    with ExitStack() as ctx:
        constants(nc, ctx, g)
        for phase in [layer0_attention, experts0, layer1_attention, layer1_cross, experts1]:
            phase(nc, ctx, g)
        store(nc, ctx, g)


def rows_of(w, k):
    return np.ascontiguousarray(w.reshape(k, P, -1).transpose(1, 0, 2))


def spread(v):
    return np.ascontiguousarray(np.broadcast_to(v.reshape(1, -1), (P, v.size)))


def columns(v, k):
    return np.ascontiguousarray(v.reshape(k, P).T)


def kernel(**inputs):
    import concourse.bacc as bacc
    from concourse.bass_utils import run_bass_kernel_spmd as run

    a = {k: np.asarray(v) for k, v in inputs.items()}
    x, c = a["x"], a["ctx_1024"]
    s2 = c.shape[1]
    xT = np.zeros((B + 1, P, KD, S), x.dtype)
    xT[:B] = x.reshape(B, S, KD, P).transpose(0, 3, 2, 1)
    om = a["L0_attn_omega"].transpose(1, 2, 0, 3).reshape(2, 8, HD0, FD0)
    omega = np.zeros((8, HD0, 2, 8, FD0), om.dtype)
    for h in range(8):
        omega[h, :, :, h, :] = om[:, h].transpose(1, 0, 2)
    node = np.repeat(a["L0_attn_quad_nodes"], M0)
    weight = np.repeat(a["L0_attn_quad_weights"], M0)
    nodes = np.stack([np.concatenate([node, node]), np.concatenate([weight, weight])], 1)
    W = a["L0_xattn_W"]
    ins = {
        "x": x.reshape(B, J, P, D).transpose(2, 0, 1, 3).reshape(P, T, D),
        "xT": xT,
        "ctxT": c.reshape(B, s2, KD, P).transpose(0, 3, 2, 1),
        "L0_attn_Wqkv": rows_of(a["L0_attn_Wqkv"], KD),
        "L0_attn_bqkv": spread(a["L0_attn_bqkv"]),
        "L0_attn_omega": omega.reshape(P, 2, 8 * FD0),
        "L0_attn_nodes": nodes,
        "L0_attn_bout": spread(a["L0_attn_bout"]),
        "L0_attn_Wout": rows_of(a["L0_attn_Wout"], KD),
        "L0_xattn_W1": rows_of(W[:, :D].T, KD),
        "L0_xattn_W2": rows_of(W[:, D:].T, KD),
        "L0_xattn_b": spread(a["L0_xattn_b"]),
        "L0_ffn_Wr": rows_of(a["L0_ffn_Wr"], KD),
        "L0_ffn_br": spread(a["L0_ffn_br"]),
    }
    ins.update(more_inputs(a))
    nc = bacc.Bacc("TRN2", target_bir_lowering=False, num_devices=1)
    g = {"S2": s2}
    arrays = {}
    for name, v in ins.items():
        v = arrays["in_" + name] = np.ascontiguousarray(v)
        g[name] = nc.dram_tensor("in_" + name, v.shape, mybir.dt.from_np(v.dtype), kind="ExternalInput").ap()
    g["out"] = nc.dram_tensor("out", x.shape, F32, kind="ExternalOutput").ap()
    build(nc, g)
    r = run(nc, [arrays], core_ids=[0])
    return r.results[0]["out"]
```

```python
from contextlib import ExitStack

import numpy as np

import concourse.bass as bass
from concourse import mybir

F32 = mybir.dt.float32
F32R = mybir.dt.float32r
I32 = mybir.dt.int32
U32 = mybir.dt.uint32
U8 = mybir.dt.uint8
ALU = mybir.AluOpType
ACT = mybir.ActivationFunctionType
AX_X = mybir.AxisListType.X

P = 128
B, S, D = 4, 512, 256
KD = D // P
J = S // P
T = B * J
LN_EPS = 1e-5

H0, HD0, R0, M0 = 16, 16, 2, 32
FD0 = R0 * M0
PAIRS0 = H0 * FD0 // P
VW0 = HD0 + 1

E, F = 8, 1024
KF = F // P


def each(eng, go, pace, it):
    eng.wait_ge(go, it)
    eng.sem_inc(pace, 1)


def ends(eng, ended):
    eng.drain().then_inc(ended, 1)


def turn(sp, ended, go, pace, it, sems):
    sp.wait_ge(ended, it * 4)
    sp.sem_inc(pace, 1)
    sp.sem_clear(range(sems[0].num, sems[-1].num + 1))
    sp.sem_inc(go, 1)


def layer0_attention(nc, sc, g):
    ctx = ExitStack()
    with ctx:
        def sb(name, shape, dt=F32):
            return ctx.enter_context(nc.sbuf_tensor(name, shape, dt))

        loop_sems = []

        def sem(name, kept=False):
            s = ctx.enter_context(nc.semaphore(name))
            if not kept:
                loop_sems.append(s)
            return s

        PS = g["PS"]
        ident, X, LG = g["ident"], g["X"], g["LG"]

        wqkv = sb("wqkv", [P, KD, 3 * D])
        wout = sb("wout0", [P, KD, D])
        w1t = sb("w1t", [P, KD, D])
        w2t = sb("w2t", [P, KD, D])
        wr = sb("wr", [P, KD, E])
        omega = sb("omega", [P, KD, KD * 2 * P])
        bqkv = sb("bqkv", [P, 3 * D])
        bout = sb("bout0", [P, D])
        bx = sb("bx", [P, D])
        brt = sb("brt", [P, E])
        nodes = sb("nodes", [P, 2])
        fscale = sb("fscale", [P, 4])
        causal = sb("causal", [P, P])
        xT = sb("xT", [P, KD, S])
        ctxT = sb("ctxT", [P, KD, g["S2"]])
        xres = sb("xres", [P, J, D])
        qk = sb("qk", [P, J, 2 * D])
        v1 = sb("v1", [P, J, H0, VW0])
        sq = sb("sq", [P, 2, 2 * D])
        ss = sb("ss", [P, J, 2 * H0])
        rn = sb("rn", [P, J, 2 * H0])
        qkT = sb("qkT", [P, 4, S])
        fe = sb("fe", [P, 4, S])
        kfT = sb("kfT", [P, PAIRS0, S])
        qbd = sb("qbd", [P, PAIRS0, J, 2 * P])
        kfR = sb("kfR", [P, J - 1, PAIRS0, P])
        scm = sb("scm", [P, 2, 4, P])
        state = sb("state", [P, PAIRS0, 2 * VW0])
        den = sb("den", [P, H0])
        rden = sb("rden", [P, H0])
        osb = sb("osb", [P, D])
        oT = sb("oT", [P, KD, P])
        r1 = sb("r1", [P, D])
        r2 = sb("r2", [P, D])
        bn = sb("bn", [P, 2, 6])
        mv = sb("mv", [P, 2, 2])
        ve = sb("ve", [P, 2])
        rs = sb("rs", [P, 2])
        x1 = sb("x1", [P, J, D])
        x1T = sb("x1T", [P, KD, P])
        x1pb = sb("x1pb", [P, D])
        x2 = sb("x2", [P, J, D])
        x2T = sb("x2T", [P, KD, P])
        lgs = sb("lgs", [P, J, E])
        csum = sb("csum", [P, KD])
        cbc = sb("cbc", [P, KD, P])
        pb = sb("pb", [P, D])

        w_loaded = sem("a_w_loaded", True)
        wqkv_loaded = sem("a_wqkv_loaded", True)
        xT_loaded = sem("a_xT_loaded", True)
        x_loaded = g["x_loaded"]
        consts = sem("a_consts", True)
        ended = sem("a_ended", True)
        go = sem("a_go", True)
        pace = sem("a_pace", True)
        chain = sem("a_chain")
        pchain = sem("a_pchain")
        ctx_loaded = sem("a_ctx_loaded")
        qkv_done = sem("a_qkv_done")
        qk_ready = sem("a_qk_ready")
        v_ready = sem("a_v_ready")
        sq_ready = sem("a_sq_ready")
        ss_ready = sem("a_ss_ready")
        qkn_ready = sem("a_qkn_ready")
        qkT_done = sem("a_qkT_done")
        qkT_ready = sem("a_qkT_ready")
        feat_done = sem("a_feat_done")
        feat_exp = sem("a_feat_exp")
        k_ready = sem("a_k_ready")
        q_clipped = sem("a_q_clipped")
        q_ready = sem("a_q_ready")
        kfR_done = sem("a_kfR_done")
        kfR_ready = sem("a_kfR_ready")
        scores_done = sem("a_scores_done")
        masked = sem("a_masked")
        av_done = sem("a_av_done")
        state_done = sem("a_state_done")
        state_ready = sem("a_state_ready")
        o_ready = sem("a_o_ready")
        oT_done = sem("a_oT_done")
        oT_ready = sem("a_oT_ready")
        proj_done = sem("a_proj_done")
        xres_ready = sem("a_xres_ready")
        r1_ready = sem("a_r1_ready")
        mv1_ready = sem("a_mv1_ready")
        rs1_ready = sem("a_rs1_ready")
        x1_ready = sem("a_x1_ready")
        x1T_done = sem("a_x1T_done")
        x1T_ready = sem("a_x1T_ready")
        x1pb_ready = sem("a_x1pb_ready")
        rn_ready = sem("a_rn_ready")
        part_done = sem("a_part_done")
        r2_ready = sem("a_r2_ready")
        mv2_ready = sem("a_mv2_ready")
        rs2_ready = sem("a_rs2_ready")
        x2_ready = sem("a_x2_ready")
        x2T_done = sem("a_x2T_done")
        x2T_ready = sem("a_x2T_ready")
        lg_done = sem("a_lg_done")
        lg_ready = sem("a_lg_ready")
        cbc_ready = sem("a_cbc_ready")
        part2_done = sem("a_part2_done")
        pb_ready = sem("a_pb_ready")

        block = ctx.enter_context(nc.Block())

        @block.sync
        def _(sp):
            sp.dma_start(wqkv[:], g["L0_attn_Wqkv"]).then_inc(wqkv_loaded, 16)
            sp.dma_start(xT[:], g["xT"][0]).then_inc(xT_loaded, 16)
            sp.dma_start(bqkv[:], g["L0_attn_bqkv"]).then_inc(wqkv_loaded, 16)
            for dst, src in ((omega, g["L0_attn_omega"]),
                             (nodes, g["L0_attn_nodes"]), (bout, g["L0_attn_bout"]), (wout, g["L0_attn_Wout"]),
                             (w1t, g["L0_xattn_W1"]), (w2t, g["L0_xattn_W2"]), (bx, g["L0_xattn_b"]),
                             (wr, g["L0_ffn_Wr"]), (brt, g["L0_ffn_br"])):
                sp.dma_start(dst[:], src).then_inc(w_loaded, 16)
            sp.dma_start(X[:], g["x"]).then_inc(x_loaded, 16)
            sp.sem_inc(go, 1)
            with sp.Fori(1, B + 1) as it:
                each(sp, go, pace, it)
                sp.dma_start(ctxT[:], g["ctxT"][bass.ds(it - 1, 1)].rearrange("o p k s -> p (o k) s"))\
                    .then_inc(ctx_loaded, 16)
                sp.wait_ge(qkv_done, J)
                sp.dma_start(xT[:], g["xT"][bass.ds(it, 1)].rearrange("o p k s -> p (o k) s"))\
                    .then_inc(xT_loaded, 16)
                turn(sp, ended, go, pace, it, loop_sems)
            g["clear"](sp, 0)
            sp.wait_ge(xT_loaded, 16 * (B + 1))

        @block.gpsimd
        def _(pool):
            n = [0]

            def link(ins):
                n[0] += 1
                ins.then_inc(pchain, 1)
                pool.wait_ge(pchain, n[0])

            nc.gpsimd.memset(causal[:], 1.0).then_inc(consts, 1)
            pool.wait_ge(consts, 1)
            nc.gpsimd.affine_select(out=causal[:], in_=causal[:], compare_op=ALU.is_ge, fill=0.0, base=0,
                                    pattern=[[1, P]], channel_multiplier=-1).then_inc(consts, 1)
            nc.gpsimd.memset(qbd[:], 0.0).then_inc(consts, 1)
            nc.gpsimd.memset(v1[:], 1.0).then_inc(consts, 1)
            pool.wait_ge(w_loaded, 16 * 9)
            nc.gpsimd.tensor_scalar(fscale[:, 3:4], nodes[:, 0:1], 0.0, 2.0, ALU.max, ALU.mult).then_inc(consts, 1)
            nc.gpsimd.tensor_scalar(fscale[:, 1:2], nodes[:, 0:1], -1.0, None, ALU.mult).then_inc(consts, 1)
            nc.gpsimd.tensor_scalar(fscale[:, 2:3], nodes[:, 1:2], 0.0, 1.0 / M0, ALU.max, ALU.mult).then_inc(consts, 1)
            pool.wait_ge(consts, 7)
            nc.gpsimd.tensor_tensor(fscale[:, 0:1], fscale[:, 3:4], g["half"][:], ALU.pow).then_inc(consts, 1)
            pool.wait_ge(x_loaded, 16)
            with pool.Fori(1, B + 1) as it:
                each(pool, go, pace, it)
                n[0] = 0
                nc.gpsimd.tensor_tensor(xres[:], X[:, bass.ds(it * J - J, J), :],
                                        bout[:, None, :].to_broadcast([P, J, D]), ALU.add).then_inc(xres_ready, 1)

                for s in range(J + 1):
                    if s < J:
                        pool.wait_ge(mv1_ready, s + 1)
                        link(nc.gpsimd.tensor_scalar(ve[:, 0:1], mv[:, 0, 1:2], LN_EPS, None, ALU.add))
                        nc.gpsimd.tensor_tensor(rs[:, 0:1], ve[:, 0:1], g["mhalf"][:], ALU.pow).then_inc(rs1_ready, 1)
                    if s >= 1:
                        pool.wait_ge(mv2_ready, s)
                        link(nc.gpsimd.tensor_scalar(ve[:, 1:2], mv[:, 1, 1:2], LN_EPS, None, ALU.add))
                        nc.gpsimd.tensor_tensor(rs[:, 1:2], ve[:, 1:2], g["mhalf"][:], ALU.pow).then_inc(rs2_ready, 1)
                ends(pool, ended)

        @block.scalar
        def _(act):
            act.wait_ge(consts, 8)
            with act.Fori(1, B + 1) as it:
                each(act, go, pace, it)
                for j in range(J + 2):
                    if j < J:
                        act.wait_ge(qk_ready, j + 1)
                        if j >= 2:
                            act.wait_ge(ss_ready, j - 1)
                        nc.scalar.activation(sq[:, j % 2, :], qk[:, j, :], ACT.Square).then_inc(sq_ready, 1)
                    if 1 <= j < J + 1:
                        act.wait_ge(ss_ready, j)
                        nc.scalar.activation(rn[:, j - 1, :], ss[:, j - 1, :], ACT.Sqrt).then_inc(rn_ready, 1)
                    if j >= 2:
                        at = j - 2
                        act.wait_ge(qkT_done, at + 1)
                        nc.scalar.copy(qkT[:, :, at * P:(at + 1) * P],
                                       PS[:, 4 + at % 2, :].rearrange("p (c n) -> p c n", c=4)).then_inc(qkT_ready, 1)

                for f in range(2 * PAIRS0):
                    p = f // 2
                    act.wait_ge(feat_done, f + 1)
                    if p >= 2:
                        act.wait_ge(q_ready if f % 2 else k_ready, p - 1)
                    nc.scalar.activation(fe[:, f % 4, :], PS[:, f % 4, :], ACT.Exp, bias=fscale[:, 1:2],
                                         scale=fscale[:, 0:1]).then_inc(feat_exp, 1)
                for p in range(PAIRS0):
                    act.wait_ge(kfR_done, p + 1)
                    nc.scalar.copy(kfR[:, :, p, :],
                                   PS[:, 4 + p % 2, 0:(J - 1) * P].rearrange("p (j n) -> p j n", n=P))\
                        .then_inc(kfR_ready, 1)

                def turned(dst, bank, done, used, ready, s):
                    act.wait_ge(done, s + 1)
                    if s >= 1:
                        act.wait_ge(used, s)
                    nc.scalar.copy(dst[:], PS[:, bank, 0:D].rearrange("p (k n) -> p k n", k=KD)).then_inc(ready, 1)

                for s in range(J + 2):
                    if 0 <= s - 1 < J:
                        turned(oT, 4, oT_done, proj_done, oT_ready, s - 1)
                    if 0 <= s - 2 < J:
                        turned(x2T, 2, x2T_done, lg_done, x2T_ready, s - 2)
                    if 0 <= s - 1 < J:
                        turned(x1T, 5, x1T_done, part_done, x1T_ready, s - 1)
                act.wait_ge(x2_ready, J)
                nc.scalar.copy(X[:, bass.ds(it * J - J, J), :], x2[:])
                act.wait_ge(lg_ready, J)
                nc.scalar.copy(LG[:, bass.ds(it * J - J, J), :], lgs[:])
                ends(act, ended)

        @block.vector
        def _(dve):
            n = [0]

            def link(ins):
                n[0] += 1
                ins.then_inc(chain, 1)
                dve.wait_ge(chain, n[0])

            dve.wait_ge(wqkv_loaded, 32)
            dve.wait_ge(consts, 8)
            with dve.Fori(1, B + 1) as it:
                each(dve, go, pace, it)
                n[0] = 0
                def add_bias(j):
                    dve.wait_ge(qkv_done, j + 1)
                    u = PS[:, 2 * (j % 2):2 * (j % 2) + 2, :].rearrange("p b n -> p (b n)")
                    nc.vector.tensor_tensor(qk[:, j, :], u[:, 0:2 * D], bqkv[:, 0:2 * D], ALU.add).then_inc(qk_ready, 1)
                    nc.vector.tensor_tensor(v1[:, j, :, 0:HD0],
                                            u[:, 2 * D:3 * D].rearrange("p (h d) -> p h d", d=HD0),
                                            bqkv[:, 2 * D:3 * D].rearrange("p (h d) -> p h d", d=HD0),
                                            ALU.add).then_inc(v_ready, 1)

                def square_sums(j):
                    dve.wait_ge(sq_ready, j + 1)
                    nc.vector.reduce_sum(ss[:, j, :], sq[:, j % 2, :].rearrange("p (h d) -> p h d", d=HD0), AX_X)\
                        .then_inc(ss_ready, 1)

                def normalise(j):
                    dve.wait_ge(rn_ready, j + 1)
                    link(nc.vector.tensor_scalar(rn[:, j, :], rn[:, j, :], 1e-12, None, ALU.max))
                    link(nc.vector.reciprocal(rn[:, j, :], rn[:, j, :]))
                    v = qk[:, j, :].rearrange("p (h d) -> p h d", d=HD0)
                    nc.vector.tensor_tensor(v, v, rn[:, j, :, None].to_broadcast([P, 2 * H0, HD0]), ALU.mult)\
                        .then_inc(qkn_ready, 1)

                for j in range(J + 2):
                    if j < J:
                        add_bias(j)
                    if 1 <= j < J + 1:
                        square_sums(j - 1)
                    if j >= 2:
                        normalise(j - 2)
                dve.wait_ge(ctx_loaded, 16)
                link(nc.vector.reduce_sum(csum[:], ctxT[:], AX_X))
                for k in range(KD):
                    ins = nc.vector.tensor_scalar(cbc[:, k, :], g["ones"][:], csum[:, k:k + 1], 1.0 / g["S2"],
                                                  ALU.mult, ALU.mult)
                ins.then_inc(cbc_ready, 1)

                dve.wait_ge(part2_done, 1)
                nc.vector.tensor_tensor(pb[:], PS[:, 7, 0:D], bx[:], ALU.add).then_inc(pb_ready, 1)
                low, high = float(np.exp(-20.0)), float(np.exp(20.0))
                for f in range(2 * PAIRS0):
                    dve.wait_ge(feat_exp, f + 1)
                    dst, ready = (fe[:, f % 4, :], q_clipped) if f % 2 else (kfT[:, f // 2, :], k_ready)
                    nc.vector.tensor_scalar(dst, fe[:, f % 4, :], high, low, ALU.min, ALU.max).then_inc(ready, 1)
                    if f % 2:
                        p = f // 2
                        dve.wait_ge(q_clipped, p + 1)
                        for half in range(2):
                            at = slice(64 * half, 64 * half + 64)
                            ins = nc.vector.tensor_scalar(
                                qbd[at, p, :, P * half:P * half + P],
                                fe[at, f % 4, :].rearrange("p (j n) -> p j n", j=J), fscale[at, 2:3], None, ALU.mult)
                        ins.then_inc(q_ready, 1)

                def mask(s, q):
                    dve.wait_ge(scores_done, 4 * s + q + 1)
                    if 4 * s + q >= 2:
                        dve.wait_ge(av_done, 4 * s + q - 1)
                    nc.vector.tensor_tensor(scm[:, q % 2, :, :], PS[:, q % 2, :].rearrange("p (h n) -> p h n", n=P),
                                            causal[:, None, :].to_broadcast([P, 4, P]), ALU.mult).then_inc(masked, 1)

                def add_state(s):
                    dve.wait_ge(state_done, s + 1)
                    dve.wait_ge(av_done, 4 * s + 4)
                    new = PS[:, 7, 0:PAIRS0 * 2 * VW0].rearrange("p (a w) -> p a w", a=PAIRS0)
                    if s == 0:
                        ins = nc.vector.tensor_copy(state[:], new)
                    else:
                        dve.wait_ge(state_ready, s)
                        ins = nc.vector.tensor_tensor(state[:], new, state[:], ALU.add)
                    ins.then_inc(state_ready, 1)

                def divide(s):
                    dve.wait_ge(av_done, 4 * s + 4)
                    if s >= 1:
                        dve.wait_ge(oT_done, s)
                    o = PS[:, 6, 0:H0 * VW0].rearrange("p (h w) -> p h w", w=VW0)
                    link(nc.vector.tensor_scalar(den[:, :, None], o[:, :, HD0:VW0], 1e-6, None, ALU.max))
                    link(nc.vector.reciprocal(rden[:], den[:]))
                    nc.vector.tensor_tensor(osb[:].rearrange("p (h d) -> p h d", d=HD0), o[:, :, 0:HD0],
                                            rden[:, :, None].to_broadcast([P, H0, HD0]), ALU.mult).then_inc(o_ready, 1)

                def residual(s, i, done, add, r, ready, mv_ready):
                    dve.wait_ge(done, s + 1)
                    if i == 1:
                        dve.wait_ge(x1pb_ready, s + 1)
                    nc.vector.tensor_tensor(r[:], PS[:, 3, D * i:D * i + D], add, ALU.add).then_inc(ready, 1)
                    dve.wait_ge(ready, s + 1)
                    link(nc.vector.bn_stats(bn[:, i, :], r[:]))
                    nc.vector.bn_aggr(mv[:, i, :], bn[:, i, :]).then_inc(mv_ready, 1)

                def norm(s, i, rs_ready, r, dst, ready):
                    dve.wait_ge(rs_ready, s + 1)
                    nc.vector.tensor_scalar(dst, r[:], mv[:, i, 0:1], rs[:, i:i + 1], ALU.subtract, ALU.mult)\
                        .then_inc(ready, 1)

                for s in range(J + 2):
                    if s < J:
                        mask(s, 0)
                        mask(s, 1)
                    if 0 <= s - 2 < J:
                        residual(s - 2, 1, part_done, x1pb[:], r2, r2_ready, mv2_ready)
                    if s < J:
                        mask(s, 2)
                    if 0 <= s - 1 < J:
                        if s == 1:
                            dve.wait_ge(xres_ready, 1)
                        residual(s - 1, 0, proj_done, xres[:, s - 1, :], r1, r1_ready, mv1_ready)
                    if 0 <= s - 2 < J:
                        norm(s - 2, 1, rs2_ready, r2, x2[:, s - 2, :], x2_ready)
                    if s < J:
                        mask(s, 3)
                    if 0 <= s - 1 < J:
                        norm(s - 1, 0, rs1_ready, r1, x1[:, s - 1, :], x1_ready)
                        dve.wait_ge(x1_ready, s)
                        nc.vector.tensor_tensor(x1pb[:], x1[:, s - 1, :], pb[:], ALU.add).then_inc(x1pb_ready, 1)
                    if s < J - 1:
                        add_state(s)
                    if s < J:
                        divide(s)
                    if 0 <= s - 2 < J:
                        dve.wait_ge(lg_done, s - 1)
                        nc.vector.tensor_tensor(lgs[:, s - 2, :], PS[:, 2, D:D + E], brt[:], ALU.add)\
                            .then_inc(lg_ready, 1)
                ends(dve, ended)

        @block.tensor
        def _(pe):
            pe.wait_ge(wqkv_loaded, 32)
            pe.wait_ge(g["consts"], g["n_consts"])
            with pe.Fori(1, B + 1) as it:
                each(pe, go, pace, it)
                pe.wait_ge(xT_loaded, 16 * it)
                pe.sem_inc(pace, 1)

                def qkv(j):
                    if j >= 2:
                        pe.wait_ge(v_ready, j - 1)
                    for half, cols in ((0, 2 * D), (1, D)):
                        for k in range(KD):
                            mm = nc.tensor.matmul(PS[:, 2 * (j % 2) + half, 0:cols], xT[:, k, j * P:(j + 1) * P],
                                                  wqkv[:, k, half * 2 * D:half * 2 * D + cols],
                                                  start=(k == 0), stop=(k == KD - 1))
                    mm.then_inc(qkv_done, 1)

                def turn_qk(j):
                    pe.wait_ge(qkn_ready, j + 1)
                    if j >= 2:
                        pe.wait_ge(qkT_ready, j - 1)
                    for c in range(4):
                        mm = nc.tensor.transpose(PS[:, 4 + j % 2, c * P:(c + 1) * P], qk[:, j, c * P:(c + 1) * P],
                                                 ident[:])
                    mm.then_inc(qkT_done, 1)

                for j in range(J + 2):
                    if j < J:
                        qkv(j)
                    if j >= 2:
                        turn_qk(j - 2)
                pe.wait_ge(w_loaded, 16 * 9)
                pe.wait_ge(cbc_ready, 1)
                for k in range(KD):
                    mm = nc.tensor.matmul(PS[:, 7, 0:D], cbc[:, k, :], w2t[:, k, :], start=(k == 0), stop=(k == KD - 1))
                mm.then_inc(part2_done, 1)
                pe.wait_ge(v_ready, J)
                pe.wait_ge(qkT_ready, J)
                for f in range(2 * PAIRS0):
                    p, q_side = f // 2, f % 2
                    if f >= 4:
                        pe.wait_ge(feat_exp, f - 3)
                    half = p // 4
                    nc.tensor.matmul(PS[:, f % 4, :], omega[:, half, (p % 4) * P:(p % 4 + 1) * P],
                                     qkT[:, half if q_side else 2 + half, :], start=True, stop=True).then_inc(feat_done, 1)
                for p in range(PAIRS0):
                    pe.wait_ge(k_ready, p + 1)
                    if p >= 2:
                        pe.wait_ge(kfR_ready, p - 1)
                    for j in range(J - 1):
                        mm = nc.tensor.transpose(PS[:, 4 + p % 2, j * P:(j + 1) * P], kfT[:, p, j * P:(j + 1) * P], ident[:])
                    mm.then_inc(kfR_done, 1)
                pe.wait_ge(feat_exp, 2 * PAIRS0)
                pe.wait_ge(pb_ready, 1)

                def scores(s, q):
                    if 4 * s + q >= 2:
                        pe.wait_ge(masked, 4 * s + q - 1)
                    if s == 0:
                        pe.wait_ge(q_ready, 2 * q + 2)
                    for i in range(2):
                        p = 2 * q + i
                        mm = nc.tensor.matmul(PS[:, q % 2, i * 2 * P:(i + 1) * 2 * P], kfT[:, p, s * P:(s + 1) * P],
                                              qbd[:, p, s, :], start=True, stop=True)
                    mm.then_inc(scores_done, 1)

                def weigh(s, q):
                    pe.wait_ge(masked, 4 * s + q + 1)
                    if s >= 1 and q == 0:
                        pe.wait_ge(o_ready, s)
                        pe.wait_ge(state_ready, s)
                    for i in range(4):
                        h = 4 * q + i
                        out = PS[:, 6, h * VW0:(h + 1) * VW0]
                        mm = nc.tensor.matmul(out, scm[:, q % 2, i, :], v1[:, s, h, :], start=True, stop=(s == 0))
                        if s >= 1:
                            mm = nc.tensor.matmul(out, qbd[:, h // 2, s, (h % 2) * P:(h % 2 + 1) * P],
                                                  state[:, h // 2, (h % 2) * VW0:(h % 2 + 1) * VW0],
                                                  start=False, stop=True)
                    mm.then_inc(av_done, 1)

                def new_state(s):
                    if s == 0:
                        pe.wait_ge(kfR_ready, PAIRS0)
                    else:
                        pe.wait_ge(state_ready, s)
                    for p in range(PAIRS0):
                        mm = nc.tensor.matmul(PS[:, 7, p * 2 * VW0:(p + 1) * 2 * VW0], kfR[:, s, p, :],
                                              v1[:, s, 2 * p:2 * p + 2, :].rearrange("p h w -> p (h w)"),
                                              start=True, stop=True)
                    mm.then_inc(state_done, 1)

                def turn_rows(s, src, bank, ready, used, done):
                    pe.wait_ge(ready, s + 1)
                    if used is not None and s >= 1:
                        pe.wait_ge(used, s)
                    if s == 0:
                        pe.wait_ge(kfR_ready, PAIRS0)
                    for k in range(KD):
                        mm = nc.tensor.transpose(PS[:, bank, k * P:(k + 1) * P], src[:, k * P:(k + 1) * P], ident[:])
                    mm.then_inc(done, 1)

                def project(s, at, lhs, ready, w, done):
                    pe.wait_ge(ready, s + 1)
                    for k in range(KD):
                        mm = nc.tensor.matmul(PS[:, 3, at:at + D], lhs[:, k, :], w[:, k, :],
                                              start=(k == 0), stop=(k == KD - 1))
                    mm.then_inc(done, 1)

                for s in range(J + 2):
                    main, first, second = s < J, 0 <= s - 1 < J, 0 <= s - 2 < J
                    if main:
                        scores(s, 0)
                        scores(s, 1)
                    if second:
                        pe.wait_ge(r1_ready, s - 1)
                        project(s - 2, D, x1T, x1T_ready, w1t, part_done)
                    if first:
                        turn_rows(s - 1, osb, 4, o_ready, oT_ready, oT_done)
                    if main:
                        weigh(s, 0)
                        scores(s, 2)
                    if first:
                        if s >= 2:
                            pe.wait_ge(r2_ready, s - 1)
                        project(s - 1, 0, oT, oT_ready, wout, proj_done)
                    if main:
                        weigh(s, 1)
                        scores(s, 3)
                    if second:
                        if s >= 3:
                            pe.wait_ge(lg_ready, s - 2)
                        turn_rows(s - 2, x2[:, s - 2, :], 2, x2_ready, x2T_ready, x2T_done)
                    if main:
                        weigh(s, 2)
                    if first:
                        turn_rows(s - 1, x1[:, s - 1, :], 5, x1_ready, x1T_ready, x1T_done)
                    if main:
                        weigh(s, 3)
                    if s < J - 1:
                        new_state(s)
                    if second:
                        pe.wait_ge(x2T_ready, s - 1)
                        for k in range(KD):
                            mm = nc.tensor.matmul(PS[:, 2, D:D + E], x2T[:, k, :], wr[:, k, :],
                                                  start=(k == 0), stop=(k == KD - 1))
                        mm.then_inc(lg_done, 1)
                ends(pe, ended)


def tiles_of(choices):
    return choices * T + E - 1


def experts(nc, top, g, layer):
    C = layer + 1
    TC = T * C
    NT = tiles_of(C)
    xs, ys = g["xs%d" % layer], g["ys%d" % layer]
    PS, X, LG, ident, ones = g["PS"], g["X"], g["LG"], g["ident"], g["ones"]
    ctx = ExitStack()
    with ctx:
        def sb(name, shape, dt=F32):
            return ctx.enter_context(nc.sbuf_tensor("f%d_%s" % (layer, name), shape, dt))

        def sem(name):
            return ctx.enter_context(nc.semaphore("f%d_%s" % (layer, name)))

        w1 = sb("w1", [P, E * KD * F])
        w2 = sb("w2", [P, E * KF * D])
        b1 = sb("b1", [P, E * KF])
        b2 = sb("b2", [P, E * D])
        slot = sb("slot", [P, TC], I32)
        tile_expert = sb("tile_expert", [P, NT + 2], I32)
        gates = sb("gates", [P, T, C])
        w_loaded, b_loaded = sem("w_loaded"), sem("b_loaded")

        def load_expert(eng, e):
            if e >= 1:
                eng.wait_ge(w_loaded, 32 * e)
            eng.dma_start(w1[:, e * KD * F:(e + 1) * KD * F], g["L%d_ffn_w1" % layer][e]).then_inc(w_loaded, 16)
            eng.dma_start(w2[:, e * KF * D:(e + 1) * KF * D], g["L%d_ffn_w2" % layer][e]).then_inc(w_loaded, 16)

        dispatch(nc, g, layer, slot, tile_expert, gates, load_expert, b1, b2, b_loaded)
        multiply(nc, g, layer, w1, w2, b1, b2, tile_expert, load_expert, w_loaded, b_loaded)
        collect(nc, g, layer, slot, gates)


EARLY = 1


def dispatch(nc, g, layer, slot, tile_expert, gates, load_expert, b1, b2, b_loaded):
    C = layer + 1
    TC = T * C
    NT = tiles_of(C)
    xs = g["xs%d" % layer]
    PS, X, LG, ones = g["PS"], g["X"], g["LG"], g["ones"]
    ctx = ExitStack()
    with ctx:
        def sb(name, shape, dt=F32):
            return ctx.enter_context(nc.sbuf_tensor("d%d_%s" % (layer, name), shape, dt))

        def sem(name):
            return ctx.enter_context(nc.semaphore("d%d_%s" % (layer, name)))

        before = sb("before", [P, P])
        iota = sb("iota", [P, NT + 2], I32)
        iotaf = sb("iotaf", [P, NT + 2])
        less = sb("less", [P, E])
        again = sb("again", [P, E, TC])
        lg2 = sb("lg2", [P, T, E])
        top = sb("top", [P, C, T])
        eq = sb("eq", [P, T, E])
        cand = sb("cand", [P, T, E])
        low = sb("low", [P, T])
        oh = sb("oh", [P, T, C, E])
        ex = sb("ex", [P, T, E])
        gd = sb("gd", [P, T])
        tot = sb("tot", [P, E, TC])
        cum = sb("cum", [P, E, TC])
        more = sb("more", [P, E, T])
        ntile = sb("ntile", [P, E])
        tend = sb("tend", [P, E])
        row0 = sb("row0", [P, E])
        base = sb("base", [P, E, TC])
        at = sb("at", [P, TC, E])
        slotf = sb("slotf", [P, TC])
        past = sb("past", [P, NT + 2, E])
        tef = sb("tef", [P, NT + 2])

        consts, chain, bchain = sem("consts"), sem("chain"), sem("bchain")
        oh_ready, counted, slot_ready = sem("oh_ready"), sem("counted"), sem("slot_ready")
        ex_in, ex_done, scattered = sem("ex_in"), sem("ex_done"), sem("scattered")
        stats_ready, rs_ready, xn_done, xn_ready = sem("stats_ready"), sem("rs_ready"), sem("xn_done"), sem("xn_ready")
        if layer == 0:
            xn = sb("xn", [P, T, D])
            lng = sb("lng", [P, D])
            lnb = sb("lnb", [P, D])
            bn = sb("bn", [P, T, 6])
            mv = sb("mv", [P, T, 2])
            rs = sb("rs", [P, T])
            ln_loaded = sem("ln_loaded")
        rows = xn if layer == 0 else X
        block = ctx.enter_context(nc.Block())

        @block.sync
        def _(sp):
            if layer == 0:
                sp.dma_start(lng[:], g["L0_ffn_ln_g"]).then_inc(ln_loaded, 16)
                sp.dma_start(lnb[:], g["L0_ffn_ln_b"]).then_inc(ln_loaded, 16)
            sp.dma_start(b1[:], g["L%d_ffn_b1" % layer]).then_inc(b_loaded, 16)
            sp.dma_start(b2[:], g["L%d_ffn_b2" % layer]).then_inc(b_loaded, 16)

        @block.gpsimd
        def _(pool):
            for e in range(EARLY):
                load_expert(pool, e)
            nc.gpsimd.memset(before[:], 1.0).then_inc(consts, 1)
            pool.wait_ge(consts, 1)
            nc.gpsimd.affine_select(out=before[:], in_=before[:], compare_op=ALU.is_gt, fill=0.0, base=0,
                                    pattern=[[1, P]], channel_multiplier=-1).then_inc(consts, 1)
            nc.gpsimd.iota(iota[:], [[1, NT + 2]], base=0, channel_multiplier=0).then_inc(consts, 1)
            nc.gpsimd.memset(again[:], 1.0).then_inc(consts, 1)
            pool.wait_ge(consts, 4)
            nc.gpsimd.memset(again[:, :, 0:1], 0.0).then_inc(consts, 1)
            nc.gpsimd.tensor_copy(iotaf[:], iota[:]).then_inc(consts, 1)
            if layer == 0:
                pool.wait_ge(stats_ready, T)
                nc.gpsimd.tensor_scalar(rs[:], mv[:, :, 1], LN_EPS, None, ALU.add).then_inc(rs_ready, 1)
                pool.wait_ge(rs_ready, 1)
                nc.gpsimd.tensor_tensor(rs[:], rs[:], g["mhalf"][:].to_broadcast([P, T]), ALU.pow).then_inc(rs_ready, 1)
            pool.wait_ge(slot_ready, 1)
            pool.wait_ge(g["xs_cleared"], 16 * (layer + 1))
            for t in range(T):
                if layer == 0:
                    pool.wait_ge(xn_ready, t + 1)
                for c in range(C):
                    n = t * C + c
                    pool.indirect_dma_start(out=xs[:, :], out_offset=bass.IndirectOffsetOnAxis(ap=slot[:, n:n + 1].bitcast(U32), axis=0),
                                            in_=rows[:, t, :], in_offset=None).then_inc(scattered, 16)
            pool.wait_ge(scattered, 16 * TC)

        @block.scalar
        def _(act):
            act.wait_ge(ex_in, 1)
            if C == 1:
                nc.scalar.activation(ex[:], ex[:], ACT.Exp).then_inc(ex_done, 1)
            else:
                nc.scalar.activation(gd[:], gd[:], ACT.Exp).then_inc(ex_done, 1)

        @block.vector
        def _(dve):
            n = [0]

            def link(ins):
                n[0] += 1
                ins.then_inc(chain, 1)
                dve.wait_ge(chain, n[0])

            dve.wait_ge(consts, 6)
            link(nc.vector.tensor_scalar(less[:], iotaf[:, 0:E], -100.0, None, ALU.add))
            for c in range(C):
                src = LG if c == 0 else lg2
                link(nc.vector.reduce_max(top[:, c, :], src[:], AX_X))
                link(nc.vector.tensor_tensor(eq[:], src[:], top[:, c, :, None].to_broadcast([P, T, E]), ALU.is_equal))
                link(nc.vector.tensor_scalar(cand[:], eq[:], -100.0, None, ALU.mult))
                link(nc.vector.tensor_tensor(cand[:], cand[:], iotaf[:, None, 0:E].to_broadcast([P, T, E]), ALU.add))
                link(nc.vector.tensor_reduce(low[:], cand[:], AX_X, ALU.min))
                ins = nc.vector.tensor_tensor(oh[:, :, c, :], less[:, None, :].to_broadcast([P, T, E]),
                                              low[:, :, None].to_broadcast([P, T, E]), ALU.is_equal)
                if c < C - 1:
                    link(ins)
                    link(nc.vector.tensor_scalar(lg2[:], oh[:, :, c, :], -1e30, None, ALU.mult))
                    link(nc.vector.tensor_tensor(lg2[:], lg2[:], LG[:], ALU.add))
                else:
                    ins.then_inc(oh_ready, 1)
            if C == 1:
                nc.vector.tensor_tensor(ex[:], LG[:], top[:, 0, :, None].to_broadcast([P, T, E]),
                                        ALU.subtract).then_inc(ex_in, 1)
            else:
                nc.vector.tensor_tensor(gd[:], top[:, 1, :], top[:, 0, :], ALU.subtract).then_inc(ex_in, 1)
            if layer == 0:
                for t in range(T):
                    nc.vector.bn_stats(bn[:, t, :], X[:, t, :]).then_inc(bchain, 1)
                for t in range(T):
                    dve.wait_ge(bchain, t + 1)
                    nc.vector.bn_aggr(mv[:, t, :], bn[:, t, :]).then_inc(stats_ready, 1)
            dve.wait_ge(ex_done, 1)
            if C == 1:
                link(nc.vector.reduce_sum(gd[:], ex[:], AX_X))
                link(nc.vector.reciprocal(gates[:, :, 0], gd[:]))
            else:
                link(nc.vector.tensor_scalar(low[:], gd[:], 1.0, None, ALU.add))
                link(nc.vector.reciprocal(gates[:, :, 0], low[:]))
                link(nc.vector.tensor_tensor(gates[:, :, 1], gates[:, :, 0], gd[:], ALU.mult))
            dve.wait_ge(counted, 1)
            sums = PS[:, 1, 0:TC * E].rearrange("p (n e) -> p e n", e=E)
            link(nc.vector.tensor_copy(tot[:], sums))
            flat = lambda a: a[:].rearrange("p e n -> p (e n)")
            link(nc.vector.tensor_tensor_scan(flat(cum), flat(again), flat(tot), 0.0, ALU.mult, ALU.add))
            link(nc.vector.tensor_scalar(slotf[:, 0:T], iotaf[:, 0:T], float(P), None, ALU.mult))
            link(nc.vector.tensor_tensor(more[:], cum[:, :, TC - 1:TC].to_broadcast([P, E, T]),
                                         slotf[:, None, 0:T].to_broadcast([P, E, T]), ALU.is_gt))
            link(nc.vector.reduce_sum(ntile[:], more[:], AX_X))
            link(nc.vector.tensor_tensor_scan(tend[:], ones[:, 0:E], ntile[:], 0.0, ALU.mult, ALU.add))
            link(nc.vector.tensor_tensor(row0[:], tend[:], ntile[:], ALU.subtract))
            link(nc.vector.tensor_scalar(row0[:], row0[:], float(P), None, ALU.mult))
            link(nc.vector.tensor_tensor(base[:], cum[:], tot[:], ALU.subtract))
            link(nc.vector.tensor_tensor(base[:], base[:], row0[:, :, None].to_broadcast([P, E, TC]), ALU.add))
            link(nc.vector.tensor_tensor(at[:], PS[:, 0, 0:TC * E].rearrange("p (n e) -> p n e", e=E),
                                         base[:].rearrange("p e n -> p n e"), ALU.add))
            link(nc.vector.tensor_tensor(at[:], at[:], oh[:].rearrange("p t c e -> p (t c) e"), ALU.mult))
            link(nc.vector.reduce_sum(slotf[:], at[:], AX_X))
            nc.vector.tensor_copy(slot[:], slotf[:]).then_inc(slot_ready, 1)
            if layer == 0:
                dve.wait_ge(rs_ready, 2)
                dve.wait_ge(ln_loaded, 32)
                for t in range(T):
                    link(nc.vector.tensor_scalar(xn[:, t, :], X[:, t, :], mv[:, t, 0:1], rs[:, t:t + 1],
                                                 ALU.subtract, ALU.mult))
                    link(nc.vector.tensor_tensor(xn[:, t, :], xn[:, t, :], lng[:], ALU.mult))
                    nc.vector.tensor_tensor(xn[:, t, :], xn[:, t, :], lnb[:], ALU.add).then_inc(xn_ready, 1)
            link(nc.vector.tensor_tensor(past[:], iotaf[:, :, None].to_broadcast([P, NT + 2, E]),
                                         tend[:, None, :].to_broadcast([P, NT + 2, E]), ALU.is_ge))
            link(nc.vector.reduce_sum(tef[:], past[:], AX_X))
            link(nc.vector.tensor_scalar(tef[:], tef[:], float(E - 1), None, ALU.min))
            link(nc.vector.tensor_copy(tile_expert[:], tef[:]))

        @block.tensor
        def _(pe):
            pe.wait_ge(oh_ready, 1)
            pe.wait_ge(consts, 2)
            flat = oh[:].rearrange("p t c e -> p (t c e)")
            nc.tensor.matmul(PS[:, 0, 0:TC * E], before[:], flat, start=True, stop=True)
            nc.tensor.matmul(PS[:, 1, 0:TC * E], ones[:], flat, start=True, stop=True).then_inc(counted, 1)


def multiply(nc, g, layer, w1, w2, b1, b2, tile_expert, load_expert, w_loaded, b_loaded):
    C = layer + 1
    NT = tiles_of(C)
    xs, ys = g["xs%d" % layer], g["ys%d" % layer]
    PS, ident = g["PS"], g["ident"]
    XB, HB, TB, YB = 0, 1, 3, 5
    ctx = ExitStack()
    with ctx:
        def sb(name, shape, dt=F32):
            return ctx.enter_context(nc.sbuf_tensor("m%d_%s" % (layer, name), shape, dt))

        def sem(name):
            return ctx.enter_context(nc.semaphore("m%d_%s" % (layer, name)))

        xin = sb("xin", [P, D])
        xT = sb("xT", [P, KD, P])
        hrow = sb("hrow", [P, F])
        hT = sb("hT", [P, KF, P])
        y = sb("y", [P, D])
        xin_loaded, xT_done, xT_ready = sem("xin_loaded"), sem("xT_done"), sem("xT_ready")
        h_done, hrow_ready, hT_done, hT_ready = sem("h_done"), sem("hrow_ready"), sem("hT_done"), sem("hT_ready")
        y_done, y_ready, y_free = sem("y_done"), sem("y_ready"), sem("y_free")
        pace = sem("pace")
        block = ctx.enter_context(nc.Block())
        rows = lambda a, i: a[bass.ds(i * P, P), :]

        @block.sync
        def _(sp):
            sp.dma_start(xin[:], xs[0:P, :]).then_inc(xin_loaded, 16)
            sp.wait_ge(xT_done, 1)
            sp.dma_start(xin[:], xs[P:2 * P, :]).then_inc(xin_loaded, 16)
            sp.sem_inc(y_free, 16)
            with sp.Fori(1, NT + 1) as it:
                sp.wait_ge(xT_done, it + 1)
                sp.dma_start(xin[:], rows(xs, it + 1)).then_inc(xin_loaded, 16)
                sp.wait_ge(y_ready, it)
                sp.dma_start(rows(ys, it - 1), y[:]).then_inc(y_free, 16)
            sp.wait_ge(y_free, 16 * (NT + 1))
            sp.wait_ge(xin_loaded, 16 * (NT + 2))

        @block.gpsimd
        def _(pool):
            for e in range(EARLY, E):
                load_expert(pool, e)
            pool.wait_ge(w_loaded, 32 * E)

        @block.tensor
        def _(pe):
            def turn_tile():
                for k in range(KD):
                    mm = nc.tensor.transpose(PS[:, XB, k * P:(k + 1) * P], xin[:, k * P:(k + 1) * P], ident[:])
                mm.then_inc(xT_done, 1)

            def hidden(e):
                pe.wait_ge(w_loaded, e * 32 + 32)
                pe.sem_inc(pace, 1)
                for n in range(F // 512):
                    for k in range(KD):
                        mm = nc.tensor.matmul(PS[:, HB + n, :], xT[:, k, :],
                                              w1[:, bass.ds(e * (KD * F) + (k * F + n * 512), 512)],
                                              start=(k == 0), stop=(k == KD - 1))
                mm.then_inc(h_done, 1)

            pe.wait_ge(xin_loaded, 16)
            turn_tile()
            pe.wait_ge(xT_ready, 1)
            hidden(pe.value_load(tile_expert[0:1, 0:1], min_val=0, max_val=E - 1))
            pe.wait_ge(xin_loaded, 32)
            turn_tile()
            with pe.Fori(1, NT + 1) as it:
                e = pe.value_load(tile_expert[0:1, bass.ds(it - 1, 1)], min_val=0, max_val=E - 1)
                e1 = pe.value_load(tile_expert[0:1, bass.ds(it, 1)], min_val=0, max_val=E - 1)
                pe.wait_ge(hrow_ready, it)
                pe.sem_inc(pace, 1)
                for c in range(KF):
                    mm = nc.tensor.transpose(PS[:, TB + c // 4, (c % 4) * P:(c % 4 + 1) * P],
                                             hrow[:, c * P:(c + 1) * P], ident[:])
                mm.then_inc(hT_done, 1)
                pe.wait_ge(xT_ready, it + 1)
                pe.sem_inc(pace, 1)
                hidden(e1)
                pe.wait_ge(xin_loaded, it * 16 + 32)
                pe.sem_inc(pace, 1)
                turn_tile()
                pe.wait_ge(hT_ready, it)
                pe.sem_inc(pace, 1)
                for c in range(KF):
                    mm = nc.tensor.matmul(PS[:, YB, 0:D], hT[:, c, :], w2[:, bass.ds(e * (KF * D) + c * D, D)],
                                          start=(c == 0), stop=(c == KF - 1))
                mm.then_inc(y_done, 1)

        def activate(eng, it, e):
            eng.wait_ge(hT_done, it)
            eng.sem_inc(pace, 1)
            for c in range(KF):
                src = PS[:, TB + c // 4, (c % 4) * P:(c % 4 + 1) * P]
                bias = b1[:, bass.ds(e * KF + c, 1)]
                if layer == 0:
                    ins = nc.vector.tensor_scalar(hT[:, c, :], src, bias, 0.0, ALU.add, ALU.max)
                else:
                    ins = nc.scalar.activation(hT[:, c, :], src, ACT.Gelu, bias=bias)
            ins.then_inc(hT_ready, 1)

        @block.scalar
        def _(act):
            turned = PS[:, XB, 0:D].rearrange("p (k n) -> p k n", k=KD)
            hidden_rows = PS[:, HB:HB + 2, :].rearrange("p b n -> p (b n)")
            act.wait_ge(b_loaded, 32)
            act.wait_ge(xT_done, 1)
            nc.scalar.copy(xT[:], turned).then_inc(xT_ready, 1)
            act.wait_ge(h_done, 1)
            nc.scalar.copy(hrow[:], hidden_rows).then_inc(hrow_ready, 1)
            act.wait_ge(xT_done, 2)
            nc.scalar.copy(xT[:], turned).then_inc(xT_ready, 1)
            with act.Fori(1, NT + 1) as it:
                if layer == 1:
                    activate(act, it, act.value_load(tile_expert[0:1, bass.ds(it - 1, 1)], min_val=0, max_val=E - 1))
                act.wait_ge(h_done, it + 1)
                act.sem_inc(pace, 1)
                nc.scalar.copy(hrow[:], hidden_rows).then_inc(hrow_ready, 1)
                act.wait_ge(xT_done, it + 2)
                act.sem_inc(pace, 1)
                nc.scalar.copy(xT[:], turned).then_inc(xT_ready, 1)

        @block.vector
        def _(dve):
            dve.wait_ge(b_loaded, 32)
            with dve.Fori(1, NT + 1) as it:
                e = dve.value_load(tile_expert[0:1, bass.ds(it - 1, 1)], min_val=0, max_val=E - 1)
                if layer == 0:
                    activate(dve, it, e)
                dve.wait_ge(y_free, it * 16)
                dve.sem_inc(pace, 1)
                dve.wait_ge(y_done, it)
                dve.sem_inc(pace, 1)
                nc.vector.tensor_tensor(y[:], PS[:, YB, 0:D], b2[:, bass.ds(e * D, D)], ALU.add).then_inc(y_ready, 1)


def collect(nc, g, layer, slot, gates):
    C = layer + 1
    ys, X = g["ys%d" % layer], g["X"]
    GROUP = 4
    ctx = ExitStack()
    with ctx:
        def sb(name, shape, dt=F32):
            return ctx.enter_context(nc.sbuf_tensor("c%d_%s" % (layer, name), shape, dt))

        def sem(name):
            return ctx.enter_context(nc.semaphore("c%d_%s" % (layer, name)))

        yg = sb("yg", [P, GROUP, C, D])
        bn, mv, ve, rs = sb("bn", [P, T, 6]), sb("mv", [P, T, 2]), sb("ve", [P, T]), sb("rs", [P, T])
        gathered = [sem("gathered%d" % i) for i in range(T // GROUP)]
        chain, stats_ready, rs_ready, used = sem("chain"), sem("stats_ready"), sem("rs_ready"), sem("used")
        block = ctx.enter_context(nc.Block())

        @block.gpsimd
        def _(pool):
            for q in range(T // GROUP):
                if q >= 1:
                    pool.wait_ge(used, q)
                for t in range(q * GROUP, (q + 1) * GROUP):
                    for c in range(C):
                        n = t * C + c
                        pool.indirect_dma_start(out=yg[:, t % GROUP, c, :], out_offset=None, in_=ys[:, :],
                                                in_offset=bass.IndirectOffsetOnAxis(ap=slot[:, n:n + 1].bitcast(U32), axis=0))\
                            .then_inc(gathered[q], 16)
            for q in range(T // GROUP):
                pool.wait_ge(stats_ready, q + 1)
                at = slice(q * GROUP, (q + 1) * GROUP)
                nc.gpsimd.tensor_scalar(ve[:, at], mv[:, at, 1], LN_EPS, None, ALU.add).then_inc(rs_ready, 1)
                pool.wait_ge(rs_ready, 2 * q + 1)
                nc.gpsimd.tensor_tensor(rs[:, at], ve[:, at], g["mhalf"][:].to_broadcast([P, GROUP]), ALU.pow)\
                    .then_inc(rs_ready, 1)

        @block.vector
        def _(dve):
            n = [0]

            def link(ins):
                n[0] += 1
                ins.then_inc(chain, 1)
                dve.wait_ge(chain, n[0])

            for q in range(T // GROUP):
                dve.wait_ge(gathered[q], 16 * GROUP * C)
                for t in range(q * GROUP, (q + 1) * GROUP):
                    for c in range(C):
                        ins = nc.vector.scalar_tensor_tensor(X[:, t, :], yg[:, t % GROUP, c, :], gates[:, t, c:c + 1],
                                                             X[:, t, :], ALU.mult, ALU.add)
                        if c == C - 1 and t % GROUP == GROUP - 1:
                            ins.then_inc(used, 1)
                            dve.wait_ge(used, q + 1)
                        else:
                            link(ins)
                    link(nc.vector.bn_stats(bn[:, t, :], X[:, t, :]))
                    ins = nc.vector.bn_aggr(mv[:, t, :], bn[:, t, :])
                ins.then_inc(stats_ready, 1)
            for q in range(T // GROUP):
                dve.wait_ge(rs_ready, 2 * q + 2)
                for t in range(q * GROUP, (q + 1) * GROUP):
                    nc.vector.tensor_scalar(X[:, t, :], X[:, t, :], mv[:, t, 0:1], rs[:, t:t + 1], ALU.subtract, ALU.mult)


def experts0(nc, top, g):
    experts(nc, top, g, 0)

H1, HD1 = 16, 64
P1 = H1 * HD1
NQ = 3 * P1 // 512


def layer1_attention(nc, top, g):
    ctx = ExitStack()
    with ctx:
        def sb(name, shape, dt=F32):
            return ctx.enter_context(nc.sbuf_tensor("l1_" + name, shape, dt))

        loop_sems = []

        def sem(name, kept=False):
            s = ctx.enter_context(nc.semaphore("l1_" + name))
            if not kept:
                loop_sems.append(s)
            return s

        PS, X, ident = g["PS"], g["X"], g["ident"]
        Xg = X[:].rearrange("p (s g) d -> p s g d", s=B)

        w = sb("w", [P, KD, 3 * P1])
        wb = sb("wb", [P, 3 * P1])
        wo = sb("wo", [P, KF, D])
        bo = sb("bo", [P, D])
        xg = sb("xg", [P, B, D])
        xres = sb("xres", [P, B, D])
        xT = sb("xT", [P, B, KD, P])
        qkv = sb("qkv", [P, B, 3 * P1])
        prod = sb("prod", [P, 2, P1])
        sc = sb("sc", [P, B, B, H1])
        mx = sb("mx", [P, B, H1])
        o = sb("o", [P, B, P1])
        oT = sb("oT", [P, 2, KF, P])
        r = sb("r", [P, B, D])
        bn, mv, ve, rs = sb("bn", [P, B, 6]), sb("mv", [P, B, 2]), sb("ve", [P, B]), sb("rs", [P, B])

        w_loaded, ended, go, pace = sem("w_loaded", True), sem("ended", True), sem("go", True), sem("pace", True)
        chain = sem("chain")
        xg_ready, xT_done, xT_ready = sem("xg_ready"), sem("xT_done"), sem("xT_ready")
        qkv_done, qkv_ready = sem("qkv_done"), sem("qkv_ready")
        sc_ready, ex_ready = sem("sc_ready"), sem("ex_ready")
        o_ready, oT_done, oT_ready, proj_done = sem("o_ready"), sem("oT_done"), sem("oT_ready"), sem("proj_done")
        mv_ready, rs_ready = sem("mv_ready"), sem("rs_ready")
        block = ctx.enter_context(nc.Block())
        CHUNKS = [(s, n) for s in range(B) for n in range(4)] + [(s, n) for s in range(B) for n in (4, 5)]
        NB = 6

        @block.sync
        def _(sp):
            for dst, src in ((w, "L1_attn_w"), (wb, "L1_attn_b"), (wo, "L1_attn_wo"), (bo, "L1_attn_bo")):
                sp.dma_start(dst[:], g[src]).then_inc(w_loaded, 16)
            g["clear"](sp, 1)
            sp.sem_inc(go, 1)
            with sp.Fori(1, J + 1) as it:
                each(sp, go, pace, it)
                turn(sp, ended, go, pace, it, loop_sems)

        @block.gpsimd
        def _(pool):
            with pool.Fori(1, J + 1) as it:
                each(pool, go, pace, it)
                for s in range(B):
                    pool.wait_ge(mv_ready, s + 1)
                    nc.gpsimd.tensor_scalar(ve[:, s:s + 1], mv[:, s, 1:2], LN_EPS, None, ALU.add).then_inc(rs_ready, 1)
                    pool.wait_ge(rs_ready, 2 * s + 1)
                    nc.gpsimd.tensor_tensor(rs[:, s:s + 1], ve[:, s:s + 1], g["mhalf"][:], ALU.pow).then_inc(rs_ready, 1)
                ends(pool, ended)

        @block.scalar
        def _(act):
            with act.Fori(1, J + 1) as it:
                each(act, go, pace, it)
                act.wait_ge(xT_done, 1)
                nc.scalar.copy(xT[:].rearrange("p s k n -> p (s k n)"),
                               PS[:, 6:8, :].rearrange("p b n -> p (b n)")).then_inc(xT_ready, 1)
                act.wait_ge(sc_ready, 1)
                nc.scalar.activation(sc[:], sc[:], ACT.Exp, scale=HD1 ** -0.5).then_inc(ex_ready, 1)
                for s in range(B):
                    act.wait_ge(oT_done, s + 1)
                    if s >= 2:
                        act.wait_ge(proj_done, s - 1)
                    nc.scalar.copy(oT[:, s % 2].rearrange("p c n -> p (c n)"),
                                   PS[:, 6:8, :].rearrange("p b n -> p (b n)")).then_inc(oT_ready, 1)
                ends(act, ended)

        @block.vector
        def _(dve):
            n = [0]

            def link(ins):
                n[0] += 1
                ins.then_inc(chain, 1)
                dve.wait_ge(chain, n[0])

            dve.wait_ge(w_loaded, 64)
            with dve.Fori(1, J + 1) as it:
                each(dve, go, pace, it)
                n[0] = 0
                nc.vector.tensor_copy(xg[:], Xg[:, :, bass.ds(it - 1, 1), :].rearrange("p s o d -> p (s o) d"))\
                    .then_inc(xg_ready, 1)
                dve.wait_ge(xg_ready, 1)
                link(nc.vector.tensor_tensor(xres[:], xg[:], bo[:, None, :].to_broadcast([P, B, D]), ALU.add))

                def add_bias(c):
                    s, m = CHUNKS[c]
                    dve.wait_ge(qkv_done, c + 1)
                    at = slice(m * 512, (m + 1) * 512)
                    nc.vector.tensor_tensor(qkv[:, s, at], PS[:, c % NB, :], wb[:, at], ALU.add).then_inc(qkv_ready, 1)

                def heads(s, part):
                    return qkv[:, s, part * P1:(part + 1) * P1].rearrange("p (h d) -> p h d", d=HD1)

                for c in range(4 * B):
                    add_bias(c)
                dve.wait_ge(qkv_ready, 4 * B)
                for i in range(B * B):
                    s, t = i // B, i % B
                    pv = prod[:, i % 2, :].rearrange("p (h d) -> p h d", d=HD1)
                    link(nc.vector.tensor_tensor(pv, heads(s, 0), heads(t, 1), ALU.mult))
                    link(nc.vector.reduce_sum(sc[:, s, t, :], pv, AX_X))
                    if i % 2 == 1:
                        add_bias(4 * B + i // 2)
                link(nc.vector.reduce_max(mx[:], sc[:].rearrange("p s t h -> p s h t"), AX_X))
                nc.vector.tensor_tensor(sc[:], sc[:], mx[:, :, None, :].to_broadcast([P, B, B, H1]),
                                        ALU.subtract).then_inc(sc_ready, 1)
                dve.wait_ge(ex_ready, 1)
                link(nc.vector.reduce_sum(mx[:], sc[:].rearrange("p s t h -> p s h t"), AX_X))
                link(nc.vector.reciprocal(mx[:], mx[:]))
                link(nc.vector.tensor_tensor(sc[:], sc[:], mx[:, :, None, :].to_broadcast([P, B, B, H1]), ALU.mult))
                dve.wait_ge(qkv_ready, NQ * B)

                def mixed(s):
                    ov = o[:, s, :].rearrange("p (h d) -> p h d", d=HD1)
                    for t in range(B):
                        pv = ov if t == 0 else prod[:, t % 2, :].rearrange("p (h d) -> p h d", d=HD1)
                        link(nc.vector.tensor_tensor(pv, heads(t, 2),
                                                     sc[:, s, t, :, None].to_broadcast([P, H1, HD1]), ALU.mult))
                        if t:
                            ins = nc.vector.tensor_tensor(ov, ov, pv, ALU.add)
                            if t < B - 1:
                                link(ins)
                    ins.then_inc(o_ready, 1)

                def residual(s):
                    dve.wait_ge(proj_done, s + 1)
                    link(nc.vector.tensor_tensor(r[:, s, :], PS[:, s, 0:D], xres[:, s, :], ALU.add))
                    link(nc.vector.bn_stats(bn[:, s, :], r[:, s, :]))
                    nc.vector.bn_aggr(mv[:, s, :], bn[:, s, :]).then_inc(mv_ready, 1)

                def norm(s):
                    dve.wait_ge(rs_ready, 2 * s + 2)
                    link(nc.vector.tensor_scalar(r[:, s, :], r[:, s, :], mv[:, s, 0:1], rs[:, s:s + 1],
                                                 ALU.subtract, ALU.mult))

                for s in range(B + 2):
                    if s < B:
                        mixed(s)
                    if 0 <= s - 1 < B:
                        residual(s - 1)
                    if 0 <= s - 2 < B:
                        norm(s - 2)
                nc.vector.tensor_copy(Xg[:, :, bass.ds(it - 1, 1), :].rearrange("p s o d -> p (s o) d"), r[:])
                ends(dve, ended)

        @block.tensor
        def _(pe):
            pe.wait_ge(w_loaded, 64)
            with pe.Fori(1, J + 1) as it:
                each(pe, go, pace, it)
                pe.wait_ge(xg_ready, 1)
                for s in range(B):
                    for k in range(KD):
                        n = s * KD + k
                        mm = nc.tensor.transpose(PS[:, 6 + n // 4, (n % 4) * P:(n % 4 + 1) * P],
                                                 xg[:, s, k * P:(k + 1) * P], ident[:])
                mm.then_inc(xT_done, 1)
                pe.wait_ge(xT_ready, 1)
                for c, (s, m) in enumerate(CHUNKS):
                    if c >= NB:
                        pe.wait_ge(qkv_ready, c - NB + 1)
                    for k in range(KD):
                        mm = nc.tensor.matmul(PS[:, c % NB, :], xT[:, s, k, :], w[:, k, m * 512:(m + 1) * 512],
                                              start=(k == 0), stop=(k == KD - 1))
                    mm.then_inc(qkv_done, 1)
                pe.wait_ge(qkv_ready, NQ * B)

                def turn_out(s):
                    pe.wait_ge(o_ready, s + 1)
                    if s >= 1:
                        pe.wait_ge(oT_ready, s)
                    for c in range(KF):
                        mm = nc.tensor.transpose(PS[:, 6 + c // 4, (c % 4) * P:(c % 4 + 1) * P],
                                                 o[:, s, c * P:(c + 1) * P], ident[:])
                    mm.then_inc(oT_done, 1)

                def project(s):
                    pe.wait_ge(oT_ready, s + 1)
                    for c in range(KF):
                        mm = nc.tensor.matmul(PS[:, s, 0:D], oT[:, s % 2, c, :], wo[:, c, :],
                                              start=(c == 0), stop=(c == KF - 1))
                    mm.then_inc(proj_done, 1)

                for s in range(B):
                    turn_out(s)
                    project(s)
                ends(pe, ended)

HX, HDX = 8, 64
PX = HX * HDX


def layer1_cross(nc, top, g):
    S2 = g["S2"]
    KEYS = S2 + S
    CT = -(-S2 // P)
    LAST = S2 - (CT - 1) * P
    KT = -(-KEYS // P)
    KLAST = KEYS - (KT - 1) * P
    CH = [(c * 512, min(512, KEYS - c * 512)) for c in range(-(-KEYS // 512))]
    NCH = len(CH)
    QU = 2
    UNITS = HX * J // QU
    GT = -(-KT // 2)
    VG = 4
    RING, TB, AVB = 4, 4, 6
    ctx = ExitStack()
    with ctx:
        def sb(name, shape, dt=F32):
            return ctx.enter_context(nc.sbuf_tensor("x_" + name, shape, dt))

        loop_sems = []

        def sem(name, kept=False):
            s = ctx.enter_context(nc.semaphore("x_" + name))
            if not kept:
                loop_sems.append(s)
            return s

        PS, X, LG, ident = g["PS"], g["X"], g["LG"], g["ident"]
        wv = sb("wv", [P, KD, PX])
        wqk = sb("wqk", [P, 2, 2, KD, 2 * HDX])
        wo = sb("wo", [P, HX, D])
        wg = sb("wg", [P, KD, E])
        cols = sb("cols", [P, 4 * KD + 1])
        NS = CT + J
        bn, mv, ve, rs = sb("bn", [P, NS, 6]), sb("mv", [P, NS, 2]), sb("ve", [P, NS]), sb("rs", [P, NS])
        KE = KEYS + KEYS % 2
        kvT = sb("kvT", [P, KD, KE])
        latT = sb("latT", [P, KD, S])
        vs = sb("vs", [P, KT, VG, 2, HDX], F32R)
        ks = sb("ks", [P, 2, KE], F32R)
        qs = sb("qs", [P, 2, S], F32R)
        ps = sb("ps", [P, 2, KT, QU * P], F32R)
        maskf = sb("maskf", [P, KEYS])
        NSM = 2 * QU
        sm = sb("sm", [P, NSM, KEYS])
        mx = sb("mx", [P, 2, NCH])
        nm = sb("nm", [P, 2])
        rsum = sb("rsum", [P, 2 * NSM])
        rrec = sb("rrec", [P, 2 * NSM])
        rb = sb("rb", [P, QU * P])
        o = sb("o", [P, HX, S])
        place = sm[:].rearrange("p a n -> p (a n)")
        at = 0
        cx = place[:, 0:CT * D].rearrange("p (t d) -> p t d", d=D)
        at += CT * D
        ln = place[:, at:at + J * D].rearrange("p (j d) -> p j d", d=D)
        at += J * D
        lx = place[:, at:at + J * D].rearrange("p (j d) -> p j d", d=D)
        at += J * D
        x5 = place[:, at:at + J * D].rearrange("p (j d) -> p j d", d=D)
        x5T = place[:, at + J * D:at + J * D + 2 * D].rearrange("p (b k n) -> p b k n", b=2, n=P)
        at += J * D + 2 * D
        mask8 = place[:, at:at + -(-S2 // 4)].bitcast(U8)[:, 0:S2]

        w_loaded, ended, go, pace = sem("w_loaded", True), sem("ended", True), sem("go", True), sem("pace", True)
        consts, kv_padded = sem("consts", True), sem("kv_padded", True)
        chain, bchain = sem("chain"), sem("bchain")
        cx_loaded, mask_loaded = sem("cx_loaded"), sem("mask_loaded")
        wqk_loaded = sem("wqk_even_loaded"), sem("wqk_odd_loaded")
        stats_ready, rs_ready, ln_ready = sem("stats_ready"), sem("rs_ready"), sem("ln_ready")
        nT_done, nT_ready, gated = sem("nT_done"), sem("nT_ready"), sem("gated")
        ring_done, ring_act, ring_free = sem("ring_done"), sem("ring_act"), sem("ring_free")
        nm_ready, p_ready, rrec_ready = sem("nm_ready"), sem("p_ready"), sem("rrec_ready")
        t_done, ph_ready, pl_ready = sem("t_done"), sem("ph_ready"), sem("pl_ready")
        av_done, lx_again, proj_done = sem("av_done"), sem("lx_again"), sem("proj_done")
        mv_ready, rs5_ready, x5_ready = sem("mv_ready"), sem("rs5_ready"), sem("x5_ready")
        x5T_done, x5T_ready, lg_done = sem("x5T_done"), sem("x5T_ready"), sem("lg_done")
        block = ctx.enter_context(nc.Block())

        GROUPS = [("lat", 0, J)] + [("ctx", t, min(4, CT - t)) for t in range(0, CT, 4)]

        def ring_uses(u, g):
            made = []
            if u == -1 and g == 0:
                made += [("q", 0, 0)] + [("k", 0, c) for c in range(NCH)]
            if u in (0, UNITS // 2):
                made.append(("v", u // (UNITS // 2), g))
            if u + 1 < UNITS and g < NCH:
                made += [("s", u + 1, 2 * g), ("s", u + 1, 2 * g + 1)]
            if u >= 0 and u % 2 == 0 and u + 2 < UNITS and g >= NCH:
                h = u // 2 + 1
                made += [[("q", h, 0), ("k", h, 0)], [("k", h, 1), ("k", h, 2)], [("k", h, 3)], [("k", h, 4)]][g - NCH]
            if u >= 1 and g == GT - 1:
                made.append(("b", u - 1, 0))
            return made

        STEPS = [(u, g) for u in range(-1, UNITS + 1) for g in range(GT)]
        USE = {use: n for n, use in enumerate(use for u, g in STEPS for use in ring_uses(u, g))}
        BUILT, total = {}, 0
        for use in USE:
            total += use[0] in "qkvb"
            BUILT[use] = total

        def width(t0, nt):
            return min(S2, (t0 + nt) * P) - t0 * P

        def even(c):
            return slice(CH[c][0], min(CH[c][0] + 512, KE)), slice(0, min(512, KE - CH[c][0]))

        def keys(t):
            return P if t < KT - 1 else KLAST

        def pair(g):
            return (P, 2) if 2 * g + 1 < KT else (KLAST, 1)

        @block.sync
        def _(sp):
            for dst, src in ((wv, "L1_xattn_Wv"), (wo, "L1_xattn_Wout"),
                             (wg, "L1_ffn_gate"), (cols, "L1_xattn_cols")):
                sp.dma_start(dst[:], g[src]).then_inc(w_loaded, 16)
            sp.sem_inc(go, 1)
            with sp.Fori(1, B + 1) as it:
                each(sp, go, pace, it)
                c = g["ctx"][bass.ds(it - 1, 1)].rearrange("o s d -> (o s) d")
                sp.dma_start(cx[:, 0:CT - 1, :], c[0:(CT - 1) * P, :].rearrange("(t p) d -> p t d", p=P)).then_inc(cx_loaded, 16)
                sp.dma_start(cx[0:LAST, CT - 1, :], c[(CT - 1) * P:S2, :]).then_inc(cx_loaded, 16)
                sp.dma_start(mask8, g["mask"][bass.ds(it - 1, 1), :].to_broadcast([P, S2])).then_inc(mask_loaded, 16)
                for h in range(HX):
                    if h >= 2:
                        sp.wait_ge(ring_done, USE["k", h - 2, NCH - 1] + 1)
                    sp.dma_start(wqk[:, h % 2], g["L1_xattn_Wqk"][h]).then_inc(wqk_loaded[h % 2], 16)
                turn(sp, ended, go, pace, it, loop_sems)

        @block.gpsimd
        def _(pool):
            nc.gpsimd.memset(maskf[:], 0.0).then_inc(consts, 1)
            if KE > KEYS:
                nc.gpsimd.memset(kvT[:, :, KEYS:KE], 0.0).then_inc(kv_padded, 1)
            with pool.Fori(1, B + 1) as it:
                each(pool, go, pace, it)
                pool.wait_ge(stats_ready, 1)
                nc.gpsimd.tensor_scalar(ve[:], mv[:, :, 1], LN_EPS, None, ALU.add).then_inc(rs_ready, 1)
                pool.wait_ge(rs_ready, 1)
                nc.gpsimd.tensor_tensor(rs[:], ve[:], g["mhalf"][:].to_broadcast([P, NS]), ALU.pow).then_inc(rs_ready, 1)
                for j in range(J):
                    pool.wait_ge(mv_ready, j + 1)
                    nc.gpsimd.tensor_scalar(ve[:, j:j + 1], mv[:, j, 1:2], LN_EPS, None, ALU.add).then_inc(rs5_ready, 1)
                    pool.wait_ge(rs5_ready, 2 * j + 1)
                    nc.gpsimd.tensor_tensor(rs[:, j:j + 1], ve[:, j:j + 1], g["mhalf"][:], ALU.pow).then_inc(rs5_ready, 1)
                ends(pool, ended)

        @block.scalar
        def _(act):
            act.wait_ge(w_loaded, 16 * 4)
            with act.Fori(1, B + 1) as it:
                each(act, go, pace, it)
                for i, (kind, t0, nt) in enumerate(GROUPS):
                    for k in range(KD):
                        n = i * KD + k
                        act.wait_ge(nT_done, n + 1)
                        if kind == "lat":
                            dst, wd, at = latT[:, k, :], S, 2 * KD
                        else:
                            wd, at = width(t0, nt), 0
                            dst = kvT[:, k, t0 * P:t0 * P + wd]
                        nc.scalar.activation(dst, PS[:, n % 4, 0:wd], ACT.Identity, bias=cols[:, at + KD + k:at + KD + k + 1],
                                             scale=cols[:, at + k:at + k + 1]).then_inc(nT_ready, 1)

                def high(use):
                    kind, a, c = use
                    act.wait_ge(ring_done, USE[use] + 1)
                    src = PS[:, USE[use] % RING, :]
                    if kind == "q":
                        ins = nc.scalar.mul(qs[:, a % 2, :], src, HDX ** -0.5)
                    elif kind == "k":
                        to, of = even(c)
                        ins = nc.scalar.copy(ks[:, 0, to], src[:, of])
                    elif kind == "b":
                        if a >= 1:
                            act.wait_ge(ring_free, USE["b", a - 1, 0] + 1)
                        ins = nc.scalar.copy(rb[:], src[:, 0:QU * P])
                    else:
                        np_, nt = pair(c)
                        ins = nc.scalar.copy(
                            vs[0:np_, 2 * c:2 * c + nt, :, 0, :],
                            src[0:np_, 0:nt * VG * HDX].rearrange("p (t h d) -> p t h d", t=nt, h=VG))
                    ins.then_inc(ring_act, 1)

                def probs(r):
                    act.wait_ge(nm_ready, r + 1)
                    nc.scalar.activation(sm[:, r % NSM, :], sm[:, r % NSM, :], ACT.Exp, bias=nm[:, r % 2:r % 2 + 1],
                                         accum_out=rsum[:, r % (2 * NSM):r % (2 * NSM) + 1]).then_inc(p_ready, 1)

                for u, g in STEPS:
                    if 0 <= u < UNITS:
                        np_, nt = pair(g)
                        act.wait_ge(t_done, u * GT + g + 1)
                        if u >= 1:
                            act.wait_ge(av_done, (u - 1) * GT + g + 1)
                        nc.scalar.copy(ps[0:np_, 0, 2 * g:2 * g + nt, :],
                                       PS[0:np_, TB + (u * GT + g) % 2, 0:nt * QU * P]
                                       .rearrange("p (t n) -> p t n", t=nt)).then_inc(ph_ready, 1)
                    for use in ring_uses(u, g):
                        if use[0] in "qkvb":
                            high(use)
                    if u + 1 < UNITS and g in (3, 5):
                        probs((u + 1) * QU + (g == 5))
                for j in range(J):
                    act.wait_ge(x5T_done, j + 1)
                    if j >= 2:
                        act.wait_ge(lg_done, j - 1)
                    nc.scalar.copy(x5T[:, j % 2].rearrange("p c n -> p (c n)"), PS[:, 4 + j % 2, 0:D]).then_inc(x5T_ready, 1)
                ends(act, ended)

        @block.vector
        def _(dve):
            n = [0]

            def link(ins):
                n[0] += 1
                ins.then_inc(chain, 1)
                dve.wait_ge(chain, n[0])

            dve.wait_ge(consts, 1)
            with dve.Fori(1, B + 1) as it:
                each(dve, go, pace, it)
                n[0] = 0
                link(nc.vector.tensor_copy(lx, X[:, bass.ds(it * J - J, J), :]))
                rows = [(lx[:, j, :], ln[:, j, :], P) for j in range(J)] + \
                       [(cx[0:P if t < CT - 1 else LAST, t, :], cx[0:P if t < CT - 1 else LAST, t, :],
                         P if t < CT - 1 else LAST) for t in range(CT)]
                link(nc.vector.memset(mv[:, NS - 1, :], 1.0))
                for i, (src, _, np_) in enumerate(rows):
                    if i == J:
                        dve.wait_ge(cx_loaded, 32)
                    nc.vector.bn_stats(bn[0:np_, i, :], src).then_inc(bchain, 1)
                for i, (src, _, np_) in enumerate(rows):
                    dve.wait_ge(bchain, i + 1)
                    ins = nc.vector.bn_aggr(mv[0:np_, i, :], bn[0:np_, i, :])
                ins.then_inc(stats_ready, 1)
                dve.wait_ge(mask_loaded, 16)
                link(nc.vector.tensor_scalar(maskf[:, 0:S2], mask8, -1e30, None, ALU.mult))
                dve.wait_ge(rs_ready, 2)
                for i, (src, dst, np_) in enumerate(rows):
                    nc.vector.tensor_scalar(dst, src, mv[0:np_, i, 0:1], rs[0:np_, i:i + 1], ALU.subtract, ALU.mult)\
                        .then_inc(ln_ready, 1)
                dve.wait_ge(nT_ready, KD)
                for k in range(KD):
                    ins = nc.vector.tensor_scalar(kvT[:, k, S2:KEYS], latT[:, k, :], cols[:, 4 * KD:4 * KD + 1], None, ALU.mult)
                ins.then_inc(gated, 1)

                def read(use):
                    kind, a, c = use
                    src = PS[:, USE[use] % RING, :]
                    dve.wait_ge(ring_done, USE[use] + 1)
                    if kind in "qkvb":
                        dve.wait_ge(ring_act, BUILT[use])
                    if kind == "s":
                        r = a * QU + c // NCH
                        c = c % NCH
                        lo, hi = CH[c][0], CH[c][0] + CH[c][1]
                        if a >= 2:
                            dve.wait_ge(t_done, (a - 1) * GT)
                        ins = nc.vector.tensor_tensor_reduce(
                            out=sm[:, r % NSM, lo:hi], in0=src[:, 0:hi - lo], in1=maskf[:, lo:hi], scale=1.0,
                            scalar=-3e38, op0=ALU.add, op1=ALU.max, accum_out=mx[:, r % 2, c:c + 1])
                    elif kind == "q":
                        half = slice(HDX, 2 * HDX)
                        ins = nc.vector.scalar_tensor_tensor(qs[half, a % 2, :], src[half, :], HDX ** -0.5,
                                                             qs[half, a % 2, :].bitcast(F32), ALU.mult, ALU.subtract)
                    elif kind == "k":
                        to, of = even(c)
                        ins = nc.vector.tensor_tensor(ks[:, 1, to], src[:, of], ks[:, 0, to].bitcast(F32), ALU.subtract)
                    elif kind == "v":
                        np_, nt = pair(c)
                        at = slice(2 * c, 2 * c + nt)
                        ins = nc.vector.tensor_tensor(
                            vs[0:np_, at, :, 1, :],
                            src[0:np_, 0:nt * VG * HDX].rearrange("p (t h d) -> p t h d", t=nt, h=VG),
                            vs[0:np_, at, :, 0, :].bitcast(F32), ALU.subtract)
                    else:
                        dve.wait_ge(av_done, (a + 1) * GT)
                        ins = nc.vector.tensor_tensor(o[:, a // 2, (a % 2) * QU * P:(a % 2 + 1) * QU * P],
                                                      PS[:, AVB + a % 2, 0:QU * P], rb[:], ALU.mult)
                    ins.then_inc(ring_free, 1)
                    if kind == "s" and c == NCH - 1:
                        dve.wait_ge(ring_free, USE[use] + 1)
                        if r >= 2:
                            dve.wait_ge(p_ready, r - 1)
                        link(nc.vector.reduce_max(nm[:, r % 2:r % 2 + 1], mx[:, r % 2, :], AX_X))
                        nc.vector.tensor_scalar(nm[:, r % 2:r % 2 + 1], nm[:, r % 2:r % 2 + 1], -1.0, None, ALU.mult)\
                            .then_inc(nm_ready, 1)

                dve.wait_ge(nT_done, KD * len(GROUPS))
                for u, g in STEPS:
                    for use in ring_uses(u, g):
                        if use[0] != "b":
                            read(use)
                    if 0 <= u < UNITS:
                        np_, nt = pair(g)
                        dve.wait_ge(ph_ready, u * GT + g + 1)
                        nc.vector.tensor_tensor(ps[0:np_, 1, 2 * g:2 * g + nt, :],
                                                PS[0:np_, TB + (u * GT + g) % 2, 0:nt * QU * P]
                                                .rearrange("p (t n) -> p t n", t=nt),
                                                ps[0:np_, 0, 2 * g:2 * g + nt, :].bitcast(F32),
                                                ALU.subtract).then_inc(pl_ready, 1)
                        if g == 0:
                            at = (u * QU) % (2 * NSM)
                            dve.wait_ge(p_ready, (u + 1) * QU)
                            nc.vector.reciprocal(rrec[:, at:at + QU], rsum[:, at:at + QU]).then_inc(rrec_ready, 1)
                    if u >= 1 and g == GT - 1:
                        read(("b", u - 1, 0))
                dve.wait_ge(t_done, UNITS * GT)
                nc.vector.tensor_copy(lx, X[:, bass.ds(it * J - J, J), :]).then_inc(lx_again, 1)
                dve.wait_ge(lx_again, 1)
                for j in range(J):
                    dve.wait_ge(proj_done, j + 1)
                    link(nc.vector.tensor_tensor(lx[:, j, :], PS[:, 2 + j % 2, 0:D], lx[:, j, :], ALU.add))
                    link(nc.vector.bn_stats(bn[:, j, :], lx[:, j, :]))
                    nc.vector.bn_aggr(mv[:, j, :], bn[:, j, :]).then_inc(mv_ready, 1)
                for j in range(J):
                    dve.wait_ge(rs5_ready, 2 * j + 2)
                    nc.vector.tensor_scalar(x5[:, j, :], lx[:, j, :], mv[:, j, 0:1], rs[:, j:j + 1], ALU.subtract, ALU.mult)\
                        .then_inc(x5_ready, 1)
                dve.wait_ge(x5_ready, J)
                nc.vector.tensor_copy(X[:, bass.ds(it * J - J, J), :], x5)
                dve.wait_ge(lg_done, J)
                nc.vector.tensor_copy(LG[:, bass.ds(it * J - J, J), :],
                                      PS[:, 6, 0:J * E].rearrange("p (j e) -> p j e", e=E))
                ends(dve, ended)

        @block.tensor
        def _(pe):
            pe.wait_ge(w_loaded, 16 * 4)
            if KE > KEYS:
                pe.wait_ge(kv_padded, 1)
            with pe.Fori(1, B + 1) as it:
                each(pe, go, pace, it)
                for i, (kind, t0, nt) in enumerate(GROUPS):
                    pe.wait_ge(ln_ready, J if kind == "lat" else J + t0 + nt)
                    for k in range(KD):
                        n = i * KD + k
                        if n >= 4:
                            pe.wait_ge(nT_ready, n - 3)
                        for t in range(nt):
                            if kind == "lat":
                                src, np_ = ln[:, t, k * P:(k + 1) * P], P
                            else:
                                np_ = P if t0 + t < CT - 1 else LAST
                                src = cx[0:np_, t0 + t, k * P:(k + 1) * P]
                            mm = nc.tensor.transpose(PS[:, n % 4, t * P:t * P + np_], src, ident[0:np_, 0:np_])
                        mm.then_inc(nT_done, 1)
                pe.wait_ge(nT_ready, KD * len(GROUPS))
                pe.wait_ge(gated, 1)

                def fill(use):
                    kind, a, c = use
                    n = USE[use]
                    bank = PS[:, n % RING, :]
                    if n >= RING:
                        pe.wait_ge(ring_free, n - RING + 1)
                    if kind == "s":
                        h, q, c = a // 2, (a % 2) * QU + c // NCH, c % NCH
                        pe.wait_ge(ring_free, USE["k", h, c] + 1)
                        of, to = even(c)
                        for part in range(2):
                            mm = nc.tensor.matmul(bank[:, to], qs[:, h % 2, q * P:(q + 1) * P], ks[:, part, of],
                                                  start=(part == 0), stop=(part == 1))
                    elif kind == "b":
                        pe.wait_ge(rrec_ready, a + 1)
                        for q in range(QU):
                            at = (a * QU + q) % (2 * NSM)
                            mm = nc.tensor.transpose(bank[:, q * P:(q + 1) * P], rrec[:, at:at + 1].to_broadcast([P, P]),
                                                     ident[:])
                    elif kind == "v":
                        for t in range(2 * c, min(2 * c + 2, KT)):
                            for k in range(KD):
                                mm = nc.tensor.matmul(bank[0:keys(t), (t % 2) * VG * HDX:(t % 2 + 1) * VG * HDX],
                                                      kvT[:, k, t * P:t * P + keys(t)],
                                                      wv[:, k, a * VG * HDX:(a + 1) * VG * HDX],
                                                      start=(k == 0), stop=(k == KD - 1))
                    else:
                        pe.wait_ge(wqk_loaded[a % 2], 16 * (a // 2 + 1))
                        for k in range(KD):
                            w = wqk[:, a % 2, 0 if kind == "q" else 1, k, :]
                            of, to = even(c)
                            rhs = latT[:, k, :] if kind == "q" else kvT[:, k, of]
                            out = bank if kind == "q" else bank[:, to]
                            mm = nc.tensor.matmul(out, w, rhs, start=(k == 0), stop=(k == KD - 1))
                    mm.then_inc(ring_done, 1)

                for u, g in STEPS:
                    if u >= 1:
                        a = u - 1
                        pe.wait_ge(pl_ready, a * GT + g + 1)
                        if g == 0 and a >= 2:
                            pe.wait_ge(ring_free, USE["b", a - 2, 0] + 1)
                        if a in (0, UNITS // 2):
                            pe.wait_ge(ring_free, USE["v", a // (UNITS // 2), g] + 1)
                        for t in range(2 * g, min(2 * g + 2, KT)):
                            for part in range(2):
                                mm = nc.tensor.matmul(PS[:, AVB + a % 2, 0:QU * P],
                                                      vs[0:keys(t), t, (a // 2) % VG].rearrange("p a d -> p (a d)"),
                                                      ps[0:keys(t), part, t, :],
                                                      start=(t == 0 and part == 0), stop=(t == KT - 1 and part == 1))
                        mm.then_inc(av_done, 1)
                    if 0 <= u < UNITS:
                        n = u * GT + g
                        if g == 0:
                            pe.wait_ge(p_ready, (u + 1) * QU)
                        if n >= 2:
                            pe.wait_ge(pl_ready, n - 1)
                        for t in range(2 * g, min(2 * g + 2, KT)):
                            for q in range(QU):
                                at = (t % 2) * QU * P + q * P
                                mm = nc.tensor.transpose(PS[0:keys(t), TB + n % 2, at:at + P],
                                                         sm[:, (u * QU + q) % NSM, t * P:t * P + keys(t)], ident[:])
                        mm.then_inc(t_done, 1)
                    for use in ring_uses(u, g):
                        fill(use)
                pe.wait_ge(ring_free, len(USE))
                for j in range(J):
                    if j >= 2:
                        pe.wait_ge(mv_ready, j - 1)
                    for h in range(HX):
                        mm = nc.tensor.matmul(PS[:, 2 + j % 2, 0:D], o[:, h, j * P:(j + 1) * P], wo[:, h, :],
                                              start=(h == 0), stop=(h == HX - 1))
                    mm.then_inc(proj_done, 1)
                pe.wait_ge(pl_ready, UNITS * GT)
                for j in range(J + 1):
                    if j < J:
                        pe.wait_ge(x5_ready, j + 1)
                        if j >= 2:
                            pe.wait_ge(x5T_ready, j - 1)
                        for k in range(KD):
                            mm = nc.tensor.transpose(PS[:, 4 + j % 2, k * P:(k + 1) * P], x5[:, j, k * P:(k + 1) * P], ident[:])
                        mm.then_inc(x5T_done, 1)
                    if j >= 1:
                        i = j - 1
                        pe.wait_ge(x5T_ready, i + 1)
                        for k in range(KD):
                            mm = nc.tensor.matmul(PS[:, 6, i * E:(i + 1) * E], x5T[:, i % 2, k, :], wg[:, k, :],
                                                  start=(k == 0), stop=(k == KD - 1))
                        mm.then_inc(lg_done, 1)
                ends(pe, ended)


def experts1(nc, top, g):
    experts(nc, top, g, 1)


def expert_inputs(a, layer, names):
    w1, b1, w2, b2 = (a["L%d_ffn_%s" % (layer, n)] for n in names)
    pre = "L%d_ffn_" % layer
    return {
        pre + "w1": w1.reshape(E, KD, P, F).transpose(0, 2, 1, 3).reshape(E, P, KD * F),
        pre + "w2": w2.reshape(E, KF, P, D).transpose(0, 2, 1, 3).reshape(E, P, KF * D),
        pre + "b1": b1.reshape(E, KF, P).transpose(2, 0, 1).reshape(P, E * KF),
        pre + "b2": spread(b2),
    }


def twice(w):
    w = w.reshape(HX, HDX, D).transpose(1, 0, 2)
    return np.concatenate([w, w], 0)


def heads_twice(wq, wk):
    w = np.stack([w.reshape(KD, P, HX, HDX).transpose(2, 1, 0, 3) for w in (wq, wk)], 2)
    return np.concatenate([w, w], -1)


def more_inputs(a):
    return {
        "L0_ffn_ln_g": spread(a["L0_ffn_ln_g"]), "L0_ffn_ln_b": spread(a["L0_ffn_ln_b"]),
        "L1_attn_w": rows_of(a["L1_attn_in_proj_weight"].T, KD), "L1_attn_b": spread(a["L1_attn_in_proj_bias"]),
        "L1_attn_wo": rows_of(a["L1_attn_out_proj_weight"].T, KF), "L1_attn_bo": spread(a["L1_attn_out_proj_bias"]),
        "ctx": a["ctx_1024"], "mask": a["mask_BxS2_bk0"],
        "L1_xattn_Wqk": heads_twice(a["L1_xattn_Wq"], a["L1_xattn_Wk"]),
        "L1_xattn_Wv": rows_of(a["L1_xattn_Wv"], KD), "L1_xattn_Wout": twice(a["L1_xattn_Wout"]),
        "L1_xattn_cols": np.concatenate(
            [columns(a["L1_xattn_" + n], KD) for n in ("gamma_media", "beta_media", "gamma_lat", "beta_lat")]
            + [np.broadcast_to(a["L1_xattn_kv_gate"].reshape(1, 1), (P, 1))], 1),
        "L1_ffn_gate": rows_of(a["L1_ffn_gate_w"], KD),
        **expert_inputs(a, 0, ("W1", "b1", "W2", "b2")),
        **expert_inputs(a, 1, ("w1", "b1", "w2", "b2")),
    }


def constants(nc, ctx, g):
    sb = lambda name, shape, dt=F32: ctx.enter_context(nc.sbuf_tensor(name, shape, dt))
    g["PS"] = ctx.enter_context(nc.psum_tensor("PS", [P, 8, 512], F32))
    g["X"] = sb("X", [P, T, D])
    g["LG"] = sb("LG", [P, T, E])
    g["ident"] = sb("ident", [P, P])
    g["ones"] = sb("ones", [P, P])
    g["half"] = sb("half", [P, 1])
    g["mhalf"] = sb("mhalf", [P, 1])
    g["x_loaded"] = ctx.enter_context(nc.semaphore("x_loaded"))
    g["consts"] = ctx.enter_context(nc.semaphore("consts_ready"))
    g["xs_cleared"] = ctx.enter_context(nc.semaphore("xs_cleared"))
    zeros = g["zeros"] = sb("zeros", [P, D])

    def clear(eng, layer):
        n = tiles_of(layer + 1) + 2
        eng.wait_ge(g["consts"], g["n_consts"])
        eng.dma_start(g["xs%d" % layer].rearrange("(n p) d -> p n d", p=P),
                      zeros[:, None, :].to_broadcast([P, n, D])).then_inc(g["xs_cleared"], 16)

    g["clear"] = clear
    for layer in range(2):
        n = tiles_of(layer + 1)
        g["xs%d" % layer] = nc.dram_tensor("xs%d" % layer, ((n + 2) * P, D), F32, kind="Internal").ap()
        g["ys%d" % layer] = nc.dram_tensor("ys%d" % layer, (n * P, D), F32, kind="Internal").ap()
    with nc.Block() as block:
        @block.gpsimd
        def _(pool):
            pool.memset(g["ident"][:], 0.0).then_inc(g["consts"], 1)
            pool.memset(g["ones"][:], 1.0).then_inc(g["consts"], 1)
            pool.memset(g["half"][:], 0.5).then_inc(g["consts"], 1)
            pool.memset(g["mhalf"][:], -0.5).then_inc(g["consts"], 1)
            pool.wait_ge(g["consts"], 4)
            pool.affine_select(out=g["ident"][:], in_=g["ident"][:], compare_op=ALU.not_equal, fill=1.0, base=0,
                               pattern=[[-1, P]], channel_multiplier=1).then_inc(g["consts"], 1)
            pool.memset(zeros[:], 0.0).then_inc(g["consts"], 1)
        g["n_consts"] = 6


def store(nc, ctx, g):
    stored = ctx.enter_context(nc.semaphore("stored"))
    with nc.Block() as block:
        @block.sync
        def _(sp):
            sp.dma_start(g["out"].rearrange("b (j p) d -> p (b j) d", p=P), g["X"][:]).then_inc(stored, 16)
            sp.wait_ge(stored, 16)


def build(nc, g):
    with ExitStack() as ctx:
        constants(nc, ctx, g)
        for phase in [layer0_attention, experts0, layer1_attention, layer1_cross, experts1]:
            phase(nc, ctx, g)
        store(nc, ctx, g)


def rows_of(w, k):
    return np.ascontiguousarray(w.reshape(k, P, -1).transpose(1, 0, 2))


def spread(v):
    return np.ascontiguousarray(np.broadcast_to(v.reshape(1, -1), (P, v.size)))


def columns(v, k):
    return np.ascontiguousarray(v.reshape(k, P).T)


def kernel(**inputs):
    import concourse.bacc as bacc
    from concourse.bass_utils import run_bass_kernel_spmd as run

    a = {k: np.asarray(v) for k, v in inputs.items()}
    x, c = a["x"], a["ctx_1024"]
    s2 = c.shape[1]
    xT = np.zeros((B + 1, P, KD, S), x.dtype)
    xT[:B] = x.reshape(B, S, KD, P).transpose(0, 3, 2, 1)
    om = a["L0_attn_omega"].transpose(1, 2, 0, 3).reshape(2, 8, HD0, FD0)
    omega = np.zeros((8, HD0, 2, 8, FD0), om.dtype)
    for h in range(8):
        omega[h, :, :, h, :] = om[:, h].transpose(1, 0, 2)
    node = np.repeat(a["L0_attn_quad_nodes"], M0)
    weight = np.repeat(a["L0_attn_quad_weights"], M0)
    nodes = np.stack([np.concatenate([node, node]), np.concatenate([weight, weight])], 1)
    W = a["L0_xattn_W"]
    ins = {
        "x": x.reshape(B, J, P, D).transpose(2, 0, 1, 3).reshape(P, T, D),
        "xT": xT,
        "ctxT": c.reshape(B, s2, KD, P).transpose(0, 3, 2, 1),
        "L0_attn_Wqkv": rows_of(a["L0_attn_Wqkv"], KD),
        "L0_attn_bqkv": spread(a["L0_attn_bqkv"]),
        "L0_attn_omega": omega.reshape(P, 2, 8 * FD0),
        "L0_attn_nodes": nodes,
        "L0_attn_bout": spread(a["L0_attn_bout"]),
        "L0_attn_Wout": rows_of(a["L0_attn_Wout"], KD),
        "L0_xattn_W1": rows_of(W[:, :D].T, KD),
        "L0_xattn_W2": rows_of(W[:, D:].T, KD),
        "L0_xattn_b": spread(a["L0_xattn_b"]),
        "L0_ffn_Wr": rows_of(a["L0_ffn_Wr"], KD),
        "L0_ffn_br": spread(a["L0_ffn_br"]),
    }
    ins.update(more_inputs(a))
    nc = bacc.Bacc("TRN2", target_bir_lowering=False, num_devices=1)
    g = {"S2": s2}
    arrays = {}
    for name, v in ins.items():
        v = arrays["in_" + name] = np.ascontiguousarray(v)
        g[name] = nc.dram_tensor("in_" + name, v.shape, mybir.dt.from_np(v.dtype), kind="ExternalInput").ap()
    g["out"] = nc.dram_tensor("out", x.shape, F32, kind="ExternalOutput").ap()
    build(nc, g)
    r = run(nc, [arrays], core_ids=[0])
    return r.results[0]["out"]
```

```python
from contextlib import ExitStack

import numpy as np

import concourse.bass as bass
from concourse import mybir

F32 = mybir.dt.float32
F32R = mybir.dt.float32r
I32 = mybir.dt.int32
U32 = mybir.dt.uint32
U8 = mybir.dt.uint8
ALU = mybir.AluOpType
ACT = mybir.ActivationFunctionType
AX_X = mybir.AxisListType.X

P = 128
B, S, D = 4, 512, 256
KD = D // P
J = S // P
T = B * J
LN_EPS = 1e-5

H0, HD0, R0, M0 = 16, 16, 2, 32
FD0 = R0 * M0
PAIRS0 = H0 * FD0 // P
VW0 = HD0 + 1

E, F = 8, 1024
KF = F // P


def each(eng, go, pace, it):
    eng.wait_ge(go, it)
    eng.sem_inc(pace, 1)


def ends(eng, ended):
    eng.drain().then_inc(ended, 1)


def turn(sp, ended, go, pace, it, sems):
    sp.wait_ge(ended, it * 4)
    sp.sem_inc(pace, 1)
    nums = sorted(s.num for s in sems)
    starts = [n for n in nums if n - 1 not in nums]
    ends_at = [n for n in nums if n + 1 not in nums]
    for first, last in zip(starts, ends_at):
        sp.sem_clear(range(first, last + 1))
    sp.sem_inc(go, 1)


def layer0_attention(nc, sc, g):
    ctx = ExitStack()
    with ctx:
        def sb(name, shape, dt=F32):
            return ctx.enter_context(nc.sbuf_tensor(name, shape, dt))

        loop_sems = []

        def sem(name, kept=False):
            s = ctx.enter_context(nc.semaphore(name))
            if not kept:
                loop_sems.append(s)
            return s

        PS = g["PS"]
        ident, X, LG = g["ident"], g["X"], g["LG"]

        wqkv = sb("wqkv", [P, KD, 3 * D])
        wout = sb("wout0", [P, KD, D])
        w1t = sb("w1t", [P, KD, D])
        w2t = sb("w2t", [P, KD, D])
        wr = sb("wr", [P, KD, E])
        omega = sb("omega", [P, KD, KD * 2 * P])
        bqkv = sb("bqkv", [P, 3 * D])
        bout = sb("bout0", [P, D])
        bx = sb("bx", [P, D])
        brt = sb("brt", [P, E])
        nodes = sb("nodes", [P, 2])
        fscale = sb("fscale", [P, 4])
        causal = sb("causal", [P, P])
        xT = sb("xT", [P, KD, S])
        ctxT = sb("ctxT", [P, KD, g["S2"]])
        xres = sb("xres", [P, J, D])
        qk = sb("qk", [P, J, 2 * D])
        v1 = sb("v1", [P, J, H0, VW0])
        sq = sb("sq", [P, 2, 2 * D])
        ss = sb("ss", [P, J, 2 * H0])
        rn = sb("rn", [P, J, 2 * H0])
        qkT = sb("qkT", [P, 4, S])
        fe = sb("fe", [P, 4, S])
        kfT = sb("kfT", [P, PAIRS0, S])
        qbd = sb("qbd", [P, PAIRS0, J, 2 * P])
        kfR = sb("kfR", [P, J - 1, PAIRS0, P])
        scm = sb("scm", [P, 2, 4, P])
        state = sb("state", [P, PAIRS0, 2 * VW0])
        den = sb("den", [P, H0])
        rden = sb("rden", [P, H0])
        osb = sb("osb", [P, D])
        oT = sb("oT", [P, KD, P])
        r1 = sb("r1", [P, D])
        r2 = sb("r2", [P, D])
        bn = sb("bn", [P, 2, 6])
        mv = sb("mv", [P, 2, 2])
        ve = sb("ve", [P, 2])
        rs = sb("rs", [P, 2])
        x1 = sb("x1", [P, J, D])
        x1T = sb("x1T", [P, KD, P])
        x1pb = sb("x1pb", [P, D])
        x2 = sb("x2", [P, J, D])
        x2T = sb("x2T", [P, KD, P])
        lgs = sb("lgs", [P, J, E])
        csum = sb("csum", [P, KD])
        cbc = sb("cbc", [P, KD, P])
        pb = sb("pb", [P, D])

        w_loaded = sem("a_w_loaded", True)
        wqkv_loaded = sem("a_wqkv_loaded", True)
        xT_loaded = sem("a_xT_loaded", True)
        ctx_loaded = sem("a_ctx_loaded", True)
        x_loaded = g["x_loaded"]
        consts = sem("a_consts", True)
        ended = sem("a_ended", True)
        go = sem("a_go", True)
        pace = sem("a_pace", True)
        chain = sem("a_chain")
        pchain = sem("a_pchain")
        qkv_done = sem("a_qkv_done")
        qk_ready = sem("a_qk_ready")
        v_ready = sem("a_v_ready")
        sq_ready = sem("a_sq_ready")
        ss_ready = sem("a_ss_ready")
        qkn_ready = sem("a_qkn_ready")
        qkT_done = sem("a_qkT_done")
        qkT_ready = sem("a_qkT_ready")
        feat_done = sem("a_feat_done")
        feat_exp = sem("a_feat_exp")
        k_ready = sem("a_k_ready")
        q_clipped = sem("a_q_clipped")
        q_ready = sem("a_q_ready")
        kfR_done = sem("a_kfR_done")
        kfR_ready = sem("a_kfR_ready")
        scores_done = sem("a_scores_done")
        masked = sem("a_masked")
        av_done = sem("a_av_done")
        state_done = sem("a_state_done")
        state_ready = sem("a_state_ready")
        o_ready = sem("a_o_ready")
        oT_done = sem("a_oT_done")
        oT_ready = sem("a_oT_ready")
        proj_done = sem("a_proj_done")
        xres_ready = sem("a_xres_ready")
        r1_ready = sem("a_r1_ready")
        mv1_ready = sem("a_mv1_ready")
        rs1_ready = sem("a_rs1_ready")
        x1_ready = sem("a_x1_ready")
        x1T_done = sem("a_x1T_done")
        x1T_ready = sem("a_x1T_ready")
        x1pb_ready = sem("a_x1pb_ready")
        rn_ready = sem("a_rn_ready")
        part_done = sem("a_part_done")
        r2_ready = sem("a_r2_ready")
        mv2_ready = sem("a_mv2_ready")
        rs2_ready = sem("a_rs2_ready")
        x2_ready = sem("a_x2_ready")
        x2T_done = sem("a_x2T_done")
        x2T_ready = sem("a_x2T_ready")
        lg_done = sem("a_lg_done")
        lg_ready = sem("a_lg_ready")
        cbc_ready = sem("a_cbc_ready")
        part2_done = sem("a_part2_done")
        pb_ready = sem("a_pb_ready")

        block = ctx.enter_context(nc.Block())

        @block.sync
        def _(sp):
            sp.dma_start(wqkv[:], g["L0_attn_Wqkv"]).then_inc(wqkv_loaded, 16)
            sp.dma_start(xT[:], g["xT"][0]).then_inc(xT_loaded, 16)
            sp.dma_start(bqkv[:], g["L0_attn_bqkv"]).then_inc(wqkv_loaded, 16)
            sp.dma_start(ctxT[:], g["ctxT"][0]).then_inc(ctx_loaded, 16)
            for dst, src in ((omega, g["L0_attn_omega"]),
                             (nodes, g["L0_attn_nodes"]), (bout, g["L0_attn_bout"]), (wout, g["L0_attn_Wout"]),
                             (w1t, g["L0_xattn_W1"]), (w2t, g["L0_xattn_W2"]), (bx, g["L0_xattn_b"]),
                             (wr, g["L0_ffn_Wr"]), (brt, g["L0_ffn_br"])):
                sp.dma_start(dst[:], src).then_inc(w_loaded, 16)
            sp.dma_start(X[:], g["x"]).then_inc(x_loaded, 16)
            sp.sem_inc(go, 1)
            with sp.Fori(1, B + 1) as it:
                each(sp, go, pace, it)
                sp.wait_ge(cbc_ready, 1)
                sp.dma_start(ctxT[:], g["ctxT"][bass.ds(it, 1)].rearrange("o p k s -> p (o k) s"))\
                    .then_inc(ctx_loaded, 16)
                sp.wait_ge(qkv_done, J)
                sp.dma_start(xT[:], g["xT"][bass.ds(it, 1)].rearrange("o p k s -> p (o k) s"))\
                    .then_inc(xT_loaded, 16)
                turn(sp, ended, go, pace, it, loop_sems)
            g["clear"](sp, 0)
            sp.wait_ge(xT_loaded, 16 * (B + 1))
            sp.wait_ge(ctx_loaded, 16 * (B + 1))

        @block.gpsimd
        def _(pool):
            n = [0]

            def link(ins):
                n[0] += 1
                ins.then_inc(pchain, 1)
                pool.wait_ge(pchain, n[0])

            nc.gpsimd.memset(causal[:], 1.0).then_inc(consts, 1)
            pool.wait_ge(consts, 1)
            nc.gpsimd.affine_select(out=causal[:], in_=causal[:], compare_op=ALU.is_ge, fill=0.0, base=0,
                                    pattern=[[1, P]], channel_multiplier=-1).then_inc(consts, 1)
            nc.gpsimd.memset(qbd[:], 0.0).then_inc(consts, 1)
            nc.gpsimd.memset(v1[:], 1.0).then_inc(consts, 1)
            pool.wait_ge(w_loaded, 16 * 9)
            nc.gpsimd.tensor_scalar(fscale[:, 3:4], nodes[:, 0:1], 0.0, 2.0, ALU.max, ALU.mult).then_inc(consts, 1)
            nc.gpsimd.tensor_scalar(fscale[:, 1:2], nodes[:, 0:1], -1.0, None, ALU.mult).then_inc(consts, 1)
            nc.gpsimd.tensor_scalar(fscale[:, 2:3], nodes[:, 1:2], 0.0, 1.0 / M0, ALU.max, ALU.mult).then_inc(consts, 1)
            pool.wait_ge(consts, 7)
            nc.gpsimd.tensor_tensor(fscale[:, 0:1], fscale[:, 3:4], g["half"][:], ALU.pow).then_inc(consts, 1)
            pool.wait_ge(x_loaded, 16)
            with pool.Fori(1, B + 1) as it:
                each(pool, go, pace, it)
                n[0] = 0
                nc.gpsimd.tensor_tensor(xres[:], X[:, bass.ds(it * J - J, J), :],
                                        bout[:, None, :].to_broadcast([P, J, D]), ALU.add).then_inc(xres_ready, 1)

                for s in range(J + 1):
                    if s < J:
                        pool.wait_ge(mv1_ready, s + 1)
                        link(nc.gpsimd.tensor_scalar(ve[:, 0:1], mv[:, 0, 1:2], LN_EPS, None, ALU.add))
                        nc.gpsimd.tensor_tensor(rs[:, 0:1], ve[:, 0:1], g["mhalf"][:], ALU.pow).then_inc(rs1_ready, 1)
                    if s >= 1:
                        pool.wait_ge(mv2_ready, s)
                        link(nc.gpsimd.tensor_scalar(ve[:, 1:2], mv[:, 1, 1:2], LN_EPS, None, ALU.add))
                        nc.gpsimd.tensor_tensor(rs[:, 1:2], ve[:, 1:2], g["mhalf"][:], ALU.pow).then_inc(rs2_ready, 1)
                ends(pool, ended)

        @block.scalar
        def _(act):
            act.wait_ge(consts, 8)
            with act.Fori(1, B + 1) as it:
                each(act, go, pace, it)
                for j in range(J + 3):
                    if j < J:
                        act.wait_ge(qk_ready, j + 1)
                        if j >= 2:
                            act.wait_ge(ss_ready, j - 1)
                        nc.scalar.activation(sq[:, j % 2, :], qk[:, j, :], ACT.Square).then_inc(sq_ready, 1)
                    if 1 <= j < J + 1:
                        act.wait_ge(ss_ready, j)
                        nc.scalar.activation(rn[:, j - 1, :], ss[:, j - 1, :], ACT.Sqrt).then_inc(rn_ready, 1)
                    if j >= 3:
                        at = j - 3
                        act.wait_ge(qkT_done, at + 1)
                        nc.scalar.copy(qkT[:, :, at * P:(at + 1) * P],
                                       PS[:, 4 + at % 2, :].rearrange("p (c n) -> p c n", c=4)).then_inc(qkT_ready, 1)

                for f in range(2 * PAIRS0):
                    p = f // 2
                    act.wait_ge(feat_done, f + 1)
                    if p >= 2:
                        act.wait_ge(q_ready if f % 2 else k_ready, p - 1)
                    nc.scalar.activation(fe[:, f % 4, :], PS[:, f % 4, :], ACT.Exp, bias=fscale[:, 1:2],
                                         scale=fscale[:, 0:1]).then_inc(feat_exp, 1)
                for p in range(PAIRS0):
                    act.wait_ge(kfR_done, p + 1)
                    nc.scalar.copy(kfR[:, :, p, :],
                                   PS[:, 4 + p % 2, 0:(J - 1) * P].rearrange("p (j n) -> p j n", n=P))\
                        .then_inc(kfR_ready, 1)

                def turned(dst, bank, done, used, ready, s):
                    act.wait_ge(done, s + 1)
                    if s >= 1:
                        act.wait_ge(used, s)
                    nc.scalar.copy(dst[:], PS[:, bank, 0:D].rearrange("p (k n) -> p k n", k=KD)).then_inc(ready, 1)

                for s in range(J + 2):
                    if 0 <= s - 1 < J:
                        turned(oT, 4, oT_done, proj_done, oT_ready, s - 1)
                    if 0 <= s - 2 < J:
                        turned(x2T, 2, x2T_done, lg_done, x2T_ready, s - 2)
                    if 0 <= s - 1 < J:
                        turned(x1T, 5, x1T_done, part_done, x1T_ready, s - 1)
                act.wait_ge(x2_ready, J)
                nc.scalar.copy(X[:, bass.ds(it * J - J, J), :], x2[:])
                act.wait_ge(lg_ready, J)
                nc.scalar.copy(LG[:, bass.ds(it * J - J, J), :], lgs[:])
                ends(act, ended)

        @block.vector
        def _(dve):
            n = [0]

            def link(ins):
                n[0] += 1
                ins.then_inc(chain, 1)
                dve.wait_ge(chain, n[0])

            dve.wait_ge(wqkv_loaded, 32)
            dve.wait_ge(consts, 8)
            with dve.Fori(1, B + 1) as it:
                each(dve, go, pace, it)
                n[0] = 0
                dve.wait_ge(ctx_loaded, 16 * it)
                dve.sem_inc(pace, 1)
                link(nc.vector.reduce_sum(csum[:], ctxT[:], AX_X))
                for k in range(KD):
                    ins = nc.vector.tensor_scalar(cbc[:, k, :], g["ones"][:], csum[:, k:k + 1], 1.0 / g["S2"],
                                                  ALU.mult, ALU.mult)
                ins.then_inc(cbc_ready, 1)

                def add_bias(j):
                    dve.wait_ge(qkv_done, j + 1)
                    u = PS[:, 2 * (j % 2):2 * (j % 2) + 2, :].rearrange("p b n -> p (b n)")
                    nc.vector.tensor_tensor(qk[:, j, :], u[:, 0:2 * D], bqkv[:, 0:2 * D], ALU.add).then_inc(qk_ready, 1)
                    nc.vector.tensor_tensor(v1[:, j, :, 0:HD0],
                                            u[:, 2 * D:3 * D].rearrange("p (h d) -> p h d", d=HD0),
                                            bqkv[:, 2 * D:3 * D].rearrange("p (h d) -> p h d", d=HD0),
                                            ALU.add).then_inc(v_ready, 1)

                def square_sums(j):
                    dve.wait_ge(sq_ready, j + 1)
                    nc.vector.reduce_sum(ss[:, j, :], sq[:, j % 2, :].rearrange("p (h d) -> p h d", d=HD0), AX_X)\
                        .then_inc(ss_ready, 1)

                def normalise(j):
                    dve.wait_ge(rn_ready, j + 1)
                    link(nc.vector.tensor_scalar(rn[:, j, :], rn[:, j, :], 1e-12, None, ALU.max))
                    link(nc.vector.reciprocal(rn[:, j, :], rn[:, j, :]))
                    v = qk[:, j, :].rearrange("p (h d) -> p h d", d=HD0)
                    nc.vector.tensor_tensor(v, v, rn[:, j, :, None].to_broadcast([P, 2 * H0, HD0]), ALU.mult)\
                        .then_inc(qkn_ready, 1)

                for j in range(J + 2):
                    if j < J:
                        add_bias(j)
                    if 1 <= j < J + 1:
                        square_sums(j - 1)
                    if j >= 2:
                        normalise(j - 2)
                dve.wait_ge(part2_done, 1)
                nc.vector.tensor_tensor(pb[:], PS[:, 7, 0:D], bx[:], ALU.add).then_inc(pb_ready, 1)
                low, high = float(np.exp(-20.0)), float(np.exp(20.0))
                for f in range(2 * PAIRS0):
                    dve.wait_ge(feat_exp, f + 1)
                    dst, ready = (fe[:, f % 4, :], q_clipped) if f % 2 else (kfT[:, f // 2, :], k_ready)
                    nc.vector.tensor_scalar(dst, fe[:, f % 4, :], high, low, ALU.min, ALU.max).then_inc(ready, 1)
                    if f % 2:
                        p = f // 2
                        dve.wait_ge(q_clipped, p + 1)
                        for half in range(2):
                            at = slice(64 * half, 64 * half + 64)
                            ins = nc.vector.tensor_scalar(
                                qbd[at, p, :, P * half:P * half + P],
                                fe[at, f % 4, :].rearrange("p (j n) -> p j n", j=J), fscale[at, 2:3], None, ALU.mult)
                        ins.then_inc(q_ready, 1)

                def mask(s, q):
                    dve.wait_ge(scores_done, 4 * s + q + 1)
                    if 4 * s + q >= 2:
                        dve.wait_ge(av_done, 4 * s + q - 1)
                    nc.vector.tensor_tensor(scm[:, q % 2, :, :], PS[:, q % 2, :].rearrange("p (h n) -> p h n", n=P),
                                            causal[:, None, :].to_broadcast([P, 4, P]), ALU.mult).then_inc(masked, 1)

                def add_state(s):
                    dve.wait_ge(state_done, s + 1)
                    dve.wait_ge(av_done, 4 * s + 4)
                    new = PS[:, 7, 0:PAIRS0 * 2 * VW0].rearrange("p (a w) -> p a w", a=PAIRS0)
                    if s == 0:
                        ins = nc.vector.tensor_copy(state[:], new)
                    else:
                        dve.wait_ge(state_ready, s)
                        ins = nc.vector.tensor_tensor(state[:], new, state[:], ALU.add)
                    ins.then_inc(state_ready, 1)

                def divide(s):
                    dve.wait_ge(av_done, 4 * s + 4)
                    if s >= 1:
                        dve.wait_ge(oT_done, s)
                    o = PS[:, 6, 0:H0 * VW0].rearrange("p (h w) -> p h w", w=VW0)
                    link(nc.vector.tensor_scalar(den[:, :, None], o[:, :, HD0:VW0], 1e-6, None, ALU.max))
                    link(nc.vector.reciprocal(rden[:], den[:]))
                    nc.vector.tensor_tensor(osb[:].rearrange("p (h d) -> p h d", d=HD0), o[:, :, 0:HD0],
                                            rden[:, :, None].to_broadcast([P, H0, HD0]), ALU.mult).then_inc(o_ready, 1)

                def residual(s, i, done, add, r, ready, mv_ready):
                    dve.wait_ge(done, s + 1)
                    if i == 1:
                        dve.wait_ge(x1pb_ready, s + 1)
                    nc.vector.tensor_tensor(r[:], PS[:, 3, D * i:D * i + D], add, ALU.add).then_inc(ready, 1)
                    dve.wait_ge(ready, s + 1)
                    link(nc.vector.bn_stats(bn[:, i, :], r[:]))
                    nc.vector.bn_aggr(mv[:, i, :], bn[:, i, :]).then_inc(mv_ready, 1)

                def norm(s, i, rs_ready, r, dst, ready):
                    dve.wait_ge(rs_ready, s + 1)
                    nc.vector.tensor_scalar(dst, r[:], mv[:, i, 0:1], rs[:, i:i + 1], ALU.subtract, ALU.mult)\
                        .then_inc(ready, 1)

                for s in range(J + 2):
                    if s < J:
                        mask(s, 0)
                        mask(s, 1)
                    if 0 <= s - 2 < J:
                        residual(s - 2, 1, part_done, x1pb[:], r2, r2_ready, mv2_ready)
                    if s < J:
                        mask(s, 2)
                    if 0 <= s - 1 < J:
                        if s == 1:
                            dve.wait_ge(xres_ready, 1)
                        residual(s - 1, 0, proj_done, xres[:, s - 1, :], r1, r1_ready, mv1_ready)
                    if 0 <= s - 2 < J:
                        norm(s - 2, 1, rs2_ready, r2, x2[:, s - 2, :], x2_ready)
                    if s < J:
                        mask(s, 3)
                    if 0 <= s - 1 < J:
                        norm(s - 1, 0, rs1_ready, r1, x1[:, s - 1, :], x1_ready)
                        dve.wait_ge(x1_ready, s)
                        nc.vector.tensor_tensor(x1pb[:], x1[:, s - 1, :], pb[:], ALU.add).then_inc(x1pb_ready, 1)
                    if s < J - 1:
                        add_state(s)
                    if s < J:
                        divide(s)
                    if 0 <= s - 2 < J:
                        dve.wait_ge(lg_done, s - 1)
                        nc.vector.tensor_tensor(lgs[:, s - 2, :], PS[:, 2, D:D + E], brt[:], ALU.add)\
                            .then_inc(lg_ready, 1)
                ends(dve, ended)

        @block.tensor
        def _(pe):
            pe.wait_ge(wqkv_loaded, 32)
            pe.wait_ge(g["consts"], g["n_consts"])
            with pe.Fori(1, B + 1) as it:
                each(pe, go, pace, it)
                pe.wait_ge(xT_loaded, 16 * it)
                pe.sem_inc(pace, 1)

                def qkv(j):
                    if j >= 2:
                        pe.wait_ge(v_ready, j - 1)
                    for half, cols in ((0, 2 * D), (1, D)):
                        for k in range(KD):
                            mm = nc.tensor.matmul(PS[:, 2 * (j % 2) + half, 0:cols], xT[:, k, j * P:(j + 1) * P],
                                                  wqkv[:, k, half * 2 * D:half * 2 * D + cols],
                                                  start=(k == 0), stop=(k == KD - 1))
                    mm.then_inc(qkv_done, 1)

                def turn_qk(j):
                    pe.wait_ge(qkn_ready, j + 1)
                    if j >= 2:
                        pe.wait_ge(qkT_ready, j - 1)
                    for c in range(4):
                        mm = nc.tensor.transpose(PS[:, 4 + j % 2, c * P:(c + 1) * P], qk[:, j, c * P:(c + 1) * P],
                                                 ident[:])
                    mm.then_inc(qkT_done, 1)

                for j in range(J):
                    qkv(j)
                pe.wait_ge(w_loaded, 16 * 9)
                pe.wait_ge(cbc_ready, 1)
                for k in range(KD):
                    mm = nc.tensor.matmul(PS[:, 7, 0:D], cbc[:, k, :], w2t[:, k, :], start=(k == 0), stop=(k == KD - 1))
                mm.then_inc(part2_done, 1)
                for j in range(J):
                    turn_qk(j)
                pe.wait_ge(v_ready, J)
                pe.wait_ge(qkT_ready, J)
                for f in range(2 * PAIRS0):
                    p, q_side = f // 2, f % 2
                    if f >= 4:
                        pe.wait_ge(feat_exp, f - 3)
                    half = p // 4
                    nc.tensor.matmul(PS[:, f % 4, :], omega[:, half, (p % 4) * P:(p % 4 + 1) * P],
                                     qkT[:, half if q_side else 2 + half, :], start=True, stop=True).then_inc(feat_done, 1)
                for p in range(PAIRS0):
                    pe.wait_ge(k_ready, p + 1)
                    if p >= 2:
                        pe.wait_ge(kfR_ready, p - 1)
                    for j in range(J - 1):
                        mm = nc.tensor.transpose(PS[:, 4 + p % 2, j * P:(j + 1) * P], kfT[:, p, j * P:(j + 1) * P], ident[:])
                    mm.then_inc(kfR_done, 1)
                pe.wait_ge(feat_exp, 2 * PAIRS0)
                pe.wait_ge(pb_ready, 1)

                def scores(s, q):
                    if 4 * s + q >= 2:
                        pe.wait_ge(masked, 4 * s + q - 1)
                    if s == 0:
                        pe.wait_ge(q_ready, 2 * q + 2)
                    for i in range(2):
                        p = 2 * q + i
                        mm = nc.tensor.matmul(PS[:, q % 2, i * 2 * P:(i + 1) * 2 * P], kfT[:, p, s * P:(s + 1) * P],
                                              qbd[:, p, s, :], start=True, stop=True)
                    mm.then_inc(scores_done, 1)

                def weigh(s, q):
                    pe.wait_ge(masked, 4 * s + q + 1)
                    if s >= 1 and q == 0:
                        pe.wait_ge(o_ready, s)
                        pe.wait_ge(state_ready, s)
                    for i in range(4):
                        h = 4 * q + i
                        out = PS[:, 6, h * VW0:(h + 1) * VW0]
                        mm = nc.tensor.matmul(out, scm[:, q % 2, i, :], v1[:, s, h, :], start=True, stop=(s == 0))
                        if s >= 1:
                            mm = nc.tensor.matmul(out, qbd[:, h // 2, s, (h % 2) * P:(h % 2 + 1) * P],
                                                  state[:, h // 2, (h % 2) * VW0:(h % 2 + 1) * VW0],
                                                  start=False, stop=True)
                    mm.then_inc(av_done, 1)

                def new_state(s):
                    if s == 0:
                        pe.wait_ge(kfR_ready, PAIRS0)
                    else:
                        pe.wait_ge(state_ready, s)
                    for p in range(PAIRS0):
                        mm = nc.tensor.matmul(PS[:, 7, p * 2 * VW0:(p + 1) * 2 * VW0], kfR[:, s, p, :],
                                              v1[:, s, 2 * p:2 * p + 2, :].rearrange("p h w -> p (h w)"),
                                              start=True, stop=True)
                    mm.then_inc(state_done, 1)

                def turn_rows(s, src, bank, ready, used, done):
                    pe.wait_ge(ready, s + 1)
                    if used is not None and s >= 1:
                        pe.wait_ge(used, s)
                    if s == 0:
                        pe.wait_ge(kfR_ready, PAIRS0)
                    for k in range(KD):
                        mm = nc.tensor.transpose(PS[:, bank, k * P:(k + 1) * P], src[:, k * P:(k + 1) * P], ident[:])
                    mm.then_inc(done, 1)

                def project(s, at, lhs, ready, w, done):
                    pe.wait_ge(ready, s + 1)
                    for k in range(KD):
                        mm = nc.tensor.matmul(PS[:, 3, at:at + D], lhs[:, k, :], w[:, k, :],
                                              start=(k == 0), stop=(k == KD - 1))
                    mm.then_inc(done, 1)

                for s in range(J + 2):
                    main, first, second = s < J, 0 <= s - 1 < J, 0 <= s - 2 < J
                    if main:
                        scores(s, 0)
                        scores(s, 1)
                    if second:
                        pe.wait_ge(r1_ready, s - 1)
                        project(s - 2, D, x1T, x1T_ready, w1t, part_done)
                    if first:
                        turn_rows(s - 1, osb, 4, o_ready, oT_ready, oT_done)
                    if main:
                        weigh(s, 0)
                        scores(s, 2)
                    if first:
                        if s >= 2:
                            pe.wait_ge(r2_ready, s - 1)
                        project(s - 1, 0, oT, oT_ready, wout, proj_done)
                    if main:
                        weigh(s, 1)
                        scores(s, 3)
                    if second:
                        if s >= 3:
                            pe.wait_ge(lg_ready, s - 2)
                        turn_rows(s - 2, x2[:, s - 2, :], 2, x2_ready, x2T_ready, x2T_done)
                    if main:
                        weigh(s, 2)
                    if first:
                        turn_rows(s - 1, x1[:, s - 1, :], 5, x1_ready, x1T_ready, x1T_done)
                    if main:
                        weigh(s, 3)
                    if s < J - 1:
                        new_state(s)
                    if second:
                        pe.wait_ge(x2T_ready, s - 1)
                        for k in range(KD):
                            mm = nc.tensor.matmul(PS[:, 2, D:D + E], x2T[:, k, :], wr[:, k, :],
                                                  start=(k == 0), stop=(k == KD - 1))
                        mm.then_inc(lg_done, 1)
                ends(pe, ended)


def tiles_of(choices):
    return choices * T + E - 1


def experts(nc, top, g, layer):
    C = layer + 1
    TC = T * C
    NT = tiles_of(C)
    xs, ys = g["xs%d" % layer], g["ys%d" % layer]
    PS, X, LG, ident, ones = g["PS"], g["X"], g["LG"], g["ident"], g["ones"]
    ctx = ExitStack()
    with ctx:
        def sb(name, shape, dt=F32):
            return ctx.enter_context(nc.sbuf_tensor("f%d_%s" % (layer, name), shape, dt))

        def sem(name):
            return ctx.enter_context(nc.semaphore("f%d_%s" % (layer, name)))

        w1 = sb("w1", [P, E * KD * F])
        w2 = sb("w2", [P, E * KF * D])
        b1 = sb("b1", [P, E * KF])
        b2 = sb("b2", [P, E * D])
        slot = sb("slot", [P, TC], I32)
        tile_expert = sb("tile_expert", [P, NT + 2], I32)
        gates = sb("gates", [P, T, C])
        w_loaded, b_loaded = sem("w_loaded"), sem("b_loaded")

        def load_expert(eng, e):
            if e >= 1:
                eng.wait_ge(w_loaded, 32 * e)
            eng.dma_start(w1[:, e * KD * F:(e + 1) * KD * F], g["L%d_ffn_w1" % layer][e]).then_inc(w_loaded, 16)
            eng.dma_start(w2[:, e * KF * D:(e + 1) * KF * D], g["L%d_ffn_w2" % layer][e]).then_inc(w_loaded, 16)

        dispatch(nc, g, layer, slot, tile_expert, gates, load_expert, b1, b2, b_loaded)
        multiply(nc, g, layer, w1, w2, b1, b2, tile_expert, load_expert, w_loaded, b_loaded)
        collect(nc, g, layer, slot, gates, w1)


EARLY = 1


def dispatch(nc, g, layer, slot, tile_expert, gates, load_expert, b1, b2, b_loaded):
    C = layer + 1
    TC = T * C
    NT = tiles_of(C)
    xs = g["xs%d" % layer]
    PS, X, LG, ones = g["PS"], g["X"], g["LG"], g["ones"]
    ctx = ExitStack()
    with ctx:
        def sb(name, shape, dt=F32):
            return ctx.enter_context(nc.sbuf_tensor("d%d_%s" % (layer, name), shape, dt))

        def sem(name):
            return ctx.enter_context(nc.semaphore("d%d_%s" % (layer, name)))

        before = sb("before", [P, P])
        iota = sb("iota", [P, NT + 2], I32)
        iotaf = sb("iotaf", [P, NT + 2])
        less = sb("less", [P, E])
        again = sb("again", [P, E, TC])
        lg2 = sb("lg2", [P, T, E])
        top = sb("top", [P, C, T])
        eq = sb("eq", [P, T, E])
        cand = sb("cand", [P, T, E])
        low = sb("low", [P, T])
        oh = sb("oh", [P, T, C, E])
        ex = sb("ex", [P, T, E])
        gd = sb("gd", [P, T])
        tot = sb("tot", [P, E, TC])
        cum = sb("cum", [P, E, TC])
        more = sb("more", [P, E, T])
        ntile = sb("ntile", [P, E])
        tend = sb("tend", [P, E])
        row0 = sb("row0", [P, E])
        base = sb("base", [P, E, TC])
        at = sb("at", [P, TC, E])
        slotf = sb("slotf", [P, TC])
        past = sb("past", [P, NT + 2, E])
        tef = sb("tef", [P, NT + 2])

        consts, chain, bchain = sem("consts"), sem("chain"), sem("bchain")
        oh_ready, counted, slot_ready = sem("oh_ready"), sem("counted"), sem("slot_ready")
        ex_in, ex_done, scattered = sem("ex_in"), sem("ex_done"), sem("scattered")
        stats_ready, rs_ready, xn_done, xn_ready = sem("stats_ready"), sem("rs_ready"), sem("xn_done"), sem("xn_ready")
        if layer == 0:
            xn = g["l1_w"][:].rearrange("p k n -> p (k n)")[:, 0:T * D].rearrange("p (t d) -> p t d", d=D)
            lng = sb("lng", [P, D])
            lnb = sb("lnb", [P, D])
            bn = sb("bn", [P, T, 6])
            mv = sb("mv", [P, T, 2])
            rs = sb("rs", [P, T])
            ln_loaded = sem("ln_loaded")
        rows = xn if layer == 0 else X
        block = ctx.enter_context(nc.Block())

        @block.sync
        def _(sp):
            if layer == 0:
                sp.dma_start(lng[:], g["L0_ffn_ln_g"]).then_inc(ln_loaded, 16)
                sp.dma_start(lnb[:], g["L0_ffn_ln_b"]).then_inc(ln_loaded, 16)
            sp.dma_start(b1[:], g["L%d_ffn_b1" % layer]).then_inc(b_loaded, 16)
            sp.dma_start(b2[:], g["L%d_ffn_b2" % layer]).then_inc(b_loaded, 16)

        @block.gpsimd
        def _(pool):
            nc.gpsimd.memset(before[:], 1.0).then_inc(consts, 1)
            pool.wait_ge(consts, 1)
            nc.gpsimd.affine_select(out=before[:], in_=before[:], compare_op=ALU.is_gt, fill=0.0, base=0,
                                    pattern=[[1, P]], channel_multiplier=-1).then_inc(consts, 1)
            nc.gpsimd.iota(iota[:], [[1, NT + 2]], base=0, channel_multiplier=0).then_inc(consts, 1)
            nc.gpsimd.memset(again[:], 1.0).then_inc(consts, 1)
            pool.wait_ge(consts, 4)
            nc.gpsimd.memset(again[:, :, 0:1], 0.0).then_inc(consts, 1)
            nc.gpsimd.tensor_copy(iotaf[:], iota[:]).then_inc(consts, 1)
            for e in range(EARLY):
                load_expert(pool, e)
            if layer == 0:
                pool.wait_ge(stats_ready, T)
                nc.gpsimd.tensor_scalar(rs[:], mv[:, :, 1], LN_EPS, None, ALU.add).then_inc(rs_ready, 1)
                pool.wait_ge(rs_ready, 1)
                nc.gpsimd.tensor_tensor(rs[:], rs[:], g["mhalf"][:].to_broadcast([P, T]), ALU.pow).then_inc(rs_ready, 1)
            pool.wait_ge(slot_ready, 1)
            pool.wait_ge(g["xs_cleared"], 16 * (layer + 1))
            for t in range(T):
                if layer == 0:
                    pool.wait_ge(xn_ready, t + 1)
                for c in range(C):
                    n = t * C + c
                    pool.indirect_dma_start(out=xs[:, :], out_offset=bass.IndirectOffsetOnAxis(ap=slot[:, n:n + 1].bitcast(U32), axis=0),
                                            in_=rows[:, t, :], in_offset=None).then_inc(scattered, 16)
            pool.wait_ge(scattered, 16 * TC)

        @block.scalar
        def _(act):
            act.wait_ge(ex_in, 1)
            if C == 1:
                nc.scalar.activation(ex[:], ex[:], ACT.Exp).then_inc(ex_done, 1)
            else:
                nc.scalar.activation(gd[:], gd[:], ACT.Exp).then_inc(ex_done, 1)

        @block.vector
        def _(dve):
            n = [0]

            def link(ins):
                n[0] += 1
                ins.then_inc(chain, 1)
                dve.wait_ge(chain, n[0])

            dve.wait_ge(consts, 6)
            link(nc.vector.tensor_scalar(less[:], iotaf[:, 0:E], -100.0, None, ALU.add))
            for c in range(C):
                src = LG if c == 0 else lg2
                link(nc.vector.reduce_max(top[:, c, :], src[:], AX_X))
                link(nc.vector.tensor_tensor(eq[:], src[:], top[:, c, :, None].to_broadcast([P, T, E]), ALU.is_equal))
                link(nc.vector.tensor_scalar(cand[:], eq[:], -100.0, None, ALU.mult))
                link(nc.vector.tensor_tensor(cand[:], cand[:], iotaf[:, None, 0:E].to_broadcast([P, T, E]), ALU.add))
                link(nc.vector.tensor_reduce(low[:], cand[:], AX_X, ALU.min))
                ins = nc.vector.tensor_tensor(oh[:, :, c, :], less[:, None, :].to_broadcast([P, T, E]),
                                              low[:, :, None].to_broadcast([P, T, E]), ALU.is_equal)
                if c < C - 1:
                    link(ins)
                    link(nc.vector.tensor_scalar(lg2[:], oh[:, :, c, :], -1e30, None, ALU.mult))
                    link(nc.vector.tensor_tensor(lg2[:], lg2[:], LG[:], ALU.add))
                else:
                    ins.then_inc(oh_ready, 1)
            if C == 1:
                nc.vector.tensor_tensor(ex[:], LG[:], top[:, 0, :, None].to_broadcast([P, T, E]),
                                        ALU.subtract).then_inc(ex_in, 1)
            else:
                nc.vector.tensor_tensor(gd[:], top[:, 1, :], top[:, 0, :], ALU.subtract).then_inc(ex_in, 1)
            if layer == 0:
                for t in range(T):
                    nc.vector.bn_stats(bn[:, t, :], X[:, t, :]).then_inc(bchain, 1)
                for t in range(T):
                    dve.wait_ge(bchain, t + 1)
                    nc.vector.bn_aggr(mv[:, t, :], bn[:, t, :]).then_inc(stats_ready, 1)
            dve.wait_ge(ex_done, 1)
            if C == 1:
                link(nc.vector.reduce_sum(gd[:], ex[:], AX_X))
                link(nc.vector.reciprocal(gates[:, :, 0], gd[:]))
            else:
                link(nc.vector.tensor_scalar(low[:], gd[:], 1.0, None, ALU.add))
                link(nc.vector.reciprocal(gates[:, :, 0], low[:]))
                link(nc.vector.tensor_tensor(gates[:, :, 1], gates[:, :, 0], gd[:], ALU.mult))
            dve.wait_ge(counted, 1)
            sums = PS[:, 1, 0:TC * E].rearrange("p (n e) -> p e n", e=E)
            link(nc.vector.tensor_copy(tot[:], sums))
            flat = lambda a: a[:].rearrange("p e n -> p (e n)")
            link(nc.vector.tensor_tensor_scan(flat(cum), flat(again), flat(tot), 0.0, ALU.mult, ALU.add))
            link(nc.vector.tensor_scalar(slotf[:, 0:T], iotaf[:, 0:T], float(P), None, ALU.mult))
            link(nc.vector.tensor_tensor(more[:], cum[:, :, TC - 1:TC].to_broadcast([P, E, T]),
                                         slotf[:, None, 0:T].to_broadcast([P, E, T]), ALU.is_gt))
            link(nc.vector.reduce_sum(ntile[:], more[:], AX_X))
            link(nc.vector.tensor_tensor_scan(tend[:], ones[:, 0:E], ntile[:], 0.0, ALU.mult, ALU.add))
            link(nc.vector.tensor_tensor(row0[:], tend[:], ntile[:], ALU.subtract))
            link(nc.vector.tensor_scalar(row0[:], row0[:], float(P), None, ALU.mult))
            link(nc.vector.tensor_tensor(base[:], cum[:], tot[:], ALU.subtract))
            link(nc.vector.tensor_tensor(base[:], base[:], row0[:, :, None].to_broadcast([P, E, TC]), ALU.add))
            link(nc.vector.tensor_tensor(at[:], PS[:, 0, 0:TC * E].rearrange("p (n e) -> p n e", e=E),
                                         base[:].rearrange("p e n -> p n e"), ALU.add))
            link(nc.vector.tensor_tensor(at[:], at[:], oh[:].rearrange("p t c e -> p (t c) e"), ALU.mult))
            link(nc.vector.reduce_sum(slotf[:], at[:], AX_X))
            nc.vector.tensor_copy(slot[:], slotf[:]).then_inc(slot_ready, 1)
            if layer == 0:
                dve.wait_ge(rs_ready, 2)
                dve.wait_ge(ln_loaded, 32)
                for t in range(T):
                    link(nc.vector.tensor_scalar(xn[:, t, :], X[:, t, :], mv[:, t, 0:1], rs[:, t:t + 1],
                                                 ALU.subtract, ALU.mult))
                    link(nc.vector.tensor_tensor(xn[:, t, :], xn[:, t, :], lng[:], ALU.mult))
                    nc.vector.tensor_tensor(xn[:, t, :], xn[:, t, :], lnb[:], ALU.add).then_inc(xn_ready, 1)
            link(nc.vector.tensor_tensor(past[:], iotaf[:, :, None].to_broadcast([P, NT + 2, E]),
                                         tend[:, None, :].to_broadcast([P, NT + 2, E]), ALU.is_ge))
            link(nc.vector.reduce_sum(tef[:], past[:], AX_X))
            link(nc.vector.tensor_scalar(tef[:], tef[:], float(E - 1), None, ALU.min))
            link(nc.vector.tensor_copy(tile_expert[:], tef[:]))

        @block.tensor
        def _(pe):
            pe.wait_ge(oh_ready, 1)
            pe.wait_ge(consts, 2)
            flat = oh[:].rearrange("p t c e -> p (t c e)")
            nc.tensor.matmul(PS[:, 0, 0:TC * E], before[:], flat, start=True, stop=True)
            nc.tensor.matmul(PS[:, 1, 0:TC * E], ones[:], flat, start=True, stop=True).then_inc(counted, 1)


def multiply(nc, g, layer, w1, w2, b1, b2, tile_expert, load_expert, w_loaded, b_loaded):
    C = layer + 1
    NT = tiles_of(C)
    xs, ys = g["xs%d" % layer], g["ys%d" % layer]
    PS, ident = g["PS"], g["ident"]
    XB, HB, TB, YB = 0, 1, 3, 5
    ctx = ExitStack()
    with ctx:
        def sb(name, shape, dt=F32):
            return ctx.enter_context(nc.sbuf_tensor("m%d_%s" % (layer, name), shape, dt))

        def sem(name):
            return ctx.enter_context(nc.semaphore("m%d_%s" % (layer, name)))

        xin = sb("xin", [P, D])
        xT = sb("xT", [P, KD, P])
        hrow = sb("hrow", [P, F])
        hT = sb("hT", [P, KF, P])
        y = sb("y", [P, D])
        xin_loaded, xT_done, xT_ready = sem("xin_loaded"), sem("xT_done"), sem("xT_ready")
        h_done, hrow_ready, hT_done, hT_ready = sem("h_done"), sem("hrow_ready"), sem("hT_done"), sem("hT_ready")
        y_done, y_ready, y_free = sem("y_done"), sem("y_ready"), sem("y_free")
        pace, prepared = sem("pace"), sem("prepared")
        block = ctx.enter_context(nc.Block())
        rows = lambda a, i: a[bass.ds(i * P, P), :]

        @block.sync
        def _(sp):
            sp.dma_start(xin[:], xs[0:P, :]).then_inc(xin_loaded, 16)
            sp.wait_ge(xT_done, 1)
            sp.dma_start(xin[:], xs[P:2 * P, :]).then_inc(xin_loaded, 16)
            sp.sem_inc(y_free, 16)
            with sp.Fori(1, NT + 1) as it:
                sp.wait_ge(xT_done, it + 1)
                sp.dma_start(xin[:], rows(xs, it + 1)).then_inc(xin_loaded, 16)
                sp.wait_ge(y_ready, it)
                sp.dma_start(rows(ys, it - 1), y[:]).then_inc(y_free, 16)
            sp.wait_ge(y_free, 16 * (NT + 1))
            sp.wait_ge(xin_loaded, 16 * (NT + 2))

        @block.gpsimd
        def _(pool):
            for e in range(EARLY, E):
                load_expert(pool, e)
            pool.wait_ge(w_loaded, 32 * E)
            if layer == 0:
                g["l1_prepare"](pool, prepared)

        @block.tensor
        def _(pe):
            def turn_tile():
                for k in range(KD):
                    mm = nc.tensor.transpose(PS[:, XB, k * P:(k + 1) * P], xin[:, k * P:(k + 1) * P], ident[:])
                mm.then_inc(xT_done, 1)

            def hidden(e):
                pe.wait_ge(w_loaded, e * 32 + 32)
                pe.sem_inc(pace, 1)
                for n in range(F // 512):
                    for k in range(KD):
                        mm = nc.tensor.matmul(PS[:, HB + n, :], xT[:, k, :],
                                              w1[:, bass.ds(e * (KD * F) + (k * F + n * 512), 512)],
                                              start=(k == 0), stop=(k == KD - 1))
                mm.then_inc(h_done, 1)

            pe.wait_ge(xin_loaded, 16)
            turn_tile()
            pe.wait_ge(xT_ready, 1)
            hidden(pe.value_load(tile_expert[0:1, 0:1], min_val=0, max_val=E - 1))
            pe.wait_ge(xin_loaded, 32)
            turn_tile()
            with pe.Fori(1, NT + 1) as it:
                e = pe.value_load(tile_expert[0:1, bass.ds(it - 1, 1)], min_val=0, max_val=E - 1)
                e1 = pe.value_load(tile_expert[0:1, bass.ds(it, 1)], min_val=0, max_val=E - 1)
                pe.wait_ge(hrow_ready, it)
                pe.sem_inc(pace, 1)
                for c in range(KF):
                    mm = nc.tensor.transpose(PS[:, TB + c // 4, (c % 4) * P:(c % 4 + 1) * P],
                                             hrow[:, c * P:(c + 1) * P], ident[:])
                mm.then_inc(hT_done, 1)
                pe.wait_ge(xT_ready, it + 1)
                pe.sem_inc(pace, 1)
                hidden(e1)
                pe.wait_ge(xin_loaded, it * 16 + 32)
                pe.sem_inc(pace, 1)
                turn_tile()
                pe.wait_ge(hT_ready, it)
                pe.sem_inc(pace, 1)
                for c in range(KF):
                    mm = nc.tensor.matmul(PS[:, YB, 0:D], hT[:, c, :], w2[:, bass.ds(e * (KF * D) + c * D, D)],
                                          start=(c == 0), stop=(c == KF - 1))
                mm.then_inc(y_done, 1)

        def activate(eng, it, e):
            eng.wait_ge(hT_done, it)
            eng.sem_inc(pace, 1)
            for c in range(KF):
                src = PS[:, TB + c // 4, (c % 4) * P:(c % 4 + 1) * P]
                bias = b1[:, bass.ds(e * KF + c, 1)]
                if layer == 0:
                    ins = nc.vector.tensor_scalar(hT[:, c, :], src, bias, 0.0, ALU.add, ALU.max)
                else:
                    ins = nc.scalar.activation(hT[:, c, :], src, ACT.Gelu, bias=bias)
            ins.then_inc(hT_ready, 1)

        @block.scalar
        def _(act):
            turned = PS[:, XB, 0:D].rearrange("p (k n) -> p k n", k=KD)
            hidden_rows = PS[:, HB:HB + 2, :].rearrange("p b n -> p (b n)")
            act.wait_ge(b_loaded, 32)
            act.wait_ge(xT_done, 1)
            nc.scalar.copy(xT[:], turned).then_inc(xT_ready, 1)
            act.wait_ge(h_done, 1)
            nc.scalar.copy(hrow[:], hidden_rows).then_inc(hrow_ready, 1)
            act.wait_ge(xT_done, 2)
            nc.scalar.copy(xT[:], turned).then_inc(xT_ready, 1)
            with act.Fori(1, NT + 1) as it:
                if layer == 1:
                    activate(act, it, act.value_load(tile_expert[0:1, bass.ds(it - 1, 1)], min_val=0, max_val=E - 1))
                act.wait_ge(h_done, it + 1)
                act.sem_inc(pace, 1)
                nc.scalar.copy(hrow[:], hidden_rows).then_inc(hrow_ready, 1)
                act.wait_ge(xT_done, it + 2)
                act.sem_inc(pace, 1)
                nc.scalar.copy(xT[:], turned).then_inc(xT_ready, 1)

        @block.vector
        def _(dve):
            dve.wait_ge(b_loaded, 32)
            with dve.Fori(1, NT + 1) as it:
                e = dve.value_load(tile_expert[0:1, bass.ds(it - 1, 1)], min_val=0, max_val=E - 1)
                if layer == 0:
                    activate(dve, it, e)
                dve.wait_ge(y_free, it * 16)
                dve.sem_inc(pace, 1)
                dve.wait_ge(y_done, it)
                dve.sem_inc(pace, 1)
                nc.vector.tensor_tensor(y[:], PS[:, YB, 0:D], b2[:, bass.ds(e * D, D)], ALU.add).then_inc(y_ready, 1)


def collect(nc, g, layer, slot, gates, room):
    C = layer + 1
    ys, X = g["ys%d" % layer], g["X"]
    GROUP = 4
    LAG = 3 - C
    ctx = ExitStack()
    with ctx:
        def sb(name, shape, dt=F32):
            return ctx.enter_context(nc.sbuf_tensor("c%d_%s" % (layer, name), shape, dt))

        def sem(name):
            return ctx.enter_context(nc.semaphore("c%d_%s" % (layer, name)))

        yg = room[:, 0:T * C * D].rearrange("p (t c d) -> p t c d", t=T, c=C)
        bn, mv, ve, rs = sb("bn", [P, T, 6]), sb("mv", [P, T, 2]), sb("ve", [P, T]), sb("rs", [P, T])
        gathered = [sem("gathered%d" % i) for i in range(T // GROUP)]
        chain, stats_ready, rs_ready = sem("chain"), sem("stats_ready"), sem("rs_ready")
        ve_ready = sem("ve_ready")
        x_ready, stored = sem("x_ready"), sem("stored")
        block = ctx.enter_context(nc.Block())

        @block.sync
        def _(sp):
            if layer == 1:
                for q in range(T // GROUP):
                    sp.wait_ge(x_ready, q + 1)
                    at = slice(q * GROUP, (q + 1) * GROUP)
                    sp.dma_start(g["out"].rearrange("b (j p) d -> p (b j) d", p=P)[:, at, :], X[:, at, :]).then_inc(stored, 16)
                sp.wait_ge(stored, 16 * (T // GROUP))

        @block.gpsimd
        def _(pool):
            for q in range(T // GROUP + LAG):
                if q < T // GROUP:
                    for n in range(q * GROUP * C, (q + 1) * GROUP * C):
                        pool.indirect_dma_start(out=yg[:, n // C, n % C, :], out_offset=None, in_=ys[:, :],
                                                in_offset=bass.IndirectOffsetOnAxis(ap=slot[:, n:n + 1].bitcast(U32), axis=0))\
                            .then_inc(gathered[q], 16)
                if q >= LAG:
                    at = slice((q - LAG) * GROUP, (q - LAG + 1) * GROUP)
                    pool.wait_ge(stats_ready, q - LAG + 1)
                    nc.gpsimd.tensor_scalar(ve[:, at], mv[:, at, 1], LN_EPS, None, ALU.add).then_inc(ve_ready, 1)
                    pool.wait_ge(ve_ready, q - LAG + 1)
                    nc.gpsimd.tensor_tensor(rs[:, at], ve[:, at], g["mhalf"][:].to_broadcast([P, GROUP]), ALU.pow)\
                        .then_inc(rs_ready, 1)

        @block.vector
        def _(dve):
            n = [0]

            def link(ins):
                n[0] += 1
                ins.then_inc(chain, 1)
                dve.wait_ge(chain, n[0])

            for q in range(T // GROUP + LAG):
                if q < T // GROUP:
                    dve.wait_ge(gathered[q], 16 * GROUP * C)
                    tiles = range(q * GROUP, (q + 1) * GROUP)
                    for c in range(C):
                        for t in tiles:
                            ins = nc.vector.scalar_tensor_tensor(X[:, t, :], yg[:, t, c, :], gates[:, t, c:c + 1],
                                                                 X[:, t, :], ALU.mult, ALU.add)
                        link(ins)
                    for t in tiles:
                        ins = nc.vector.bn_stats(bn[:, t, :], X[:, t, :])
                    link(ins)
                    for t in tiles:
                        ins = nc.vector.bn_aggr(mv[:, t, :], bn[:, t, :])
                    ins.then_inc(stats_ready, 1)
                if q >= LAG:
                    dve.wait_ge(rs_ready, q - LAG + 1)
                    for t in range((q - LAG) * GROUP, (q - LAG + 1) * GROUP):
                        ins = nc.vector.tensor_scalar(X[:, t, :], X[:, t, :], mv[:, t, 0:1], rs[:, t:t + 1],
                                                      ALU.subtract, ALU.mult)
                    ins.then_inc(x_ready, 1)


def experts0(nc, top, g):
    experts(nc, top, g, 0)


H1, HD1 = 16, 64
P1 = H1 * HD1
NB1 = 3 * P1 + D
BF16 = mybir.dt.bfloat16


def layer1_weights(nc, ctx, g):
    w = g["l1_w"] = ctx.enter_context(nc.sbuf_tensor("l1_w", [P, KD, 3 * P1], F32))
    wo = g["l1_wo"] = ctx.enter_context(nc.sbuf_tensor("l1_wo", [P, KF, D], F32))
    loaded = g["l1_loaded"] = ctx.enter_context(nc.semaphore("l1_w_loaded"))

    bias = g["l1_bias"] = ctx.enter_context(nc.sbuf_tensor("l1_bias", [3, NB1], BF16))
    ones3 = g["l1_ones3"] = ctx.enter_context(nc.sbuf_tensor("l1_ones3", [3, P], BF16))
    b_loaded = ctx.enter_context(nc.semaphore("l1_b_loaded"))
    sent = g["l1_bias_sent"] = ctx.enter_context(nc.semaphore("l1_bias_sent"))

    def prepare(pool, chain):
        whole = w[0:1].rearrange("p k n -> p (k n)")[:, 0:NB1]
        first = w[0:1].rearrange("p k n -> p (k n)")[:, NB1:NB1 + NB1 // 2].bitcast(BF16)
        second = wo[0:1].rearrange("p k n -> p (k n)")[:, 0:NB1 // 2].bitcast(BF16)
        n = [0]

        def link(ins):
            n[0] += 1
            ins.then_inc(chain, 1)
            pool.wait_ge(chain, n[0])

        pool.dma_start(whole, g["L1_attn_b"][0:1, :]).then_inc(b_loaded, 16)
        pool.wait_ge(g["consts"], g["n_consts"])
        link(nc.gpsimd.tensor_copy(ones3[:], g["ones"][0:3, :]))
        pool.wait_ge(b_loaded, 16)
        for i, part in enumerate((first, second, first)):
            if i == 2:
                pool.wait_ge(sent, 32)
            link(nc.gpsimd.tensor_copy(part, whole))
            pool.dma_start(bias[i:i + 1, :], part).then_inc(sent, 16)
            if i < 2:
                link(nc.gpsimd.tensor_tensor(whole, whole, part, ALU.subtract))
        pool.wait_ge(sent, 48)
        for k in range(KD):
            for part in range(3):
                at = slice(part * P1, (part + 1) * P1)
                pool.dma_start(w[:, k, at], g["L1_attn_w"][:, k, at]).then_inc(loaded, 16)
        for k in range(0, KF, 4):
            pool.dma_start(wo[:, k:k + 4, :], g["L1_attn_wo"][:, k:k + 4, :]).then_inc(loaded, 16)
        g["l1_loads"] = 3 * KD + KF // 4

    g["l1_prepare"] = prepare


def layer1_attention(nc, top, g):
    ctx = ExitStack()
    with ctx:
        def sb(name, shape, dt=F32):
            return ctx.enter_context(nc.sbuf_tensor("l1_" + name, shape, dt))

        def sem(name):
            return ctx.enter_context(nc.semaphore("l1_" + name))

        PS, X, ident = g["PS"], g["X"], g["ident"]
        w, wo, w_loaded = g["l1_w"], g["l1_wo"], g["l1_loaded"]
        RING, PB, OB = 4, 4, 6
        bias, ones3, bias_sent = g["l1_bias"], g["l1_ones3"], g["l1_bias_sent"]
        xT = sb("xT", [P, B, KD, P])
        qkv = sb("qkv", [P, 2, B, 3 * P1])
        prod = sb("prod", [P, 2, P1])
        pp = sb("pp", [P, 2, P1])
        sc = sb("sc", [P, B, B, H1])
        mx = sb("mx", [P, B, H1])
        o = sb("o", [P, B, P1])
        oT = sb("oT", [P, 2, KF, P])
        r = sb("r", [P, B, D])
        bn, mv, ve, rs = sb("bn", [P, B, 6]), sb("mv", [P, B, 2]), sb("ve", [P, B]), sb("rs", [P, B])
        chain = sem("chain")
        ring_done, ring_free = sem("ring_done"), sem("ring_free")
        pp_ready, pp_used, sc_ready, ex_ready, attn_ready = sem("pp_ready"), sem("pp_used"), sem("sc_ready"), sem("ex_ready"), sem("attn_ready")
        third_added, o_ready = sem("third_added"), sem("o_ready")
        oT_done, oT_ready, proj_done = sem("oT_done"), sem("oT_ready"), sem("proj_done")
        r_ready, mv_ready, rs_ready, x_ready = sem("r_ready"), sem("mv_ready"), sem("rs_ready"), sem("x_ready")
        block = ctx.enter_context(nc.Block())

        TURNED = B // 2
        CHUNKS = [(s, n) for s in range(B) for n in range(4)] + [(s, n) for s in range(B) for n in (4, 5)]
        USES = TURNED + len(CHUNKS)
        QK = TURNED + 4 * B
        PAIRS = sorted(((s, t) for s in range(B) for t in range(B)), key=max)
        POOL_PAIRS = (2, 5, 8, 11, 14)
        NP = len(POOL_PAIRS)

        def tile(s, grp):
            return X[:, s * J + grp, :]

        def heads(grp, s, part):
            return qkv[:, grp % 2, s, part * P1:(part + 1) * P1].rearrange("p (h d) -> p h d", d=HD1)

        def by_head(a):
            return a.rearrange("p (h d) -> p h d", d=HD1)

        def share(s, t):
            return sc[:, s, t, :, None].to_broadcast([P, H1, HD1])

        def rstd(pool, grp):
            pool.wait_ge(mv_ready, (grp + 1) * B)
            nc.gpsimd.tensor_scalar(ve[:], mv[:, :, 1], LN_EPS, None, ALU.add).then_inc(rs_ready, 1)
            pool.wait_ge(rs_ready, 2 * grp + 1)
            nc.gpsimd.tensor_tensor(rs[:], ve[:], g["mhalf"][:].to_broadcast([P, B]), ALU.pow).then_inc(rs_ready, 1)

        @block.sync
        def _(sp):
            g["clear"](sp, 1)

        @block.gpsimd
        def _(pool):
            for grp in range(J):
                for k, i in enumerate(POOL_PAIRS):
                    s, t = PAIRS[i]
                    pool.wait_ge(ring_free, grp * USES + TURNED + 4 * (max(s, t) + 1))
                    if k == 0:
                        if grp >= 1:
                            pool.wait_ge(third_added, grp * B)
                            pool.wait_ge(o_ready, grp * B)
                    elif k >= 2:
                        pool.wait_ge(pp_used, grp * NP + k - 1)
                    nc.gpsimd.tensor_tensor(by_head(pp[:, k % 2, :]), heads(grp, s, 0), heads(grp, t, 1), ALU.mult)\
                        .then_inc(pp_ready, 1)
                if grp >= 1:
                    rstd(pool, grp - 1)
                for s in range(B):
                    if s == 0:
                        pool.wait_ge(attn_ready, grp + 1)
                        pool.wait_ge(ring_free, (grp + 1) * USES)
                        pool.wait_ge(pp_used, (grp + 1) * NP)
                    for t in (2, 3):
                        if s >= 1:
                            pool.wait_ge(third_added if t == 2 else o_ready, grp * B + s)
                        nc.gpsimd.tensor_tensor(by_head(pp[:, t % 2, :]), heads(grp, t, 2), share(s, t), ALU.mult)\
                            .then_inc(pp_ready, 1)
            rstd(pool, J - 1)

        @block.scalar
        def _(act):
            def move(grp, u):
                n = grp * USES + u
                act.wait_ge(ring_done, n + 1)
                if u < TURNED:
                    dst = xT[:, 2 * u:2 * u + 2].rearrange("p s k n -> p (s k n)")
                else:
                    s, m = CHUNKS[u - TURNED]
                    dst = qkv[:, grp % 2, s, m * 512:(m + 1) * 512]
                    if grp >= 2 and u == TURNED:
                        act.wait_ge(o_ready, (grp - 1) * B)
                nc.scalar.copy(dst, PS[:, n % RING, :]).then_inc(ring_free, 1)

            for u in range(USES):
                move(0, u)
            for grp in range(J):
                for u in range(USES):
                    if grp + 1 < J:
                        move(grp + 1, u)
                    if u == (3 if grp == 0 else 11):
                        act.wait_ge(sc_ready, grp + 1)
                        nc.scalar.activation(sc[:], sc[:], ACT.Exp, scale=HD1 ** -0.5).then_inc(ex_ready, 1)
                for s in range(B):
                    n = grp * B + s
                    act.wait_ge(oT_done, n + 1)
                    if n >= 2:
                        act.wait_ge(proj_done, n - 1)
                    nc.scalar.copy(oT[:, s % 2].rearrange("p c n -> p (c n)"),
                                   PS[:, OB:OB + 2, :].rearrange("p b n -> p (b n)")).then_inc(oT_ready, 1)

        @block.vector
        def _(dve):
            n = [0]

            def token(ins):
                n[0] += 1
                ins.then_inc(chain, 1)
                return n[0]

            def link(ins):
                dve.wait_ge(chain, token(ins))

            def residual(grp, s):
                if s == 0:
                    dve.wait_ge(proj_done, (grp + 1) * B)
                nc.vector.tensor_tensor(r[:, s, :], PS[:, PB + s // 2, (s % 2) * D:(s % 2 + 1) * D], tile(s, grp), ALU.add)\
                    .then_inc(r_ready, 1)
                dve.wait_ge(r_ready, grp * B + s + 1)
                link(nc.vector.bn_stats(bn[:, s, :], r[:, s, :]))
                nc.vector.bn_aggr(mv[:, s, :], bn[:, s, :]).then_inc(mv_ready, 1)

            def norm(grp):
                dve.wait_ge(rs_ready, 2 * grp + 2)
                for s in range(B):
                    nc.vector.tensor_scalar(tile(s, grp), r[:, s, :], mv[:, s, 0:1], rs[:, s:s + 1],
                                            ALU.subtract, ALU.mult).then_inc(x_ready, 1)

            def score(grp, i, product):
                s, t = PAIRS[i]
                if i in POOL_PAIRS:
                    k = POOL_PAIRS.index(i)
                    dve.wait_ge(pp_ready, grp * (NP + 2 * B) + k + 1)
                    nc.vector.reduce_sum(sc[:, s, t, :], by_head(pp[:, k % 2, :]), AX_X).then_inc(pp_used, 1)
                else:
                    dve.wait_ge(chain, product)
                    token(nc.vector.reduce_sum(sc[:, s, t, :], by_head(prod[:, own(i) % 2, :]), AX_X))

            def own(i):
                return i - sum(p < i for p in POOL_PAIRS)

            for grp in range(J):
                product = {}
                for i in range(B * B + 1):
                    if i < B * B and i not in POOL_PAIRS:
                        if own(i) >= 2:
                            dve.wait_ge(chain, n[0])
                        s, t = PAIRS[i]
                        dve.wait_ge(ring_free, grp * USES + TURNED + 4 * (max(s, t) + 1))
                        product[i] = token(nc.vector.tensor_tensor(
                            by_head(prod[:, own(i) % 2, :]), heads(grp, s, 0), heads(grp, t, 1), ALU.mult))
                    if i >= 1:
                        score(grp, i - 1, product.get(i - 1))
                    if grp >= 1 and i in (4, 5, 6, 7):
                        residual(grp - 1, i - 4)
                if grp >= 1:
                    norm(grp - 1)
                dve.wait_ge(chain, n[0])
                dve.wait_ge(pp_used, (grp + 1) * NP)
                link(nc.vector.reduce_max(mx[:], sc[:].rearrange("p s t h -> p s h t"), AX_X))
                nc.vector.tensor_tensor(sc[:], sc[:], mx[:, :, None, :].to_broadcast([P, B, B, H1]),
                                        ALU.subtract).then_inc(sc_ready, 1)
                dve.wait_ge(ex_ready, grp + 1)
                link(nc.vector.reduce_sum(mx[:], sc[:].rearrange("p s t h -> p s h t"), AX_X))
                link(nc.vector.reciprocal(mx[:], mx[:]))
                nc.vector.tensor_tensor(sc[:], sc[:], mx[:, :, None, :].to_broadcast([P, B, B, H1]), ALU.mult)\
                    .then_inc(attn_ready, 1)
                dve.wait_ge(attn_ready, grp + 1)
                dve.wait_ge(ring_free, (grp + 1) * USES)
                for s in range(B):
                    at = grp * (NP + 2 * B) + NP + 2 * s
                    if grp >= 1:
                        dve.wait_ge(oT_done, (grp - 1) * B + s + 1)
                    first = token(nc.vector.tensor_tensor(by_head(o[:, s, :]), heads(grp, 0, 2), share(s, 0), ALU.mult))
                    link(nc.vector.tensor_tensor(by_head(prod[:, 0, :]), heads(grp, 1, 2), share(s, 1), ALU.mult))
                    link(nc.vector.tensor_tensor(o[:, s, :], o[:, s, :], prod[:, 0, :], ALU.add))
                    dve.wait_ge(pp_ready, at + 1)
                    nc.vector.tensor_tensor(o[:, s, :], o[:, s, :], pp[:, 0, :], ALU.add).then_inc(third_added, 1)
                    dve.wait_ge(third_added, grp * B + s + 1)
                    dve.wait_ge(pp_ready, at + 2)
                    nc.vector.tensor_tensor(o[:, s, :], o[:, s, :], pp[:, 1, :], ALU.add).then_inc(o_ready, 1)
            for s in range(B):
                residual(J - 1, s)
            norm(J - 1)
            dve.wait_ge(x_ready, J * B)

        @block.tensor
        def _(pe):
            def fill(grp, u):
                n = grp * USES + u
                if n >= RING:
                    pe.wait_ge(ring_free, n - RING + 1)
                bank = PS[:, n % RING, :]
                if u < TURNED:
                    for i in range(2):
                        for k in range(KD):
                            mm = nc.tensor.transpose(bank[:, (i * KD + k) * P:(i * KD + k + 1) * P],
                                                     tile(2 * u + i, grp)[:, k * P:(k + 1) * P], ident[:])
                else:
                    s, m = CHUNKS[u - TURNED]
                    if u == TURNED:
                        pe.wait_ge(ring_free, grp * USES + TURNED)
                    at = slice(m * 512, (m + 1) * 512)
                    nc.tensor.matmul(bank, ones3[:], bias[:, at], start=True, stop=False)
                    for k in range(KD):
                        mm = nc.tensor.matmul(bank, xT[:, s, k, :], w[:, k, at], start=False, stop=(k == KD - 1))
                mm.then_inc(ring_done, 1)

            def turn_out(grp, s):
                n = grp * B + s
                pe.wait_ge(o_ready, n + 1)
                if n >= 1:
                    pe.wait_ge(oT_ready, n)
                for c in range(KF):
                    mm = nc.tensor.transpose(PS[:, OB + c // 4, (c % 4) * P:(c % 4 + 1) * P],
                                             o[:, s, c * P:(c + 1) * P], ident[:])
                mm.then_inc(oT_done, 1)

            def project(grp, s):
                pe.wait_ge(oT_ready, grp * B + s + 1)
                if grp >= 1:
                    pe.wait_ge(r_ready, grp * B)
                out = PS[:, PB + s // 2, (s % 2) * D:(s % 2 + 1) * D]
                nc.tensor.matmul(out, ones3[:], bias[:, 3 * P1:NB1], start=True, stop=False)
                for c in range(KF):
                    mm = nc.tensor.matmul(out, oT[:, s % 2, c, :], wo[:, c, :], start=False, stop=(c == KF - 1))
                mm.then_inc(proj_done, 1)

            pe.wait_ge(w_loaded, 16 * g["l1_loads"])
            pe.wait_ge(bias_sent, 48)
            for u in range(USES):
                fill(0, u)
            for grp in range(J):
                if grp + 1 < J:
                    for u in range(USES):
                        fill(grp + 1, u)
                turn_out(grp, 0)
                for s in range(B):
                    if s + 1 < B:
                        turn_out(grp, s + 1)
                    project(grp, s)

HX, HDX = 8, 64
PX = HX * HDX


def layer1_cross(nc, top, g):
    S2 = g["S2"]
    KEYS = S2 + S
    CT = -(-S2 // P)
    LAST = S2 - (CT - 1) * P
    KT = -(-KEYS // P)
    KLAST = KEYS - (KT - 1) * P
    CH = [(c * 512, min(512, KEYS - c * 512)) for c in range(-(-KEYS // 512))]
    NCH = len(CH)
    QU = 2
    UNITS = HX * J // QU
    GT = -(-KT // 2)
    VG = 2
    VT = 512 // (VG * HDX)
    VU = 2 * VG
    RING, TB, AVB = 4, 4, 6
    ctx = ExitStack()
    with ctx:
        def sb(name, shape, dt=F32):
            return ctx.enter_context(nc.sbuf_tensor("x_" + name, shape, dt))

        loop_sems = []

        def sem(name, kept=False):
            s = ctx.enter_context(nc.semaphore("x_" + name))
            if not kept:
                loop_sems.append(s)
            return s

        PS, X, LG, ident = g["PS"], g["X"], g["LG"], g["ident"]
        wv = sb("wv", [P, KD, PX])
        wq = sb("wq", [P, 2, KD, 2 * HDX])
        wk = sb("wk", [P, 2, KD, 2 * HDX])
        wo = sb("wo", [P, HX, D])
        wg = sb("wg", [P, KD, E])
        cols = sb("cols", [P, 4 * KD + 1])
        NS = CT + J
        bn, mv, ve, rs = sb("bn", [P, NS, 6]), sb("mv", [P, NS, 2]), sb("ve", [P, NS]), sb("rs", [P, NS])
        KE = KEYS + KEYS % 2
        kvT = sb("kvT", [P, KD, KE])
        latT = sb("latT", [P, KD, S])
        vs = sb("vs", [P, KT, VG, 2, HDX], F32R)
        ks = sb("ks", [P, 2, 2, KE], F32R)
        qs = sb("qs", [P, 2, 2, S], F32R)
        ps = sb("ps", [P, 2, KT, QU * P], F32R)
        maskf = sb("maskf", [P, KEYS])
        NSM = 2 * QU
        sm = sb("sm", [P, NSM, KEYS])
        mx = sb("mx", [P, 2, NCH])
        nm = sb("nm", [P, 2])
        rsum = sb("rsum", [P, 2, 2 * NSM])
        rrec = sb("rrec", [P, 2 * NSM])
        rb = sb("rb", [P, QU * P])
        o = sb("o", [P, HX, S])
        place = sm[:].rearrange("p a n -> p (a n)")
        at = 0
        cx = place[:, 0:CT * D].rearrange("p (t d) -> p t d", d=D)
        at += CT * D
        ln = place[:, at:at + J * D].rearrange("p (j d) -> p j d", d=D)
        at += J * D
        lx = place[:, at:at + J * D].rearrange("p (j d) -> p j d", d=D)
        at += J * D
        x5 = place[:, at:at + J * D].rearrange("p (j d) -> p j d", d=D)
        x5T = place[:, at + J * D:at + J * D + 2 * D].rearrange("p (b k n) -> p b k n", b=2, n=P)
        at += J * D + 2 * D
        mask8 = place[:, at:at + -(-S2 // 4)].bitcast(U8)[:, 0:S2]

        w_loaded, ended, go, pace = sem("w_loaded", True), sem("ended", True), sem("go", True), sem("pace", True)
        consts, kv_padded = sem("consts", True), sem("kv_padded", True)
        cx_loaded, cx_bn, cx_stats, cx_eps, cx_rs, cx_ready = (
            sem("cx_" + name, True) for name in ("loaded", "bn", "stats", "eps", "rs", "ready"))
        chain, bchain = sem("chain"), sem("bchain")
        mask_loaded = sem("mask_loaded")
        wq_loaded = sem("wq_even_loaded"), sem("wq_odd_loaded")
        wk_loaded = sem("wk_even_loaded"), sem("wk_odd_loaded")
        stats_ready, rs_ready, ln_ready = sem("stats_ready"), sem("rs_ready"), sem("ln_ready")
        nT_done, nT_ready, gated = sem("nT_done"), sem("nT_ready"), sem("gated")
        ring_done, ring_act, ring_free = sem("ring_done"), sem("ring_act"), sem("ring_free")
        nm_ready, p_ready, rrec_ready = sem("nm_ready"), sem("p_ready"), sem("rrec_ready")
        t_done, ph_ready, pl_ready = sem("t_done"), sem("ph_ready"), sem("pl_ready")
        av_done, lx_again, proj_done = sem("av_done"), sem("lx_again"), sem("proj_done")
        mv_ready, rs5_ready, x5_ready = sem("mv_ready"), sem("rs5_ready"), sem("x5_ready")
        x5T_done, x5T_ready, lg_done = sem("x5T_done"), sem("x5T_ready"), sem("lg_done")
        block = ctx.enter_context(nc.Block())

        GROUPS = [("ctx", t, min(4, CT - t)) for t in range(0, CT, 4)] + [("lat", 0, J)]

        S_PLACES = (2, 2, 2, 2, 2, 0, 0, 0, 0)
        BUILD_PLACES = (5, 7)
        EXP_PLACES = (3, 4, 6, 7)
        V_PLACES = tuple(min(2 * i + 1, GT - 1) for i in range(-(-KT // VT)))

        def ring_uses(u, g):
            made = []
            if u == -1 and g == 0:
                made += [("q", 0, 0)] + [("k", 0, c) for c in range(NCH)]
            if 0 <= u < UNITS and u % VU == 0 and g in V_PLACES:
                made.append(("v", u // VU, V_PLACES.index(g)))
            if u + 1 < UNITS:
                first = sum(S_PLACES[:g])
                made += [("s", u + 1, c) for c in range(first, first + S_PLACES[g])]
            if g in BUILD_PLACES:
                p, step = (u + 5) // 4, (u + 5) % 4
                build = ((("k", p, 0), ("q", 2 * p - 1, 0)), (("k", p, 1),), (("k", p, 2), ("q", 2 * p, 0)),
                         tuple(("k", p, c) for c in range(3, NCH)))[step]
                at = BUILD_PLACES.index(g)
                for use in build[at:at + 1] if g != BUILD_PLACES[-1] else build[at:]:
                    if use[1] < (HX // 2 if use[0] == "k" else HX):
                        made.append(use)
            if u >= 1 and g == GT - 1:
                made.append(("b", u - 1, 0))
            return made

        STEPS = [(u, g) for u in range(-1, UNITS + 1) for g in range(GT)]
        USE = {use: n for n, use in enumerate(use for u, g in STEPS for use in ring_uses(u, g))}
        BUILT, total = {}, 0
        for use in USE:
            total += use[0] in "qkvb"
            BUILT[use] = total

        def width(t0, nt):
            return min(S2, (t0 + nt) * P) - t0 * P

        def even(c):
            return slice(CH[c][0], min(CH[c][0] + 512, KE)), slice(0, min(512, KE - CH[c][0]))

        def keys(t):
            return P if t < KT - 1 else KLAST

        def values_of(c):
            nt = min(VT, KT - VT * c)
            assert nt == 1 or VT * c + nt < KT
            return keys(VT * c), slice(VT * c, VT * c + nt), nt

        def pair(g):
            return (P, 2) if 2 * g + 1 < KT else (KLAST, 1)

        @block.sync
        def _(sp):
            def load_context(b):
                c = g["ctx"][b].rearrange("o s d -> (o s) d")
                sp.dma_start(cx[:, 0:CT - 1, :], c[0:(CT - 1) * P, :].rearrange("(t p) d -> p t d", p=P)).then_inc(cx_loaded, 16)
                sp.dma_start(cx[0:LAST, CT - 1, :], c[(CT - 1) * P:S2, :]).then_inc(cx_loaded, 16)

            load_context(slice(0, 1))
            for dst, src in ((wv, "L1_xattn_Wv"), (wo, "L1_xattn_Wout"),
                             (wg, "L1_ffn_gate"), (cols, "L1_xattn_cols")):
                sp.dma_start(dst[:], g[src]).then_inc(w_loaded, 16)
            sp.sem_inc(go, 1)
            with sp.Fori(1, B + 1) as it:
                each(sp, go, pace, it)
                sp.dma_start(mask8, g["mask"][bass.ds(it - 1, 1), :].to_broadcast([P, S2])).then_inc(mask_loaded, 16)
                sp.dma_start(wk[:, 0], g["L1_xattn_Wk"][0]).then_inc(wk_loaded[0], 16)
                for p in range(HX // 2):
                    for h in (2 * p, 2 * p + 1):
                        if h >= 2:
                            sp.wait_ge(ring_done, USE["q", h - 2, 0] + 1)
                        sp.dma_start(wq[:, h % 2], g["L1_xattn_Wq"][h]).then_inc(wq_loaded[h % 2], 16)
                    if p + 1 < HX // 2:
                        if p >= 1:
                            sp.wait_ge(ring_done, USE["k", p - 1, NCH - 1] + 1)
                        sp.dma_start(wk[:, (p + 1) % 2], g["L1_xattn_Wk"][p + 1]).then_inc(wk_loaded[(p + 1) % 2], 16)
                sp.wait_ge(t_done, (UNITS - 1) * GT)
                load_context(bass.ds(it, 1))
                turn(sp, ended, go, pace, it, loop_sems)
            sp.wait_ge(cx_loaded, 32 * (B + 1))

        @block.gpsimd
        def _(pool):
            nc.gpsimd.memset(maskf[:], 0.0).then_inc(consts, 1)
            nc.gpsimd.memset(mv[:, NS - 1, :], 1.0).then_inc(consts, 1)
            if KE > KEYS:
                nc.gpsimd.memset(kvT[:, :, KEYS:KE], 0.0).then_inc(kv_padded, 1)

            def context_rstd(n):
                pool.wait_ge(cx_stats, n)
                pool.sem_inc(pace, 1)
                nc.gpsimd.tensor_scalar(ve[:, J:NS], mv[:, J:NS, 1], LN_EPS, None, ALU.add).then_inc(cx_eps, 1)
                pool.wait_ge(cx_eps, n)
                pool.sem_inc(pace, 1)
                nc.gpsimd.tensor_tensor(rs[:, J:NS], ve[:, J:NS], g["mhalf"][:].to_broadcast([P, CT]), ALU.pow)\
                    .then_inc(cx_rs, 1)

            context_rstd(1)
            with pool.Fori(1, B + 1) as it:
                each(pool, go, pace, it)
                pool.wait_ge(stats_ready, 1)
                nc.gpsimd.tensor_scalar(ve[:, 0:J], mv[:, 0:J, 1], LN_EPS, None, ALU.add).then_inc(rs_ready, 1)
                pool.wait_ge(rs_ready, 1)
                nc.gpsimd.tensor_tensor(rs[:, 0:J], ve[:, 0:J], g["mhalf"][:].to_broadcast([P, J]), ALU.pow).then_inc(rs_ready, 1)
                context_rstd(it + 1)
                for j in range(J):
                    pool.wait_ge(mv_ready, j + 1)
                    nc.gpsimd.tensor_scalar(ve[:, j:j + 1], mv[:, j, 1:2], LN_EPS, None, ALU.add).then_inc(rs5_ready, 1)
                    pool.wait_ge(rs5_ready, 2 * j + 1)
                    nc.gpsimd.tensor_tensor(rs[:, j:j + 1], ve[:, j:j + 1], g["mhalf"][:], ALU.pow).then_inc(rs5_ready, 1)
                ends(pool, ended)

        @block.scalar
        def _(act):
            act.wait_ge(w_loaded, 16 * 4)
            with act.Fori(1, B + 1) as it:
                each(act, go, pace, it)
                for i, (kind, t0, nt) in enumerate(GROUPS):
                    for k in range(KD):
                        n = i * KD + k
                        act.wait_ge(nT_done, n + 1)
                        if kind == "lat":
                            dst, wd, at = latT[:, k, :], S, 2 * KD
                        else:
                            wd, at = width(t0, nt), 0
                            dst = kvT[:, k, t0 * P:t0 * P + wd]
                        nc.scalar.activation(dst, PS[:, n % 4, 0:wd], ACT.Identity, bias=cols[:, at + KD + k:at + KD + k + 1],
                                             scale=cols[:, at + k:at + k + 1]).then_inc(nT_ready, 1)

                def high(use):
                    kind, a, c = use
                    act.wait_ge(ring_done, USE[use] + 1)
                    src = PS[:, USE[use] % RING, :]
                    if kind == "q":
                        ins = nc.scalar.mul(qs[:, a % 2, 0, :], src, HDX ** -0.5)
                    elif kind == "k":
                        to, of = even(c)
                        for i in range(2):
                            own = slice(i * HDX, (i + 1) * HDX)
                            ins = nc.scalar.copy(ks[own, a % 2, i, to], src[own, of])
                    elif kind == "b":
                        if a >= 1:
                            act.wait_ge(ring_free, USE["b", a - 1, 0] + 1)
                        ins = nc.scalar.copy(rb[:], src[:, 0:QU * P])
                    else:
                        np_, at, nt = values_of(c)
                        ins = nc.scalar.copy(
                            vs[0:np_, at, :, 0, :],
                            src[0:np_, 0:nt * VG * HDX].rearrange("p (t h d) -> p t h d", t=nt, h=VG))
                    ins.then_inc(ring_act, 1)

                def probs(r, half):
                    of = (slice(0, KEYS // 2), slice(KEYS // 2, KEYS))[half]
                    at = r % (2 * NSM)
                    if half == 0:
                        act.wait_ge(nm_ready, r + 1)
                    ins = nc.scalar.activation(sm[:, r % NSM, of], sm[:, r % NSM, of], ACT.Exp, bias=nm[:, r % 2:r % 2 + 1],
                                               accum_out=rsum[:, half, at:at + 1])
                    if half == 1:
                        ins.then_inc(p_ready, 1)

                for u, g in STEPS:
                    if 0 <= u < UNITS:
                        np_, nt = pair(g)
                        act.wait_ge(t_done, u * GT + g + 1)
                        if u >= 1:
                            act.wait_ge(av_done, (u - 1) * GT + g + 1)
                        nc.scalar.copy(ps[0:np_, 0, 2 * g:2 * g + nt, :],
                                       PS[0:np_, TB + (u * GT + g) % 2, 0:nt * QU * P]
                                       .rearrange("p (t n) -> p t n", t=nt)).then_inc(ph_ready, 1)
                    for use in ring_uses(u, g):
                        if use[0] in "qkvb":
                            high(use)
                    if u + 1 < UNITS and g in EXP_PLACES:
                        q, half = divmod(EXP_PLACES.index(g), 2)
                        probs((u + 1) * QU + q, half)
                for j in range(J):
                    act.wait_ge(x5T_done, j + 1)
                    if j >= 2:
                        act.wait_ge(lg_done, j - 1)
                    nc.scalar.copy(x5T[:, j % 2].rearrange("p c n -> p (c n)"), PS[:, 4 + j % 2, 0:D]).then_inc(x5T_ready, 1)
                ends(act, ended)

        @block.vector
        def _(dve):
            n = [0]

            def link(ins):
                n[0] += 1
                ins.then_inc(chain, 1)
                dve.wait_ge(chain, n[0])

            dve.wait_ge(consts, 2)
            tiles = [(J + t, cx[0:P if t < CT - 1 else LAST, t, :], P if t < CT - 1 else LAST) for t in range(CT)]

            def context_stats(n):
                dve.wait_ge(cx_loaded, n * 32)
                dve.sem_inc(pace, 1)
                for i, x, np_ in tiles:
                    ins = nc.vector.bn_stats(bn[0:np_, i, :], x)
                ins.then_inc(cx_bn, 1)
                dve.wait_ge(cx_bn, n)
                dve.sem_inc(pace, 1)
                for i, x, np_ in tiles:
                    ins = nc.vector.bn_aggr(mv[0:np_, i, :], bn[0:np_, i, :])
                ins.then_inc(cx_stats, 1)

            def context_norm(n):
                dve.wait_ge(cx_rs, n)
                dve.sem_inc(pace, 1)
                for i, x, np_ in tiles:
                    ins = nc.vector.tensor_scalar(x, x, mv[0:np_, i, 0:1], rs[0:np_, i:i + 1], ALU.subtract, ALU.mult)
                ins.then_inc(cx_ready, 1)

            context_stats(1)
            context_norm(1)
            with dve.Fori(1, B + 1) as it:
                each(dve, go, pace, it)
                n[0] = 0
                link(nc.vector.tensor_copy(lx, X[:, bass.ds(it * J - J, J), :]))
                for j in range(J):
                    nc.vector.bn_stats(bn[:, j, :], lx[:, j, :]).then_inc(bchain, 1)
                for j in range(J):
                    dve.wait_ge(bchain, j + 1)
                    ins = nc.vector.bn_aggr(mv[:, j, :], bn[:, j, :])
                ins.then_inc(stats_ready, 1)
                dve.wait_ge(mask_loaded, 16)
                link(nc.vector.tensor_scalar(maskf[:, 0:S2], mask8, -1e30, None, ALU.mult))
                dve.wait_ge(rs_ready, 2)
                for j in range(J):
                    nc.vector.tensor_scalar(ln[:, j, :], lx[:, j, :], mv[:, j, 0:1], rs[:, j:j + 1], ALU.subtract, ALU.mult)\
                        .then_inc(ln_ready, 1)
                dve.wait_ge(nT_ready, KD * len(GROUPS))
                for k in range(KD):
                    ins = nc.vector.tensor_scalar(kvT[:, k, S2:KEYS], latT[:, k, :], cols[:, 4 * KD:4 * KD + 1], None, ALU.mult)
                ins.then_inc(gated, 1)

                def read(use):
                    kind, a, c = use
                    src = PS[:, USE[use] % RING, :]
                    dve.wait_ge(ring_done, USE[use] + 1)
                    if kind in "qkvb":
                        dve.wait_ge(ring_act, BUILT[use])
                    if kind == "s":
                        r = a * QU + c // NCH
                        c = c % NCH
                        lo, hi = CH[c][0], CH[c][0] + CH[c][1]
                        if a >= 2:
                            dve.wait_ge(t_done, (a - 1) * GT)
                        ins = nc.vector.tensor_tensor_reduce(
                            out=sm[:, r % NSM, lo:hi], in0=src[:, 0:hi - lo], in1=maskf[:, lo:hi], scale=1.0,
                            scalar=-3e38, op0=ALU.add, op1=ALU.max, accum_out=mx[:, r % 2, c:c + 1])
                    elif kind == "q":
                        ins = nc.vector.scalar_tensor_tensor(qs[:, a % 2, 1, :], src, HDX ** -0.5,
                                                             qs[:, a % 2, 0, :].bitcast(F32), ALU.mult, ALU.subtract)
                    elif kind == "k":
                        to, of = even(c)
                        for i in range(2):
                            own, other = slice(i * HDX, (i + 1) * HDX), slice((1 - i) * HDX, (2 - i) * HDX)
                            ins = nc.vector.tensor_tensor(ks[other, a % 2, i, to], src[own, of],
                                                          ks[own, a % 2, i, to].bitcast(F32), ALU.subtract)
                    elif kind == "v":
                        np_, at, nt = values_of(c)
                        ins = nc.vector.tensor_tensor(
                            vs[0:np_, at, :, 1, :],
                            src[0:np_, 0:nt * VG * HDX].rearrange("p (t h d) -> p t h d", t=nt, h=VG),
                            vs[0:np_, at, :, 0, :].bitcast(F32), ALU.subtract)
                    else:
                        dve.wait_ge(av_done, (a + 1) * GT)
                        ins = nc.vector.tensor_tensor(o[:, a // 2, (a % 2) * QU * P:(a % 2 + 1) * QU * P],
                                                      PS[:, AVB + a % 2, 0:QU * P], rb[:], ALU.mult)
                    ins.then_inc(ring_free, 1)
                    if kind == "s" and c == NCH - 1:
                        dve.wait_ge(ring_free, USE[use] + 1)
                        if r >= 2:
                            dve.wait_ge(p_ready, r - 1)
                        link(nc.vector.reduce_max(nm[:, r % 2:r % 2 + 1], mx[:, r % 2, :], AX_X))
                        nc.vector.tensor_scalar(nm[:, r % 2:r % 2 + 1], nm[:, r % 2:r % 2 + 1], -1.0, None, ALU.mult)\
                            .then_inc(nm_ready, 1)

                dve.wait_ge(nT_done, KD * len(GROUPS))
                for u, g in STEPS:
                    if 0 <= u < UNITS:
                        np_, nt = pair(g)
                        dve.wait_ge(ph_ready, u * GT + g + 1)
                        nc.vector.tensor_tensor(ps[0:np_, 1, 2 * g:2 * g + nt, :],
                                                PS[0:np_, TB + (u * GT + g) % 2, 0:nt * QU * P]
                                                .rearrange("p (t n) -> p t n", t=nt),
                                                ps[0:np_, 0, 2 * g:2 * g + nt, :].bitcast(F32),
                                                ALU.subtract).then_inc(pl_ready, 1)
                        if g == 0:
                            at = (u * QU) % (2 * NSM)
                            dve.wait_ge(p_ready, (u + 1) * QU)
                            link(nc.vector.tensor_tensor(rrec[:, at:at + QU], rsum[:, 0, at:at + QU], rsum[:, 1, at:at + QU], ALU.add))
                            nc.vector.reciprocal(rrec[:, at:at + QU], rrec[:, at:at + QU]).then_inc(rrec_ready, 1)
                    for use in ring_uses(u, g):
                        if use[0] != "b":
                            read(use)
                    if u >= 1 and g == GT - 1:
                        read(("b", u - 1, 0))
                dve.wait_ge(t_done, UNITS * GT)
                nc.vector.tensor_copy(lx, X[:, bass.ds(it * J - J, J), :]).then_inc(lx_again, 1)
                dve.wait_ge(lx_again, 1)
                context_stats(it + 1)
                for j in range(J):
                    if j == J // 2:
                        context_norm(it + 1)
                    dve.wait_ge(proj_done, j + 1)
                    link(nc.vector.tensor_tensor(lx[:, j, :], PS[:, 2 + j % 2, 0:D], lx[:, j, :], ALU.add))
                    link(nc.vector.bn_stats(bn[:, j, :], lx[:, j, :]))
                    nc.vector.bn_aggr(mv[:, j, :], bn[:, j, :]).then_inc(mv_ready, 1)
                for j in range(J):
                    dve.wait_ge(rs5_ready, 2 * j + 2)
                    nc.vector.tensor_scalar(x5[:, j, :], lx[:, j, :], mv[:, j, 0:1], rs[:, j:j + 1], ALU.subtract, ALU.mult)\
                        .then_inc(x5_ready, 1)
                dve.wait_ge(x5_ready, J)
                nc.vector.tensor_copy(X[:, bass.ds(it * J - J, J), :], x5)
                dve.wait_ge(lg_done, J)
                nc.vector.tensor_copy(LG[:, bass.ds(it * J - J, J), :],
                                      PS[:, 6, 0:J * E].rearrange("p (j e) -> p j e", e=E))
                ends(dve, ended)

        @block.tensor
        def _(pe):
            pe.wait_ge(w_loaded, 16 * 4)
            if KE > KEYS:
                pe.wait_ge(kv_padded, 1)
            with pe.Fori(1, B + 1) as it:
                each(pe, go, pace, it)
                pe.wait_ge(cx_ready, it)
                pe.sem_inc(pace, 1)
                for i, (kind, t0, nt) in enumerate(GROUPS):
                    if kind == "lat":
                        pe.wait_ge(ln_ready, J)
                    for k in range(KD):
                        n = i * KD + k
                        if n >= 4:
                            pe.wait_ge(nT_ready, n - 3)
                        for t in range(nt):
                            if kind == "lat":
                                src, np_ = ln[:, t, k * P:(k + 1) * P], P
                            else:
                                np_ = P if t0 + t < CT - 1 else LAST
                                src = cx[0:np_, t0 + t, k * P:(k + 1) * P]
                            mm = nc.tensor.transpose(PS[:, n % 4, t * P:t * P + np_], src, ident[0:np_, 0:np_])
                        mm.then_inc(nT_done, 1)
                pe.wait_ge(nT_ready, KD * len(GROUPS))
                pe.wait_ge(gated, 1)

                def fill(use):
                    kind, a, c = use
                    n = USE[use]
                    bank = PS[:, n % RING, :]
                    if n >= RING:
                        pe.wait_ge(ring_free, n - RING + 1)
                    if kind == "s":
                        h, q, c = a // 2, (a % 2) * QU + c // NCH, c % NCH
                        pe.wait_ge(ring_free, max(USE["k", h // 2, c], USE["q", h, 0]) + 1)
                        of, to = even(c)
                        for part in range(2):
                            mm = nc.tensor.matmul(bank[:, to], qs[:, h % 2, part, q * P:(q + 1) * P],
                                                  ks[:, (h // 2) % 2, h % 2, of],
                                                  start=(part == 0), stop=(part == 1))
                    elif kind == "b":
                        pe.wait_ge(rrec_ready, a + 1)
                        for q in range(QU):
                            at = (a * QU + q) % (2 * NSM)
                            mm = nc.tensor.transpose(bank[:, q * P:(q + 1) * P], rrec[:, at:at + 1].to_broadcast([P, P]),
                                                     ident[:])
                    elif kind == "v":
                        for t in range(VT * c, min(VT * c + VT, KT)):
                            for k in range(KD):
                                mm = nc.tensor.matmul(bank[0:keys(t), (t % VT) * VG * HDX:(t % VT + 1) * VG * HDX],
                                                      kvT[:, k, t * P:t * P + keys(t)],
                                                      wv[:, k, a * VG * HDX:(a + 1) * VG * HDX],
                                                      start=(k == 0), stop=(k == KD - 1))
                    else:
                        loaded = wq_loaded if kind == "q" else wk_loaded
                        pe.wait_ge(loaded[a % 2], 16 * (a // 2 + 1))
                        for k in range(KD):
                            w = (wq if kind == "q" else wk)[:, a % 2, k, :]
                            of, to = even(c)
                            rhs = latT[:, k, :] if kind == "q" else kvT[:, k, of]
                            out = bank if kind == "q" else bank[:, to]
                            mm = nc.tensor.matmul(out, w, rhs, start=(k == 0), stop=(k == KD - 1))
                    mm.then_inc(ring_done, 1)

                for u, g in STEPS:
                    if u >= 1:
                        a = u - 1
                        pe.wait_ge(pl_ready, a * GT + g + 1)
                        if g == 0 and a >= 2:
                            pe.wait_ge(ring_free, USE["b", a - 2, 0] + 1)
                        if a % VU == 0:
                            pe.wait_ge(ring_free, USE["v", a // VU, 2 * g // VT] + 1)
                        for t in range(2 * g, min(2 * g + 2, KT)):
                            for part in range(2):
                                mm = nc.tensor.matmul(PS[:, AVB + a % 2, 0:QU * P],
                                                      vs[0:keys(t), t, (a // 2) % VG].rearrange("p a d -> p (a d)"),
                                                      ps[0:keys(t), part, t, :],
                                                      start=(t == 0 and part == 0), stop=(t == KT - 1 and part == 1))
                        mm.then_inc(av_done, 1)
                    if 0 <= u < UNITS:
                        n = u * GT + g
                        if g == 0:
                            pe.wait_ge(p_ready, (u + 1) * QU)
                        if n >= 2:
                            pe.wait_ge(pl_ready, n - 1)
                        for t in range(2 * g, min(2 * g + 2, KT)):
                            for q in range(QU):
                                at = (t % 2) * QU * P + q * P
                                mm = nc.tensor.transpose(PS[0:keys(t), TB + n % 2, at:at + P],
                                                         sm[:, (u * QU + q) % NSM, t * P:t * P + keys(t)], ident[:])
                        mm.then_inc(t_done, 1)
                    for use in ring_uses(u, g):
                        fill(use)
                pe.wait_ge(ring_free, len(USE))
                for j in range(J):
                    if j >= 2:
                        pe.wait_ge(mv_ready, j - 1)
                    for h in range(HX):
                        mm = nc.tensor.matmul(PS[:, 2 + j % 2, 0:D], o[:, h, j * P:(j + 1) * P], wo[:, h, :],
                                              start=(h == 0), stop=(h == HX - 1))
                    mm.then_inc(proj_done, 1)
                pe.wait_ge(pl_ready, UNITS * GT)
                for j in range(J + 1):
                    if j < J:
                        pe.wait_ge(x5_ready, j + 1)
                        if j >= 2:
                            pe.wait_ge(x5T_ready, j - 1)
                        for k in range(KD):
                            mm = nc.tensor.transpose(PS[:, 4 + j % 2, k * P:(k + 1) * P], x5[:, j, k * P:(k + 1) * P], ident[:])
                        mm.then_inc(x5T_done, 1)
                    if j >= 1:
                        i = j - 1
                        pe.wait_ge(x5T_ready, i + 1)
                        for k in range(KD):
                            mm = nc.tensor.matmul(PS[:, 6, i * E:(i + 1) * E], x5T[:, i % 2, k, :], wg[:, k, :],
                                                  start=(k == 0), stop=(k == KD - 1))
                        mm.then_inc(lg_done, 1)
                ends(pe, ended)


def experts1(nc, top, g):
    experts(nc, top, g, 1)


def expert_inputs(a, layer, names):
    w1, b1, w2, b2 = (a["L%d_ffn_%s" % (layer, n)] for n in names)
    pre = "L%d_ffn_" % layer
    return {
        pre + "w1": w1.reshape(E, KD, P, F).transpose(0, 2, 1, 3).reshape(E, P, KD * F),
        pre + "w2": w2.reshape(E, KF, P, D).transpose(0, 2, 1, 3).reshape(E, P, KF * D),
        pre + "b1": b1.reshape(E, KF, P).transpose(2, 0, 1).reshape(P, E * KF),
        pre + "b2": spread(b2),
    }


def twice(w):
    w = w.reshape(HX, HDX, D).transpose(1, 0, 2)
    return np.concatenate([w, w], 0)


def heads_twice(w):
    w = w.reshape(KD, P, HX, HDX).transpose(2, 1, 0, 3)
    return np.concatenate([w, w], -1)


def by_pair(w):
    return w.reshape(KD, P, HX // 2, 2 * HDX).transpose(2, 1, 0, 3)


def one_more(c):
    return np.concatenate([c, np.zeros((1,) + c.shape[1:], c.dtype)], 0)


def more_inputs(a):
    return {
        "L0_ffn_ln_g": spread(a["L0_ffn_ln_g"]), "L0_ffn_ln_b": spread(a["L0_ffn_ln_b"]),
        "L1_attn_w": rows_of(a["L1_attn_in_proj_weight"].T, KD), 
        "L1_attn_b": spread(np.concatenate([a["L1_attn_in_proj_bias"], a["L1_attn_out_proj_bias"]])),
        "L1_attn_wo": rows_of(a["L1_attn_out_proj_weight"].T, KF),
        "ctx": one_more(a["ctx_1024"]), "mask": a["mask_BxS2_bk0"],
        "L1_xattn_Wq": heads_twice(a["L1_xattn_Wq"]), "L1_xattn_Wk": by_pair(a["L1_xattn_Wk"]),
        "L1_xattn_Wv": rows_of(a["L1_xattn_Wv"], KD), "L1_xattn_Wout": twice(a["L1_xattn_Wout"]),
        "L1_xattn_cols": np.concatenate(
            [columns(a["L1_xattn_" + n], KD) for n in ("gamma_media", "beta_media", "gamma_lat", "beta_lat")]
            + [np.broadcast_to(a["L1_xattn_kv_gate"].reshape(1, 1), (P, 1))], 1),
        "L1_ffn_gate": rows_of(a["L1_ffn_gate_w"], KD),
        **expert_inputs(a, 0, ("W1", "b1", "W2", "b2")),
        **expert_inputs(a, 1, ("w1", "b1", "w2", "b2")),
    }


def constants(nc, ctx, g):
    sb = lambda name, shape, dt=F32: ctx.enter_context(nc.sbuf_tensor(name, shape, dt))
    g["PS"] = ctx.enter_context(nc.psum_tensor("PS", [P, 8, 512], F32))
    g["X"] = sb("X", [P, T, D])
    g["LG"] = sb("LG", [P, T, E])
    g["ident"] = sb("ident", [P, P])
    g["ones"] = sb("ones", [P, P])
    g["half"] = sb("half", [P, 1])
    g["mhalf"] = sb("mhalf", [P, 1])
    g["x_loaded"] = ctx.enter_context(nc.semaphore("x_loaded"))
    g["consts"] = ctx.enter_context(nc.semaphore("consts_ready"))
    g["xs_cleared"] = ctx.enter_context(nc.semaphore("xs_cleared"))
    zeros = g["zeros"] = sb("zeros", [P, D])

    def clear(eng, layer):
        n = tiles_of(layer + 1) + 2
        eng.wait_ge(g["consts"], g["n_consts"])
        eng.dma_start(g["xs%d" % layer].rearrange("(n p) d -> p n d", p=P),
                      zeros[:, None, :].to_broadcast([P, n, D])).then_inc(g["xs_cleared"], 16)

    g["clear"] = clear
    for layer in range(2):
        n = tiles_of(layer + 1)
        g["xs%d" % layer] = nc.dram_tensor("xs%d" % layer, ((n + 2) * P, D), F32, kind="Internal").ap()
        g["ys%d" % layer] = nc.dram_tensor("ys%d" % layer, (n * P, D), F32, kind="Internal").ap()
    with nc.Block() as block:
        @block.gpsimd
        def _(pool):
            pool.memset(g["ident"][:], 0.0).then_inc(g["consts"], 1)
            pool.memset(g["ones"][:], 1.0).then_inc(g["consts"], 1)
            pool.memset(g["half"][:], 0.5).then_inc(g["consts"], 1)
            pool.memset(g["mhalf"][:], -0.5).then_inc(g["consts"], 1)
            pool.wait_ge(g["consts"], 4)
            pool.affine_select(out=g["ident"][:], in_=g["ident"][:], compare_op=ALU.not_equal, fill=1.0, base=0,
                               pattern=[[-1, P]], channel_multiplier=1).then_inc(g["consts"], 1)
            pool.memset(zeros[:], 0.0).then_inc(g["consts"], 1)
        g["n_consts"] = 6


def build(nc, g):
    with ExitStack() as ctx:
        constants(nc, ctx, g)
        layer0_attention(nc, ctx, g)
        with ExitStack() as early:
            layer1_weights(nc, early, g)
            experts0(nc, ctx, g)
            layer1_attention(nc, ctx, g)
        layer1_cross(nc, ctx, g)
        experts1(nc, ctx, g)


def rows_of(w, k):
    return np.ascontiguousarray(w.reshape(k, P, -1).transpose(1, 0, 2))


def spread(v):
    return np.ascontiguousarray(np.broadcast_to(v.reshape(1, -1), (P, v.size)))


def columns(v, k):
    return np.ascontiguousarray(v.reshape(k, P).T)


def kernel(**inputs):
    import concourse.bacc as bacc
    from concourse.bass_utils import run_bass_kernel_spmd as run

    a = {k: np.asarray(v) for k, v in inputs.items()}
    x, c = a["x"], a["ctx_1024"]
    s2 = c.shape[1]
    xT = np.zeros((B + 1, P, KD, S), x.dtype)
    xT[:B] = x.reshape(B, S, KD, P).transpose(0, 3, 2, 1)
    om = a["L0_attn_omega"].transpose(1, 2, 0, 3).reshape(2, 8, HD0, FD0)
    omega = np.zeros((8, HD0, 2, 8, FD0), om.dtype)
    for h in range(8):
        omega[h, :, :, h, :] = om[:, h].transpose(1, 0, 2)
    node = np.repeat(a["L0_attn_quad_nodes"], M0)
    weight = np.repeat(a["L0_attn_quad_weights"], M0)
    nodes = np.stack([np.concatenate([node, node]), np.concatenate([weight, weight])], 1)
    W = a["L0_xattn_W"]
    ins = {
        "x": x.reshape(B, J, P, D).transpose(2, 0, 1, 3).reshape(P, T, D),
        "xT": xT,
        "ctxT": one_more(c.reshape(B, s2, KD, P).transpose(0, 3, 2, 1)),
        "L0_attn_Wqkv": rows_of(a["L0_attn_Wqkv"], KD),
        "L0_attn_bqkv": spread(a["L0_attn_bqkv"]),
        "L0_attn_omega": omega.reshape(P, 2, 8 * FD0),
        "L0_attn_nodes": nodes,
        "L0_attn_bout": spread(a["L0_attn_bout"]),
        "L0_attn_Wout": rows_of(a["L0_attn_Wout"], KD),
        "L0_xattn_W1": rows_of(W[:, :D].T, KD),
        "L0_xattn_W2": rows_of(W[:, D:].T, KD),
        "L0_xattn_b": spread(a["L0_xattn_b"]),
        "L0_ffn_Wr": rows_of(a["L0_ffn_Wr"], KD),
        "L0_ffn_br": spread(a["L0_ffn_br"]),
    }
    ins.update(more_inputs(a))
    nc = bacc.Bacc("TRN2", target_bir_lowering=False, num_devices=1)
    g = {"S2": s2}
    arrays = {}
    for name, v in ins.items():
        v = arrays["in_" + name] = np.ascontiguousarray(v)
        g[name] = nc.dram_tensor("in_" + name, v.shape, mybir.dt.from_np(v.dtype), kind="ExternalInput").ap()
    g["out"] = nc.dram_tensor("out", x.shape, F32, kind="ExternalOutput").ap()
    build(nc, g)
    r = run(nc, [arrays], core_ids=[0])
    return r.results[0]["out"]
```
